# Optimizing a Trainium2 kernel written in Bass

```python
import numpy as np
import jax
import jax.numpy as jnp

def _softmax(x, axis=-1):
    return jax.nn.softmax(x, axis=axis)

def _gelu(x):
    return jax.nn.gelu(x, approximate=True)

def _silu(x):
    return jax.nn.silu(x)

def _sigmoid(x):
    return jax.nn.sigmoid(x)

def _layernorm(x, axis=-1, eps=1e-05):
    m = jnp.mean(x, axis=axis, keepdims=True)
    v = jnp.var(x, axis=axis, keepdims=True)
    return (x - m) / jnp.sqrt(v + eps)

def _scatter_add(tgt, idx, src, axis=0):
    return tgt.at[idx].add(src)

def _segment_sum(src, seg, n):
    return jax.ops.segment_sum(src, seg, n)
kernel_name = 'mk_flamingo_gated_d2_seqx_r8_5927fa'

def setup_inputs(seed: int=0):
    np.random.seed(seed)
    _w = jnp.asarray

    def _rec_inputs():
        import jax
        import jax.numpy as jnp
        _rk = jax.random.key(seed)
        x = 2.818e-05 + 1 * jax.random.normal(jax.random.fold_in(_rk, 1), (4, 256, 256), jnp.float32)
        _lenS = 256 - jax.random.randint(jax.random.fold_in(_rk, 7), (4,), 0, max(1, 256 // 4) + 1, jnp.int32)
        _lenS2 = 256 - jax.random.randint(jax.random.fold_in(_rk, 8), (4,), 0, max(1, 256 // 4) + 1, jnp.int32)
        _ctx_1024P = jax.random.normal(jax.random.fold_in(_rk, 11), (4, 16, 128), jnp.float32)
        _ctx_1024c = jax.random.dirichlet(jax.random.fold_in(_rk, 511), 0.3 * jnp.ones((16,), jnp.float32), (4, 256))
        _ctx_1024t = jnp.einsum('bsk,bkd->bsd', _ctx_1024c, _ctx_1024P)
        _ctx_1024t = _ctx_1024t * jax.lax.rsqrt(jnp.mean(jnp.square(_ctx_1024t)) + 1e-12) * 0.953939
        ctx_1024 = 7.22013e-05 + 1.00017 * (_ctx_1024t + 0.3 * jax.random.normal(jax.random.fold_in(_rk, 611), (4, 256, 128), jnp.float32))
        fside_BxSx2_0 = jax.random.uniform(jax.random.fold_in(_rk, 12), (4, 256, 2), jnp.float32, 0.0, 0.999707)
        _g = jax.random.normal(jax.random.fold_in(_rk, 9001), (2, 2), jnp.float32)
        _g = jnp.sign(_g) * jnp.maximum(jnp.abs(_g), 1.0) + (_g == 0) * 1.0
        g_xattn = _g[0]
        g_ffn = _g[1]
        return (x, ctx_1024, fside_BxSx2_0, g_xattn, g_ffn)
    x, ctx_1024, fside_BxSx2_0, g_xattn, g_ffn = _rec_inputs()

    def _L0_xattn_setup():
        import jax, jax.numpy as jnp
        import numpy as np
        B_, L_, D_MODEL = (4, 256, 128)
        D_STATE, D_CONV, EXPAND = (16, 4, 2)
        D_INNER = EXPAND * D_MODEL
        DT_RANK = (D_MODEL + 15) // 16

        def silu(x):
            return x * jax.nn.sigmoid(x)
        key = jax.random.key(seed)
        ks = jax.random.split(key, 10)
        f32 = jnp.float32
        hidden_states = jax.random.normal(ks[0], (B_, L_, D_MODEL), dtype=f32)
        z = jax.random.normal(ks[1], (B_, D_INNER, L_), dtype=f32)
        in_proj_w = jax.random.normal(ks[2], (D_INNER, D_MODEL), dtype=f32) * 0.02
        conv_w = jax.random.normal(ks[3], (D_INNER, 1, D_CONV), dtype=f32) * 0.1
        conv_b = jax.random.normal(ks[4], (D_INNER,), dtype=f32) * 0.02
        x_proj_w = jax.random.normal(ks[5], (DT_RANK + 2 * D_STATE, D_INNER), dtype=f32) * 0.02
        dt_proj_w = jax.random.uniform(ks[6], (D_INNER, DT_RANK), dtype=f32, minval=-DT_RANK ** (-0.5), maxval=DT_RANK ** (-0.5))
        dt = jnp.exp(jax.random.uniform(ks[7], (D_INNER,), dtype=f32, minval=np.log(0.001), maxval=np.log(0.1)))
        dt_proj_b = jnp.log(jnp.expm1(dt))
        A_log = jnp.log(jnp.broadcast_to(jnp.arange(1, D_STATE + 1, dtype=f32), (D_INNER, D_STATE)))
        D = jnp.ones((D_INNER,), f32)
        return {'hidden_states': hidden_states, 'z': z, 'in_proj_w': in_proj_w, 'conv_w': conv_w, 'conv_b': conv_b, 'x_proj_w': x_proj_w, 'dt_proj_w': dt_proj_w, 'dt_proj_b': dt_proj_b, 'A_log': A_log, 'D': D}
    _L0_xattn_all = _L0_xattn_setup()
    _L0_xattn_in = {k: v for k, v in _L0_xattn_all.items() if k in ('in_proj_w', 'conv_w', 'conv_b', 'x_proj_w', 'dt_proj_w', 'dt_proj_b', 'A_log', 'D')}
    del _L0_xattn_all

    def _L0_ffn_setup():
        import jax, jax.numpy as jnp
        import numpy as np
        B, T, D = (1, 128, 256)
        F_DIM = 176
        E = 8
        TOPK = 2
        key = jax.random.key(seed)
        ks = jax.random.split(key, 5)
        x = jax.random.normal(ks[0], (B, T, D), dtype=jnp.float32)
        gate_w = jax.random.normal(ks[1], (E, D), dtype=jnp.float32) * 0.02
        gate_proj = jax.random.normal(ks[2], (E, F_DIM, D), dtype=jnp.float32) * 0.02
        up_proj = jax.random.normal(ks[3], (E, F_DIM, D), dtype=jnp.float32) * 0.02
        down_proj = jax.random.normal(ks[4], (E, D, F_DIM), dtype=jnp.float32) * 0.02
        return {'x': x, 'gate_w': gate_w, 'gate_proj': gate_proj, 'up_proj': up_proj, 'down_proj': down_proj}
    _L0_ffn_all = _L0_ffn_setup()
    _L0_ffn_in = {k: v for k, v in _L0_ffn_all.items() if k in ('gate_w', 'gate_proj', 'up_proj', 'down_proj')}
    del _L0_ffn_all

    def _L1_xattn_setup():
        import jax, jax.numpy as jnp
        import numpy as np
        DIM = 256
        CTX_DIM = 128
        N_HEADS = 32
        HEAD_DIM = DIM // N_HEADS
        POS_DIM = 2
        B, N, CTXN = (2, 256, 256)
        ROPE_BASE = 10000.0

        def apply_axial_rope(x, pos):
            b, n, h, d = x.shape
            p = pos.shape[-1]
            dpa = d // p
            half = dpa // 2
            freqs = ROPE_BASE ** (-jnp.arange(half, dtype=x.dtype) / half)
            ang = pos[..., :, None] * freqs
            cos = jnp.cos(ang)[:, :, None, :, :]
            sin = jnp.sin(ang)[:, :, None, :, :]
            xr = x.reshape(b, n, h, p, half, 2)
            x1, x2 = (xr[..., 0], xr[..., 1])
            out = jnp.stack([x1 * cos - x2 * sin, x1 * sin + x2 * cos], axis=-1)
            return out.reshape(b, n, h, d)
        key = jax.random.key(seed)
        ks = jax.random.split(key, 8)
        x = jax.random.normal(ks[0], (B, N, DIM), jnp.float32)
        ctx = jax.random.normal(ks[1], (B, CTXN, CTX_DIM), jnp.float32)
        pos_map = jax.random.uniform(ks[2], (B, N, POS_DIM), jnp.float32)
        ctx_pos_map = jax.random.uniform(ks[3], (B, CTXN, POS_DIM), jnp.float32)
        Wq = jax.random.normal(ks[4], (DIM, DIM), jnp.float32) / np.sqrt(DIM)
        Wkv = jax.random.normal(ks[5], (CTX_DIM, 2 * DIM), jnp.float32) / np.sqrt(CTX_DIM)
        Wout = jax.random.normal(ks[6], (DIM, DIM), jnp.float32) / np.sqrt(DIM)
        bout = jnp.zeros((DIM,), jnp.float32)
        return {'x': x, 'ctx': ctx, 'pos_map': pos_map, 'ctx_pos_map': ctx_pos_map, 'Wq': Wq, 'Wkv': Wkv, 'Wout': Wout, 'bout': bout}
    _L1_xattn_all = _L1_xattn_setup()
    _L1_xattn_in = {k: v for k, v in _L1_xattn_all.items() if k in ('Wq', 'Wkv', 'Wout', 'bout')}
    del _L1_xattn_all

    def _L1_ffn_setup():
        import jax, jax.numpy as jnp
        import numpy as np
        import math
        N_EMBD = 256
        N_HEAD = 16
        HEAD_DIM = N_EMBD // N_HEAD
        B, T = (2, 256)
        key = jax.random.key(seed)
        k1, k2, k3 = jax.random.split(key, 3)
        x = jax.random.normal(k1, (B, T, N_EMBD), dtype=jnp.float32)
        W_gate = jax.random.normal(k2, (N_HEAD, N_EMBD), dtype=jnp.float32) * 0.02
        W_qkv = jax.random.normal(k3, (3 * N_EMBD, N_EMBD), dtype=jnp.float32) * 0.02
        return {'x': x, 'W_gate': W_gate, 'W_qkv': W_qkv}
    _L1_ffn_all = _L1_ffn_setup()
    _L1_ffn_in = {k: v for k, v in _L1_ffn_all.items() if k in ('W_gate', 'W_qkv')}
    del _L1_ffn_all
    return {'x': x, 'ctx_1024': ctx_1024, 'fside_BxSx2_0': fside_BxSx2_0, 'g_xattn': g_xattn, 'g_ffn': g_ffn, 'L0_xattn_in_proj_w': _L0_xattn_in['in_proj_w'], 'L0_xattn_conv_w': _L0_xattn_in['conv_w'], 'L0_xattn_conv_b': _L0_xattn_in['conv_b'], 'L0_xattn_x_proj_w': _L0_xattn_in['x_proj_w'], 'L0_xattn_dt_proj_w': _L0_xattn_in['dt_proj_w'], 'L0_xattn_dt_proj_b': _L0_xattn_in['dt_proj_b'], 'L0_xattn_A_log': _L0_xattn_in['A_log'], 'L0_xattn_D': _L0_xattn_in['D'], 'L0_ffn_gate_w': _L0_ffn_in['gate_w'], 'L0_ffn_gate_proj': _L0_ffn_in['gate_proj'], 'L0_ffn_up_proj': _L0_ffn_in['up_proj'], 'L0_ffn_down_proj': _L0_ffn_in['down_proj'], 'L1_xattn_Wq': _L1_xattn_in['Wq'], 'L1_xattn_Wkv': _L1_xattn_in['Wkv'], 'L1_xattn_Wout': _L1_xattn_in['Wout'], 'L1_xattn_bout': _L1_xattn_in['bout'], 'L1_ffn_W_gate': _L1_ffn_in['W_gate'], 'L1_ffn_W_qkv': _L1_ffn_in['W_qkv']}

def reference(x, ctx_1024, fside_BxSx2_0, g_xattn, g_ffn, L0_xattn_in_proj_w, L0_xattn_conv_w, L0_xattn_conv_b, L0_xattn_x_proj_w, L0_xattn_dt_proj_w, L0_xattn_dt_proj_b, L0_xattn_A_log, L0_xattn_D, L0_ffn_gate_w, L0_ffn_gate_proj, L0_ffn_up_proj, L0_ffn_down_proj, L1_xattn_Wq, L1_xattn_Wkv, L1_xattn_Wout, L1_xattn_bout, L1_ffn_W_gate, L1_ffn_W_qkv):
    import jax
    import jax.numpy as jnp

    def _L0_xattn_ref(hidden_states, z, in_proj_w, conv_w, conv_b, x_proj_w, dt_proj_w, dt_proj_b, A_log, D):
        import jax, jax.numpy as jnp
        import numpy as np
        B_, L_, D_MODEL = (4, 256, 128)
        D_STATE, D_CONV, EXPAND = (16, 4, 2)
        D_INNER = EXPAND * D_MODEL
        DT_RANK = (D_MODEL + 15) // 16

        def silu(x):
            return x * jax.nn.sigmoid(x)
        Bsz, L, _ = hidden_states.shape
        d_inner, _, d_conv = conv_w.shape
        dt_rank = dt_proj_w.shape[1]
        d_state = A_log.shape[1]
        x = jnp.einsum('bld,ed->bel', hidden_states, in_proj_w)
        xc = jax.lax.conv_general_dilated(x, conv_w, window_strides=(1,), padding=[(d_conv - 1, 0)], feature_group_count=d_inner, dimension_numbers=('NCH', 'OIH', 'NCH'))
        x = silu(xc + conv_b[None, :, None])
        x_dbl = jnp.einsum('bdl,ed->bel', x, x_proj_w)
        dt_low, Bm, Cm = jnp.split(x_dbl, [dt_rank, dt_rank + d_state], axis=1)
        dt = jnp.einsum('brl,dr->bdl', dt_low, dt_proj_w)
        dt = jax.nn.softplus(dt + dt_proj_b[None, :, None])
        A = -jnp.exp(A_log)
        dt_t = jnp.moveaxis(dt, -1, 0)
        B_t = jnp.moveaxis(Bm, -1, 0)
        C_t = jnp.moveaxis(Cm, -1, 0)
        u_t = jnp.moveaxis(x, -1, 0)

        def step(state, inp):
            d, b, c, u = inp
            dA = jnp.exp(d[..., None] * A)
            state = state * dA + (d * u)[..., None] * b[:, None, :]
            y = jnp.einsum('bdn,bn->bd', state, c)
            return (state, y)
        state0 = jnp.zeros((Bsz, d_inner, d_state), x.dtype)
        _, ys = jax.lax.scan(step, state0, (dt_t, B_t, C_t, u_t))
        y = jnp.moveaxis(ys, 0, 2)
        y = y + D[None, :, None] * x
        y = y * silu(z)
        return jnp.swapaxes(y, 1, 2)

    def _L0_ffn_ref(x, gate_w, gate_proj, up_proj, down_proj):
        import jax, jax.numpy as jnp
        import numpy as np
        B, T, D = (1, 128, 256)
        F_DIM = 176
        E = 8
        TOPK = 2
        b, t, d = x.shape
        x_flat = x.reshape(-1, d)
        n = x_flat.shape[0]
        router_logits = x_flat @ gate_w.T
        top_w, sel = jax.lax.top_k(router_logits, TOPK)
        top_w = jax.nn.softmax(top_w, axis=-1)
        tok_ids = jnp.arange(n)[:, None]
        tw = jnp.zeros((n, E), dtype=x.dtype).at[tok_ids, sel].add(top_w)
        g = jnp.einsum('nd,efd->enf', x_flat, gate_proj)
        u = jnp.einsum('nd,efd->enf', x_flat, up_proj)
        h = jax.nn.silu(g) * u
        eo = jnp.einsum('enf,edf->end', h, down_proj)
        out = jnp.einsum('end,ne->nd', eo, tw)
        return out.reshape(b, t, d)

    def _L1_xattn_ref(x, ctx, pos_map, ctx_pos_map, Wq, Wkv, Wout, bout):
        import jax, jax.numpy as jnp
        import numpy as np
        DIM = 256
        CTX_DIM = 128
        N_HEADS = 32
        HEAD_DIM = DIM // N_HEADS
        POS_DIM = 2
        B, N, CTXN = (2, 256, 256)
        ROPE_BASE = 10000.0

        def apply_axial_rope(x, pos):
            b, n, h, d = x.shape
            p = pos.shape[-1]
            dpa = d // p
            half = dpa // 2
            freqs = ROPE_BASE ** (-jnp.arange(half, dtype=x.dtype) / half)
            ang = pos[..., :, None] * freqs
            cos = jnp.cos(ang)[:, :, None, :, :]
            sin = jnp.sin(ang)[:, :, None, :, :]
            xr = x.reshape(b, n, h, p, half, 2)
            x1, x2 = (xr[..., 0], xr[..., 1])
            out = jnp.stack([x1 * cos - x2 * sin, x1 * sin + x2 * cos], axis=-1)
            return out.reshape(b, n, h, d)
        b, n, _ = x.shape
        ctx_n = ctx.shape[1]
        q = (x @ Wq).reshape(b, n, N_HEADS, HEAD_DIM)
        k, v = jnp.split(ctx @ Wkv, 2, axis=-1)
        k = k.reshape(b, ctx_n, N_HEADS, HEAD_DIM)
        v = v.reshape(b, ctx_n, N_HEADS, HEAD_DIM)
        q = apply_axial_rope(q, pos_map)
        k = apply_axial_rope(k, ctx_pos_map)
        scale = 1.0 / np.sqrt(HEAD_DIM).astype(np.float32)
        logits = jnp.einsum('bqhd,bkhd->bhqk', q, k) * scale
        w = jax.nn.softmax(logits, axis=-1)
        attn = jnp.einsum('bhqk,bkhd->bqhd', w, v)
        attn = attn.reshape(b, n, N_HEADS * HEAD_DIM)
        return attn @ Wout + bout

    def _L1_ffn_ref(x, W_gate, W_qkv):
        import jax, jax.numpy as jnp
        import numpy as np
        import math
        N_EMBD = 256
        N_HEAD = 16
        HEAD_DIM = N_EMBD // N_HEAD
        B, T = (2, 256)
        Bb, Tt, C = x.shape
        H, hd = (N_HEAD, HEAD_DIM)
        gating = jax.nn.softmax(x @ W_gate.T, axis=-1)
        idx = jnp.argmax(gating, axis=-1)
        indicator = jax.nn.one_hot(idx, H, dtype=gating.dtype)
        top1_val = jnp.max(gating, axis=-1, keepdims=True)
        gating_top1 = indicator * top1_val
        qkv = x @ W_qkv.T
        q, k, v = jnp.split(qkv, 3, axis=-1)
        k = k.reshape(Bb, Tt, H, hd)
        v = v.reshape(Bb, Tt, H, hd)
        k_shared = jnp.einsum('bth,bthd->btd', indicator, k)
        v_shared = jnp.einsum('bth,bthd->btd', gating_top1, v)
        q = q.reshape(Bb, Tt, H, hd).transpose(0, 2, 1, 3)
        att = jnp.einsum('bhqd,bkd->bhqk', q, k_shared) * (1.0 / math.sqrt(hd))
        causal = jnp.tril(jnp.ones((Tt, Tt), dtype=bool))
        att = jnp.where(causal[None, None, :, :], att, -jnp.inf)
        att = jax.nn.softmax(att, axis=-1)
        y = jnp.einsum('bhqk,bkd->bhqd', att, v_shared)
        y = y.transpose(0, 2, 1, 3).reshape(Bb, Tt, C)
        return y
    x = x + jnp.tanh(g_xattn[0]) * _L0_xattn_ref(ctx_1024, _layernorm(x, axis=-1), L0_xattn_in_proj_w, L0_xattn_conv_w, L0_xattn_conv_b, L0_xattn_x_proj_w, L0_xattn_dt_proj_w, L0_xattn_dt_proj_b, L0_xattn_A_log, L0_xattn_D)
    x = x + jnp.tanh(g_ffn[0]) * _L0_ffn_ref(_layernorm(x, axis=-1), L0_ffn_gate_w, L0_ffn_gate_proj, L0_ffn_up_proj, L0_ffn_down_proj)
    x = x + jnp.tanh(g_xattn[1]) * _L1_xattn_ref(_layernorm(x, axis=-1), ctx_1024, fside_BxSx2_0, fside_BxSx2_0, L1_xattn_Wq, L1_xattn_Wkv, L1_xattn_Wout, L1_xattn_bout)
    x = x + jnp.tanh(g_ffn[1]) * _L1_ffn_ref(_layernorm(x, axis=-1), L1_ffn_W_gate, L1_ffn_W_qkv)
    return x

_drawn_inputs = setup_inputs


def setup_inputs(seed=0):
    import zlib

    import numpy as np

    out = dict(_drawn_inputs(seed))
    spreads = {'g_ffn': (-1.0, 0.6), 'L0_xattn_D': (1.0, 0.6), 'L1_xattn_bout': (0.0, 0.8)}
    factors = {'L0_xattn_in_proj_w': 6.258,
     'L0_xattn_conv_w': 6.502,
     'L0_xattn_conv_b': 8.0,
     'L0_xattn_x_proj_w': 8.0,
     'L0_xattn_dt_proj_w': 8.0,
     'L0_xattn_dt_proj_b': 8.0,
     'L0_xattn_A_log': 8.0,
     'L0_ffn_gate_w': 8.0,
     'L0_ffn_gate_proj': 8.0,
     'L0_ffn_up_proj': 8.0,
     'L0_ffn_down_proj': 8.0,
     'L1_ffn_W_gate': 39.328,
     'L1_ffn_W_qkv': 28.44,
     'fside_BxSx2_0': 8.0,
     'L1_xattn_Wq': 8.0,
     'L1_xattn_Wkv': 4.017,
     'L1_xattn_Wout': 3.985}
    for name, (base, spread) in spreads.items():
        noise = np.random.default_rng([zlib.crc32(name.encode()), seed]).standard_normal(out[name].shape)
        drawn = base * np.exp(spread * noise) if base else spread * noise
        out[name] = jnp.asarray(drawn.astype(out[name].dtype))
    for name, factor in factors.items():
        out[name] = (out[name] * factor).astype(out[name].dtype)
    return out
```

```python
from contextlib import ExitStack

import concourse.bass as bass
from concourse import mybir

F32 = mybir.dt.float32
BF16 = mybir.dt.bfloat16
I32 = mybir.dt.int32
ALU = mybir.AluOpType
ACT = mybir.ActivationFunctionType
AX = mybir.AxisListType

P = 128
B, L, C = 4, 256, 256
T = B * L // P
NT = B * L
CTX = 128
NS, RANK, KCONV = 16, 8, 4
E, FD = 8, 176
NF = E * FD // P
H1, D1 = 32, 8
H2, D2 = 16, 16
EPS = 1e-5
SMALL = 0.05
TWO_PI_HI = 6.28125
TWO_PI_LO = 2.0 * 3.141592653589793 - 6.28125
ROUND = 12582912.0
PI_IN = 3.1415925


def flamingo_program(nc, d, out):
    ctx = ExitStack()
    with ctx:
        def sb(name, shape, dt=F32):
            return ctx.enter_context(nc.sbuf_tensor(name, shape, dt))

        sems = {}

        def S(name):
            if name not in sems:
                sems[name] = ctx.enter_context(nc.semaphore(name))
            return sems[name]

        x = sb("x", [P, T, C])
        xn = sb("xn", [P, T, C])
        xnT = sb("xnT", [P, 2, NT])
        stats = sb("stats", [P, T, 6])
        mv = sb("mv", [P, T, 2])
        lnv = sb("lnv", [P, T])
        rstd = sb("rstd", [P, T])
        gates = sb("gates", [P, 4])
        tg = sb("tg", [P, 4])
        consts = sb("consts", [P, 4])
        ident = sb("ident", [P, P])
        identb = sb("identb", [P, P], BF16)
        negsel = sb("negsel", [64, H1, P], BF16)
        maskA = sb("maskA", [P, 2, 256], BF16)
        maskB = sb("maskB", [P, 2, 256], BF16)
        hm1 = sb("hm1", [P, 4])
        hm2 = sb("hm2", [P, 2])
        rank8 = sb("rank8", [P, E])
        rank16 = sb("rank16", [P, H2])
        onesr = sb("onesr", [1, P])
        wq1 = sb("wq1", [P, 2, C])
        wq2 = sb("wq2", [P, 2, C])
        wout = sb("wout", [P, 2, C])
        bout = sb("bout", [1, C])
        wqkv = sb("wqkv", [P, 2, 3 * C])
        wg16 = sb("wg16", [P, 2, H2])
        wg8 = sb("wg8", [P, 2, E])
        ex8 = sb("ex8", [E, NF, P])
        k1T = sb("k1T", [P, 2, NT])
        k2T = sb("k2T", [P, 2, NT])
        vaug = sb("vaug", [P, T, H1, 32])
        cosT = sb("cosT", [P, NT])
        sinT = sb("sinT", [P, NT])
        area = sb("area", [P, 22000])
        used = [0]

        def part(shape, dt=F32, rows=P):
            n = 1
            for s in shape:
                n *= s
            w = n if dt != BF16 else n // 2
            a = area[0:rows, used[0]:used[0] + w]
            used[0] += w
            if dt != F32:
                a = a.bitcast(dt)
            if len(shape) == 2:
                a = a.rearrange("p (a b) -> p a b", a=shape[0])
            elif len(shape) == 3:
                a = a.rearrange("p (a b c) -> p a b c", a=shape[0], b=shape[1])
            return a

        wk1 = part([C]); wk2 = part([C]); wv = part([C]); win = part([C])
        ctxT = part([NT])
        xproj = part([2, 104]); dtw = part([C]); convw = part([2, KCONV]); convb = part([2])
        dtb = part([2]); negA = part([2, NS]); Dp = part([2])
        pos = part([T, 2]); ang = part([T, 8]); rnd = part([T, 8]); trig = part([T, 8])
        ecs = part([2, P], rows=8); csT = part([NT], rows=8)
        sel = part([2 * NS, P], BF16, rows=96)
        dsplit = part([NT], BF16, rows=96)
        zg = part([2, NT]); u = part([2, NT]); dt = part([2, NT]); w = part([2, NT])
        scan0 = used[0]
        xin = part([2, B * (L + 3)]); mid3 = part([NT], rows=P); conv = part([2, NT])
        midb = part([NT], BF16, rows=96); lob = part([NT], BF16, rows=96); hib = part([NT], BF16, rows=96)
        end0 = used[0]
        xp = xin.rearrange("p a (b l) -> p a b l", b=B)
        absx = xin[:, :, 0:NT]
        expx = conv
        used[0] = scan0
        dA = [part([NT]) for _ in range(2)]
        end0 = max(end0, used[0])
        used[0] = scan0
        dA = [part([NT]) for _ in range(2)]
        Bsb = [area[:, 0:NT], area[:, NT:2 * NT]]
        dBu = part([2, NT]); hst = part([2, NT])
        prod = xn[:, :, :].rearrange("p (a t) c -> p a (t c)", a=2)
        assert max(end0, used[0]) <= 22000, (end0, used[0])
        yT = xnT
        used[0] = 0
        gateT = part([2, E * FD]); upT = part([2, E * FD]); downT = part([NF, C])
        hid = part([NF, 512])
        sg = part([2, 512]); h1 = part([2, 512])
        rl = part([T, E]); i1 = part([T, E]); i2 = part([T, E]); tmp8 = part([T, E]); tw = part([T, E])
        m1 = part([T]); m2 = part([T]); mi = part([T]); w1 = part([T]); w2 = part([T]); twT = part([NT], rows=8)
        assert used[0] <= 22000, used[0]
        used[0] = 0
        qm = part([2, 4, NT])
        Pb = [part([4 * 256]) for _ in range(4)]
        osb = part([8, 256]); qr = part([2, NT]); attn = part([T, C])
        mx = part([T, 64]); mTb = part([NT], BF16, rows=64); rec = part([T, H1]); mlow = part([NT], rows=64)
        assert used[0] <= 22000, used[0]
        qm2 = qm[:, :, 0:2, :]
        ksT = k1T[:, 0, :]
        krep = attn[:, :, 0:P]
        kv = k2T[:, 0, 0:256]
        gl = rec
        va2 = vaug[:, :, 0, :]
        gi = sb("gi", [P, T, H2]); gm = sb("gm", [P, T]); gt = sb("gt", [P, T, H2]); gs = sb("gs", [P, T])
        kvp = sb("kvp", [P, 2, 512]); ksv = sb("ksv", [P, T, 2, D2])
        fin = sb("fin", [P, 2, C])

        psum = ctx.enter_context(nc.psum_tensor("psum", [P, 8, 512], F32))

        def bank(i, n=1):
            return psum[:, i:i + n, :].rearrange("p a b -> p (a b)")

        dqs = []

        block = ctx.enter_context(nc.Block())
        xt = d["x"].rearrange("b (t p) c -> p (b t) c", p=P)
        ot = out.rearrange("b (t p) c -> p (b t) c", p=P)

        @block.sync
        def _(sp):
            def load(dst, name, s):
                sp.dma_start(dst, d[name]).then_inc(S(s), 16)

            load(ctxT, "ctxT", "ld_in")
            load(win, "win", "ld_in")
            sp.dma_start(x[:, :, :], xt).then_inc(S("ld_x"), 16)
            load(pos, "pos", "ld_pos")
            for dst, name in ((convw, "convw"), (convb, "convb"), (xproj, "xproj"), (dtb, "dtb"),
                              (negA, "alog"), (Dp, "dp"), (gates[:, :], "gates"), (ident[:, :], "ident"), (ecs, "ecs"),
                              (sel, "sel"), (hm1[:, :], "hm1"), (hm2[:, :], "hm2"), (consts[:, :], "consts")):
                load(dst, name, "ld_small")
            sp.dma_start(dtw[96:104, :], d["dtw"]).then_inc(S("ld_small"), 16)
            for dst, name in ((wv, "wv"), (wk1, "wk1"), (wk2, "wk2")):
                load(dst, name, "ld_kv")
            for dst, name in ((identb[:, :], "identb"), (negsel[:, :, :], "negsel"), (maskA[:, :, :], "maskA"),
                              (maskB[:, :, :], "maskB"), (rank8[:, :], "rank8"), (rank16[:, :], "rank16"),
                              (wq1[:, :, :], "wq1"), (wq2[:, :, :], "wq2"), (wout[:, :, :], "wout"),
                              (bout[:, :], "bout"), (wqkv[:, :, :], "wqkv"), (wg16[:, :, :], "wg16"),
                              (wg8[:, :, :], "wg8"), (ex8[:, :, :], "ex8"), (onesr[:, :], "onesr")):
                load(dst, name, "ld_late")
            sp.wait_ge(S("y_gated"), 2)
            for dst, name in ((gateT, "gateT"), (upT, "upT")):
                load(dst, name, "ld_moe")
            load(downT, "downT", "ld_down")
            for t in range(T // 2):
                sp.wait_ge(S("fin_ready"), t + 1)
                sp.dma_start(ot[:, 2 * t:2 * t + 2, :], x[:, 2 * t:2 * t + 2, :]).then_inc(S("stored"), 16)
            sp.wait_ge(S("stored"), 16 * (T // 2))

        @block.tensor
        def _(pe):
            def turn_tiles(src_of, at, ready, done):
                for t in range(T):
                    pe.wait_ge(S(ready), t + 1)
                    for k in range(2):
                        m = pe.transpose(psum[:, at + 2 * k + t // 4, P * (t % 4):P * (t % 4) + P],
                                         src_of(t, k), ident[:, :])
                    m.then_inc(S(done), 1)

            pe.wait_ge(S("ld_in"), 32)
            for k in range(2):
                for c in range(2):
                    m = pe.matmul(bank(2 * k + c), win[:, P * k:P * k + P], ctxT[:, 512 * c:512 * c + 512],
                                  start=True, stop=True)
            m.then_inc(S("inproj"), 1)
            pe.wait_ge(S("ld_small"), 16 * 14)
            pe.wait_ge(S("trig_ready"), 1)
            for t in range(T):
                m = pe.transpose(psum[0:8, 4 + t // 4, P * (t % 4):P * (t % 4) + P], trig[:, t, :], ident[:, :])
            m.then_inc(S("cs_turned"), 1)
            pe.wait_ge(S("cs_copied"), 1)
            for i in range(2):
                for c in range(2):
                    m = pe.matmul(bank(6 - 2 * i + c), ecs[:, i, :], csT[:, 512 * c:512 * c + 512],
                                  start=True, stop=True)
                m.then_inc(S("cs_spread"), 1)
            pe.wait_ge(S("ld_kv"), 48)
            pe.wait_ge(S("cs_out"), 2)
            for t in range(T):
                m = pe.matmul(psum[:, 4 + t // 2, C * (t % 2):C * (t % 2) + C], ctxT[:, P * t:P * t + P], wv[:, :],
                              start=True, stop=True)
            m.then_inc(S("v_proj"), 1)
            pe.wait_ge(S("u_ready"), 2)
            pe.wait_ge(S("xin_copied"), 2)
            for c in range(2):
                for k in range(2):
                    m = pe.matmul(psum[0:104, c, :], xproj[:, k, :], u[:, k, 512 * c:512 * c + 512],
                                  start=(k == 0), stop=(k == 1))
            m.then_inc(S("xdbl"), 1)
            pe.wait_ge(S("v_out"), 4)
            for n, wk in enumerate((wk1, wk2)):
                if n:
                    pe.wait_ge(S("k_out"), 2)
                for k in range(2):
                    for c in range(2):
                        m = pe.matmul(bank(4 + 2 * k + c), wk[:, P * k:P * k + P], ctxT[:, 512 * c:512 * c + 512],
                                      start=True, stop=True)
                m.then_inc(S("k_proj"), 1)
                if n == 0:
                    pe.wait_ge(S("dtlow"), 1)
                    pe.wait_ge(S("split_read"), 1)
                    for k in range(2):
                        for c in range(2):
                            m = pe.matmul(bank(2 * k + c), dtw[96:104, P * k:P * k + P],
                                          mid3[96:104, 512 * c:512 * c + 512], start=True, stop=True)
                    m.then_inc(S("dtpre"), 1)
            units = 2 * NS
            pe.wait_ge(S("split_done"), 1)
            pe.wait_ge(S("dtpre_read"), 4)
            pe.wait_ge(S("k_out"), 4)

            def spread(at, row):
                for c in range(2):
                    m = pe.matmul(bank(at + c), sel[:, row, :], dsplit[:, 512 * c:512 * c + 512],
                                  start=True, stop=True)
                return m

            def add_state(i):
                pe.wait_ge(S("prod_ready"), i + 1)
                if i == NS:
                    pe.wait_ge(S("y_taken"), 1)
                for c in range(2):
                    m = pe.matmul(bank(6 + c), ident[:, :], prod[:, i % 2, 512 * c:512 * c + 512],
                                  start=(i % NS == 0), stop=(i % NS == NS - 1))
                m.then_inc(S("y_sum"), 1)

            for i in range(units):
                n = i % NS
                if i >= 2:
                    pe.wait_ge(S("b_copied"), i - 1)
                spread(2 * (i % 2), n).then_inc(S("b_spread"), 1)
                if i >= 1:
                    pe.wait_ge(S("prod_ready"), i)
                spread(4, NS + n).then_inc(S("c_spread"), 1)
                if i >= 1:
                    add_state(i - 1)
            add_state(units - 1)
            pe.wait_ge(S("b_copied"), units)
            pe.wait_ge(S("y_gated"), 2)
            for t in range(T):
                for k in range(2):
                    m = pe.transpose(psum[:, t // 2, C * (t % 2) + P * k:C * (t % 2) + P * k + P],
                                     yT[:, k, P * t:P * t + P], ident[:, :])
                if t % 2:
                    m.then_inc(S("y_turned"), 1)

            pe.wait_ge(S("ld_late"), 16 * 15)
            pe.wait_ge(S("x1"), 4)
            turn_tiles(lambda t, k: xn[:, t, P * k:P * k + P], 0, "xn1", "n1_turned")
            pe.wait_ge(S("n1_out"), 4)
            for t in range(T):
                for k in range(2):
                    m = pe.matmul(psum[:, 4, E * t:E * t + E], xnT[:, k, P * t:P * t + P], wg8[:, k, :],
                                  start=(k == 0), stop=(k == 1))
            m.then_inc(S("router"), 1)
            pe.wait_ge(S("ld_moe"), 32)

            def weights_of(i):
                c = i // NF
                if i == 0:
                    pe.wait_ge(S("tw_ready"), 1)
                    for t in range(T):
                        m = pe.transpose(psum[0:E, 6 + t // 4, P * (t % 4):P * (t % 4) + P], tw[:, t, :],
                                         ident[:, :])
                    m.then_inc(S("tw_turned"), 1)
                    pe.wait_ge(S("twT_ready"), 1)
                if i >= 2:
                    pe.wait_ge(S("hid_ready"), i - 1)
                pe.matmul(bank(3 * (i % 2) + 2), ex8[:, i % NF, :], twT[:, 512 * c:512 * c + 512],
                          start=True, stop=True).then_inc(S("tw_spread"), 1)

            def down(c):
                pe.wait_ge(S("hid_ready"), NF * (c + 1))
                if c:
                    pe.wait_ge(S("x2"), 2)
                for t in range(4):
                    for f in range(NF):
                        m = pe.matmul(psum[:, 6 + t // 2, C * (t % 2):C * (t % 2) + C],
                                      hid[:, f, P * t:P * t + P], downT[:, f, :],
                                      start=(f == 0), stop=(f == NF - 1))
                    if t % 2:
                        m.then_inc(S("down"), 1)

            for i in range(2 * NF):
                c, f = i // NF, i % NF
                if i == 1:
                    pe.wait_ge(S("router_read"), 1)
                if i >= 2:
                    pe.wait_ge(S("silu_done"), i - 1)
                    pe.wait_ge(S("gu_done"), i - 1)
                for n, wt in enumerate((gateT, upT)):
                    for k in range(2):
                        m = pe.matmul(bank(3 * (i % 2) + n), wt[:, k, P * f:P * f + P],
                                      xnT[:, k, 512 * c:512 * c + 512], start=(k == 0), stop=(k == 1))
                    m.then_inc(S("gate_up"), 1)
                if i >= 1:
                    weights_of(i - 1)
                if i == NF:
                    pe.wait_ge(S("ld_down"), 16)
                    down(0)
            weights_of(2 * NF - 1)
            down(1)

            pe.wait_ge(S("x2"), 4)
            turn_tiles(lambda t, k: xn[:, t, P * k:P * k + P], 0, "xn2", "n2_turned")
            pe.wait_ge(S("n2_out"), 4)
            for n, wt in enumerate((wq1, wq2)):
                for k in range(2):
                    for c in range(2):
                        for kk in range(2):
                            m = pe.matmul(bank(4 * n + 2 * k + c), wt[:, kk, P * k:P * k + P],
                                          xnT[:, kk, 512 * c:512 * c + 512], start=(kk == 0), stop=(kk == 1))
                    m.then_inc(S("q_proj"), 1)
            pe.wait_ge(S("q_masked"), 8)
            pe.wait_ge(S("k_rotated"), 1)
            for g in range(T * 8):
                t, half, rg = g // 8, g // 4 % 2, g % 4
                r = slice(32 * rg, 32 * rg + 32)
                if g >= 4:
                    pe.wait_ge(S("max1"), g - 3)
                for j in range(4):
                    m = pe.matmul(psum[:, 2 * (g % 4) + j // 2, 256 * (j % 2):256 * (j % 2) + 256],
                                  qm[r, half, j, P * t:P * t + P], k1T[r, half, L * (t // 2):L * (t // 2) + L],
                                  start=True, stop=True)
                m.then_inc(S("logit1"), 1)

            def turn_maxima(ready, done):
                pe.wait_ge(S(ready), 1)
                for t in range(T):
                    m = pe.transpose(psum[0:64, t // 4, P * (t % 4):P * (t % 4) + P], mx[:, t, :], ident[:, :])
                m.then_inc(S(done), 1)

            turn_maxima("mx_dup1", "mx_turned1")
            pe.wait_ge(S("m_split1"), 1)

            def weighted(tag, g, per, lhs_of, cols):
                pe.wait_ge(S("prob" + tag), 2 * g + 2)
                if g >= 2:
                    pe.wait_ge(S("o_copied" + tag), g - 1)
                for kt in range(2):
                    q0 = cols[kt]
                    for j in range(4):
                        n = 256 - q0
                        m = pe.matmul(psum[32 * j:32 * j + 32, 4 + g % 2, q0:256], lhs_of(g, kt, j),
                                      Pb[2 * (g % 2) + kt][:, n * j:n * j + n],
                                      start=(kt == 0), stop=(kt == 1), skip_group_check=True,
                                      tile_position=(0, 32 * j))
                m.then_inc(S("o_sum" + tag), 1)

            def turn_out(tag, b, per):
                pe.wait_ge(S("o_copied" + tag), per * (b + 1))
                for qt in range(2):
                    i = 2 * b + qt
                    if i >= 1:
                        pe.wait_ge(S("o_norm" + tag), i)
                    for g in range(per):
                        m = pe.transpose(psum[:, 6 + g // 4, P * (g % 4):P * (g % 4) + P],
                                         osb[:, g, P * qt:P * qt + P], ident[:, :])
                    m.then_inc(S("o_turned" + tag), 1)

            for g in range(B * 8):
                b, half, rg = g // 8, g // 4 % 2, g % 4
                r = slice(32 * rg, 32 * rg + 32)
                for kt in range(2):
                    i = 2 * g + kt
                    if i >= 2:
                        pe.wait_ge(S("prob1"), i - 1)
                    for jj in range(2):
                        o = 2 * (i % 2) + jj
                        pe.matmul(bank(o), k1T[r, half, L * b + P * kt:L * b + P * kt + P],
                                  qm[r, half, 2 * jj:2 * jj + 2, L * b:L * b + L], start=True, stop=False,
                                  skip_group_check=True)
                        for j in range(2):
                            m = pe.matmul(psum[:, o, 256 * j:256 * j + 256],
                                          negsel[:, 16 * half + 4 * rg + 2 * jj + j, :], mTb[:, L * b:L * b + L],
                                          start=False, stop=(j == 1), skip_group_check=True)
                    m.then_inc(S("lt1"), 1)
                if g >= 1:
                    weighted("1", g - 1, 8, lambda gg, k, j: vaug[:, 2 * (gg // 8) + k, 4 * (gg % 8) + j, :], (0, 0))
                    if g % 8 == 0:
                        turn_out("1", g // 8 - 1, 8)
            weighted("1", 4 * 8 - 1, 8, lambda gg, k, j: vaug[:, 2 * (gg // 8) + k, 4 * (gg % 8) + j, :], (0, 0))
            turn_out("1", 3, 8)
            turn_tiles(lambda t, k: attn[:, t, P * k:P * k + P], 0, "o_norm1", "attn_turned")
            pe.wait_ge(S("attnT_out"), 4)
            for t in range(T):
                dst = psum[:, 4 + t // 2, C * (t % 2):C * (t % 2) + C]
                if t == 4:
                    pe.wait_ge(S("o_norm1"), 8)
                for k in range(2):
                    pe.matmul(dst, xnT[:, k, P * t:P * t + P], wout[:, k, :], start=(k == 0), stop=False)
                m = pe.matmul(dst, onesr[:, :], bout[:, :], start=False, stop=True)
                if t % 2:
                    m.then_inc(S("proj1"), 1)

            pe.wait_ge(S("x3"), 4)
            turn_tiles(lambda t, k: xn[:, t, P * k:P * k + P], 0, "xn3", "n3_turned")
            pe.wait_ge(S("n3_out"), 4)
            for t in range(T):
                for k in range(2):
                    m = pe.matmul(psum[:, 4, H2 * t:H2 * t + H2], xnT[:, k, P * t:P * t + P], wg16[:, k, :],
                                  start=(k == 0), stop=(k == 1))
            m.then_inc(S("gate_logit"), 1)
            for k in range(2):
                for c in range(2):
                    for kk in range(2):
                        m = pe.matmul(bank(2 * k + c), wqkv[:, kk, P * k:P * k + P],
                                      xnT[:, kk, 512 * c:512 * c + 512], start=(kk == 0), stop=(kk == 1))
                m.then_inc(S("q2_proj"), 1)
            for t in range(T):
                if t >= 2:
                    pe.wait_ge(S("kv_read"), t - 1)
                for kk in range(2):
                    m = pe.matmul(bank(5 + t % 2), xnT[:, kk, P * t:P * t + P], wqkv[:, kk, C:3 * C],
                                  start=(kk == 0), stop=(kk == 1))
                m.then_inc(S("kv_proj"), 1)
            pe.wait_ge(S("krep_ready"), 1)
            pe.wait_ge(S("kv_read"), T)
            for t in range(T):
                m = pe.transpose(psum[:, 6 + t // 4, P * (t % 4):P * (t % 4) + P], krep[:, t, :], ident[:, :])
            m.then_inc(S("ks_turned"), 1)
            pe.wait_ge(S("ks_out"), 1)
            pe.wait_ge(S("q2_masked"), 4)
            for g in range(2 * T):
                t, half = g // 2, g % 2
                qt, b = t % 2, t // 2
                n = P * (qt + 1)
                if g >= 2:
                    pe.wait_ge(S("max2"), g - 1)
                for rg in range(4):
                    r = slice(32 * rg, 32 * rg + 32)
                    o = psum[:, 4 * (g % 2) + rg, 0:2 * n]
                    pe.matmul(o, identb[:, :], maskA[:, :, 256 - n:256], start=True, stop=False,
                              skip_group_check=True)
                    for j in range(2):
                        m = pe.matmul(o[:, n * j:n * j + n], qm2[r, half, j, P * t:P * t + P],
                                      ksT[r, L * b:L * b + n], start=False, stop=(j == 1), skip_group_check=True)
                m.then_inc(S("logit2"), 1)
            turn_maxima("mx_dup2", "mx_turned2")
            pe.wait_ge(S("m_split2"), 1)
            va2_of = lambda gg, k, j: va2[:, 2 * (gg // 4) + k, :]
            for g in range(B * 4):
                b, g4 = g // 4, g % 4
                half = g4 // 2
                for kt in range(2):
                    i = 2 * g + kt
                    n = 256 - P * kt
                    if i >= 2:
                        pe.wait_ge(S("prob2"), i - 1)
                    for jj in range(2):
                        rg = 2 * (g4 % 2) + jj
                        r = slice(32 * rg, 32 * rg + 32)
                        o = psum[:, 2 * (i % 2) + jj, 0:2 * n]
                        pe.matmul(o, identb[:, :], maskB[:, :, 0:n], start=True, stop=False, skip_group_check=True)
                        pe.matmul(o, ksT[r, L * b + P * kt:L * b + P * kt + P],
                                  qm2[r, half, :, L * b + P * kt:L * b + L], start=False, stop=False,
                                  skip_group_check=True)
                        for j in range(2):
                            m = pe.matmul(o[:, n * j:n * j + n], negsel[:, 4 * g4 + 2 * jj + j, :],
                                          mTb[:, L * b + P * kt:L * b + L], start=False, stop=(j == 1),
                                          skip_group_check=True)
                    m.then_inc(S("lt2"), 1)
                if g >= 1:
                    weighted("2", g - 1, 4, va2_of, (0, P))
                    if g % 4 == 0:
                        turn_out("2", g // 4 - 1, 4)
            weighted("2", 15, 4, va2_of, (0, P))
            turn_out("2", 3, 4)

        @block.scalar
        def _(act):
            chain = [0]

            def link(ins):
                chain[0] += 1
                ins.then_inc(S("act_chain"), 1)
                act.wait_ge(S("act_chain"), chain[0])

            def rstd_of(n):
                act.wait_ge(S("mv"), n + 1)
                link(act.activation(lnv[:, :], mv[:, :, 1], ACT.Ln, bias=consts[:, 0:1]))
                act.activation(rstd[:, :], lnv[:, :], ACT.Exp, scale=-0.5).then_inc(S("rstd"), 1)

            def evacuate(turned, done):
                act.wait_ge(S(turned), 4)
                act.activation(xnT[:, 0, 0:512], bank(0), ACT.Copy).then_inc(S(done), 1)
                act.wait_ge(S(turned), 8)
                act.activation(xnT[:, 0, 512:1024], bank(1), ACT.Copy).then_inc(S(done), 1)

            act.wait_ge(S("inproj"), 1)
            act.wait_ge(S("xin_zero"), 1)
            for k in range(2):
                act.activation(xp[:, k, :, 3:3 + L], bank(2 * k, 2).rearrange("p (b l) -> p b l", b=B),
                               ACT.Copy).then_inc(S("xin_copied"), 1)
            act.wait_ge(S("ld_small"), 16 * 14)
            act.activation(tg[:, :], gates[:, :], ACT.Tanh).then_inc(S("tg"), 1)
            act.activation(negA, negA, ACT.Exp).then_inc(S("expA"), 1)
            rstd_of(0)
            act.wait_ge(S("ang_ready"), 1)
            act.activation(trig, ang, ACT.Sin).then_inc(S("trig_ready"), 1)
            act.wait_ge(S("cs_turned"), 1)
            act.activation(csT, psum[0:8, 4:6, :].rearrange("p a b -> p (a b)"), ACT.Copy).then_inc(S("cs_copied"), 1)
            for i, dst in enumerate((cosT, sinT)):
                act.wait_ge(S("cs_spread"), i + 1)
                act.activation(dst[:, :], bank(6 - 2 * i, 2), ACT.Copy).then_inc(S("cs_out"), 1)
            for k in range(2):
                act.wait_ge(S("conv_done"), k + 1)
                act.activation(u[:, k, :], conv[:, k, :], ACT.Silu, bias=convb[:, k:k + 1]).then_inc(S("u_ready"), 1)
            act.wait_ge(S("xn0"), T)
            for k in range(2):
                act.activation(zg[:, k, :].rearrange("p (b l) -> p b l", b=B), xn[:, k:T:2, :], ACT.Silu)\
                   .then_inc(S("z_out"), 1)
            act.wait_ge(S("xdbl"), 1)
            act.activation(mid3[96:104, :], psum[96:104, 0:2, :].rearrange("p a b -> p (a b)"), ACT.Copy)\
               .then_inc(S("dtlow"), 1)
            act.activation(hib, psum[0:96, 0:2, :].rearrange("p a b -> p (a b)"), ACT.Copy).then_inc(S("hi_ready"), 1)
            act.wait_ge(S("v_proj"), 1)
            act.wait_ge(S("vaug_ones"), 1)
            for n in range(4):
                act.activation(vaug[:, 2 * n:2 * n + 2, :, 0:D1],
                               bank(4 + n).rearrange("p (t h e) -> p t h e", t=2, h=H1), ACT.Copy)\
                   .then_inc(S("v_out"), 1)
            act.wait_ge(S("dtpre"), 1)
            for k in range(2):
                act.activation(absx[:, k, :], bank(2 * k, 2), ACT.Abs, bias=dtb[:, k:k + 1])\
                   .then_inc(S("dtpre_read"), 1)
                act.activation(dt[:, k, :], bank(2 * k, 2), ACT.Relu, bias=dtb[:, k:k + 1])\
                   .then_inc(S("dtpre_read"), 1)
            act.wait_ge(S("dtpre_read"), 3)
            for k in range(2):
                if k:
                    act.wait_ge(S("dtpre_read"), 4)
                link(act.activation(expx[:, k, :], absx[:, k, :], ACT.Exp, scale=-1.0))
                act.activation(w[:, k, :], expx[:, k, :], ACT.Ln, bias=consts[:, 1:2]).then_inc(S("ln_ready"), 1)
            for n, dst in enumerate((k1T, k2T)):
                act.wait_ge(S("k_proj"), n + 1)
                for k in range(2):
                    act.activation(dst[:, k, :], bank(4 + 2 * k, 2), ACT.Copy).then_inc(S("k_out"), 1)
            act.wait_ge(S("w_ready"), 1)
            act.wait_ge(S("negA"), 1)
            act.wait_ge(S("dA_zero"), 1)
            for i in range(2 * NS):
                k, n = i // NS, i % NS
                if k and n == 0:
                    act.wait_ge(S("w_ready"), 2)
                act.wait_ge(S("b_spread"), i + 1)
                if i >= 2:
                    act.wait_ge(S("dBu_ready"), i - 1)
                act.activation(Bsb[i % 2], bank(2 * (i % 2), 2), ACT.Copy).then_inc(S("b_copied"), 1)
                if i >= 2:
                    act.wait_ge(S("scanned"), i - 1)
                act.activation(dA[i % 2].rearrange("p (b l) -> p b l", b=B)[:, :, 1:L],
                               dt[:, k, :].rearrange("p (b l) -> p b l", b=B)[:, :, 1:L], ACT.Exp,
                               scale=negA[:, k, n:n + 1]).then_inc(S("dA_ready"), 1)
            rstd_of(1)
            evacuate("n1_turned", "n1_out")
            act.wait_ge(S("m_diff"), 1)
            act.activation(w1, w2, ACT.Exp).then_inc(S("e2"), 1)
            for i in range(2 * NF):
                act.wait_ge(S("gate_up"), 2 * i + 1)
                if i >= 2:
                    act.wait_ge(S("gu_done"), i - 1)
                act.activation(sg[:, i % 2, :], bank(3 * (i % 2)), ACT.Silu).then_inc(S("silu_done"), 1)
            rstd_of(2)
            evacuate("n2_turned", "n2_out")
            for k in range(2):
                act.wait_ge(S("q_rotated"), k + 1)
                for j in range(2):
                    act.activation(qm[:, k, j, :], qr[:, k, :], ACT.Copy, scale=hm1[:, j:j + 1])\
                       .then_inc(S("q_masked"), 1)

            def low_part(n):
                act.wait_ge(S(f"mx_turned{n}"), 1)
                act.activation(mTb[0:64, :], psum[0:64, 0:2, :].rearrange("p a b -> p (a b)"), ACT.Copy)\
                   .then_inc(S(f"m_hi{n}"), 1)

            low_part(1)
            for i in range(2 * 8 * B):
                g, kt = i // 2, i % 2
                act.wait_ge(S("lt1"), i + 1)
                if g >= 2:
                    act.wait_ge(S("o_sum1"), g - 1)
                act.activation(Pb[2 * (g % 2) + kt], bank(2 * (i % 2), 2), ACT.Exp, scale=float(D1) ** -0.5)\
                   .then_inc(S("prob1"), 1)
            evacuate("attn_turned", "attnT_out")
            rstd_of(3)
            evacuate("n3_turned", "n3_out")
            act.wait_ge(S("gdiff"), 1)
            act.activation(gt[:, :, :], gt[:, :, :], ACT.Exp).then_inc(S("gexp"), 1)
            for k in range(2):
                act.wait_ge(S("q2_proj"), k + 1)
                for j in range(2):
                    act.activation(qm2[:, k, j, :], bank(2 * k, 2), ACT.Copy, scale=hm2[:, j:j + 1])\
                       .then_inc(S("q2_masked"), 1)
            act.wait_ge(S("ks_turned"), 1)
            act.activation(ksT, bank(6, 2), ACT.Copy).then_inc(S("ks_out"), 1)
            low_part(2)
            for i in range(2 * 4 * B):
                g, kt = i // 2, i % 2
                n = 256 - P * kt
                act.wait_ge(S("lt2"), i + 1)
                if g >= 2:
                    act.wait_ge(S("o_sum2"), g - 1)
                act.activation(Pb[2 * (g % 2) + kt][:, 0:4 * n].rearrange("p (a b) -> p a b", a=2),
                               psum[:, 2 * (i % 2):2 * (i % 2) + 2, 0:2 * n], ACT.Exp, scale=float(D2) ** -0.5)\
                   .then_inc(S("prob2"), 1)

        @block.gpsimd
        def _(pool):
            pool.memset(vaug[:, :, :, :], 1.0).then_inc(S("vaug_ones"), 1)
            for i in range(2 * NS):
                k = i // NS
                if i % NS == 0:
                    pool.wait_ge(S("w_ready"), k + 1)
                pool.wait_ge(S("b_copied"), i + 1)
                if i >= 2:
                    pool.wait_ge(S("scanned"), i - 1)
                pool.tensor_tensor(dBu[:, i % 2, :], w[:, k, :], Bsb[i % 2], ALU.mult).then_inc(S("dBu_ready"), 1)
            pool.wait_ge(S("k_out"), 4)
            pool.wait_ge(S("cs_out"), 2)
            for k in range(2):
                pool.tensor_tensor(k1T[:, k, :], k1T[:, k, :], cosT[:, :], ALU.mult).then_inc(S("k_rot"), 1)
                pool.tensor_tensor(k2T[:, k, :], k2T[:, k, :], sinT[:, :], ALU.mult).then_inc(S("k_rot"), 1)
            pool.wait_ge(S("k_rot"), 4)
            for k in range(2):
                m = pool.tensor_tensor(k1T[:, k, :], k1T[:, k, :], k2T[:, k, :], ALU.add)
                if k == 0:
                    m.then_inc(S("k_rot"), 1)
                else:
                    pool.wait_ge(S("k_rot"), 5)
                    m.then_inc(S("k_rotated"), 1)

        @block.vector
        def _(v):
            chain = [0]

            def link(ins):
                chain[0] += 1
                ins.then_inc(S("dve_chain"), 1)
                v.wait_ge(S("dve_chain"), chain[0])

            def norm_stats(n, tiles=range(T), ready=None):
                for t in range(T):
                    if ready:
                        v.wait_ge(S(ready), t // 2 + 1)
                    last = v.bn_stats(stats[:, t, :], x[:, t, :])
                link(last)
                for t in range(T):
                    last = v.bn_aggr(mv[:, t, :], stats[:, t, :])
                last.then_inc(S("mv"), 1)

            def norm_apply(n, name):
                v.wait_ge(S("rstd"), n + 1)
                for t in range(T):
                    v.tensor_scalar(xn[:, t, :], x[:, t, :], mv[:, t, 0:1], rstd[:, t:t + 1],
                                    ALU.subtract, ALU.mult).then_inc(S(name), 1)

            def evacuate(turned, done):
                v.wait_ge(S(turned), 4)
                v.tensor_copy(xnT[:, 1, 0:512], bank(2)).then_inc(S(done), 1)
                v.wait_ge(S(turned), 8)
                v.tensor_copy(xnT[:, 1, 512:1024], bank(3)).then_inc(S(done), 1)

            v.memset(xp[:, :, :, 0:3], 0.0).then_inc(S("xin_zero"), 1)
            v.wait_ge(S("ld_pos"), 16)
            a4 = ang.rearrange("p t (s a i) -> p t s a i", s=2, a=2)
            for s in range(2):
                for i in range(2):
                    last = v.tensor_scalar(a4[:, :, s, :, i], pos, 10000.0 ** (-i / 2), None, ALU.mult)
            link(last)
            for s in range(2):
                c8 = slice(4 * s, 4 * s + 4)
                last = v.tensor_scalar(rnd[:, :, c8], ang[:, :, c8], 1.0 / 6.283185307179586,
                                       0.25 if s == 0 else 0.0, ALU.mult, ALU.add)
            link(last)
            link(v.tensor_scalar(rnd, rnd, ROUND, None, ALU.add))
            link(v.tensor_scalar(rnd, rnd, ROUND, None, ALU.subtract))
            link(v.scalar_tensor_tensor(ang, rnd, -TWO_PI_HI, ang, ALU.mult, ALU.add))
            link(v.scalar_tensor_tensor(ang, rnd, -TWO_PI_LO, ang, ALU.mult, ALU.add))
            link(v.tensor_scalar(ang[:, :, 0:4], ang[:, :, 0:4], 1.5707963267948966, None, ALU.add))
            v.tensor_scalar(ang, ang, PI_IN, -PI_IN, ALU.min, ALU.max).then_inc(S("ang_ready"), 1)
            v.wait_ge(S("ld_x"), 16)
            norm_stats(0)
            v.wait_ge(S("ld_small"), 16 * 14)
            for k in range(2):
                v.wait_ge(S("xin_copied"), k + 1)
                cv = conv[:, k, :].rearrange("p (b l) -> p b l", b=B)
                link(v.tensor_scalar(cv, xp[:, k, :, 0:L], convw[:, k, 0:1], None, ALU.mult))
                for j in range(1, KCONV):
                    m = v.scalar_tensor_tensor(cv, xp[:, k, :, j:j + L], convw[:, k, j:j + 1], cv,
                                               ALU.mult, ALU.add)
                    if j < KCONV - 1:
                        link(m)
                m.then_inc(S("conv_done"), 1)
                if k == 0:
                    norm_apply(0, "xn0")
            v.wait_ge(S("expA"), 1)
            v.tensor_scalar(negA, negA, -1.0, None, ALU.mult).then_inc(S("negA"), 1)
            v.wait_ge(S("hi_ready"), 1)
            xd = psum[0:96, 0:2, :].rearrange("p a b -> p (a b)")
            rest = mid3[0:96, :]
            v.tensor_tensor(rest, xd, hib, ALU.subtract).then_inc(S("split_read"), 1)
            v.wait_ge(S("split_read"), 1)
            link(v.tensor_copy(midb, rest))
            link(v.tensor_tensor(rest, rest, midb, ALU.subtract))
            link(v.tensor_copy(lob, rest))
            v.tensor_copy(dsplit[0:32, :], hib[0:32, :])
            v.tensor_copy(dsplit[32:64, :], midb[32:64, :])
            v.tensor_copy(dsplit[64:96, :], lob[64:96, :]).then_inc(S("split_done"), 1)
            for k in range(2):
                v.wait_ge(S("ln_ready"), k + 1)
                e, s = expx[:, k, :], absx[:, k, :]
                link(v.tensor_scalar(s, e, 0.2, -0.25, ALU.mult, ALU.add))
                link(v.tensor_tensor(s, s, e, ALU.mult))
                link(v.scalar_tensor_tensor(s, s, 1.0 / 3.0, e, ALU.add, ALU.mult))
                link(v.scalar_tensor_tensor(s, s, -0.5, e, ALU.add, ALU.mult))
                link(v.scalar_tensor_tensor(s, s, 1.0, e, ALU.add, ALU.mult))
                small = xn[:, 0:4, :].rearrange("p a b -> p (a b)").bitcast(I32)
                if k == 0:
                    v.wait_ge(S("z_out"), 2)
                link(v.tensor_scalar(small, e, SMALL, None, ALU.is_lt))
                link(v.copy_predicated(w[:, k, :], small, s))
                link(v.tensor_tensor(dt[:, k, :], dt[:, k, :], w[:, k, :], ALU.add))
                v.tensor_tensor(w[:, k, :], dt[:, k, :], u[:, k, :], ALU.mult).then_inc(S("w_ready"), 1)
            for i in range(2):
                last = v.memset(dA[i].rearrange("p (b l) -> p b l", b=B)[:, :, 0:1], 0.0)
            last.then_inc(S("dA_zero"), 1)
            v.wait_ge(S("k_out"), 4)

            def take_y(k):
                v.wait_ge(S("y_sum"), NS * (k + 1))
                v.scalar_tensor_tensor(yT[:, k, :], u[:, k, :], Dp[:, k:k + 1], bank(6, 2),
                                       ALU.mult, ALU.add).then_inc(S("y_taken"), 1)
                v.wait_ge(S("y_taken"), k + 1)
                v.tensor_tensor(yT[:, k, :], yT[:, k, :], zg[:, k, :], ALU.mult).then_inc(S("y_gated"), 1)

            for i in range(2 * NS):
                v.wait_ge(S("dA_ready"), i + 1)
                v.wait_ge(S("dBu_ready"), i + 1)
                v.tensor_tensor_scan(hst[:, i % 2, :], dA[i % 2], dBu[:, i % 2, :], 0.0, ALU.mult, ALU.add)\
                 .then_inc(S("scanned"), 1)
                if i == NS:
                    take_y(0)
                v.wait_ge(S("scanned"), i + 1)
                v.wait_ge(S("c_spread"), i + 1)
                if i >= 2:
                    v.wait_ge(S("y_sum"), i - 1)
                v.tensor_tensor(prod[:, i % 2, :], hst[:, i % 2, :], bank(4, 2), ALU.mult)\
                 .then_inc(S("prod_ready"), 1)
            take_y(1)
            v.wait_ge(S("tg"), 1)

            def residual(n, turned, banks, gate, name, t0=0):
                for c in range(n):
                    v.wait_ge(S(turned), t0 // 2 + c + 1)
                    xs = x[:, t0 + 2 * c:t0 + 2 * c + 2, :].rearrange("p a b -> p (a b)")
                    v.scalar_tensor_tensor(xs, bank(banks + c), tg[:, gate:gate + 1], xs, ALU.mult, ALU.add)\
                     .then_inc(S(name), 1)

            residual(4, "y_turned", 0, 0, "x1")
            norm_stats(1, ready="x1")
            norm_apply(1, "xn1")
            evacuate("n1_turned", "n1_out")
            v.wait_ge(S("router"), 1)
            v.tensor_copy(rl, psum[:, 4, 0:T * E].rearrange("p (t e) -> p t e", t=T)).then_inc(S("router_read"), 1)
            v.wait_ge(S("router_read"), 1)

            def bc(a, n):
                return a.unsqueeze(2).to_broadcast([P, T, n])

            def first_best(val, m, ind, work, best, rank, n):
                link(v.tensor_reduce(m, val, AX.X, ALU.max))
                link(v.tensor_tensor(work, val, bc(m, n), ALU.is_equal))
                link(v.tensor_tensor(work, work, rank.unsqueeze(1).to_broadcast([P, T, n]), ALU.mult))
                link(v.tensor_reduce(best, work, AX.X, ALU.max))
                link(v.tensor_tensor(ind, work, bc(best, n), ALU.is_equal))

            first_best(rl, m1, i1, tmp8, mi, rank8[:, :], E)
            link(v.scalar_tensor_tensor(rl, i1, -1e30, rl, ALU.mult, ALU.add))
            first_best(rl, m2, i2, tmp8, mi, rank8[:, :], E)
            v.tensor_tensor(w2, m2, m1, ALU.subtract).then_inc(S("m_diff"), 1)
            v.wait_ge(S("e2"), 1)
            link(v.tensor_scalar(w2, w1, 1.0, None, ALU.add))
            link(v.reciprocal(m1, w2))
            link(v.tensor_tensor(m2, m1, w1, ALU.mult))
            link(v.tensor_tensor(i1, i1, bc(m1, E), ALU.mult))
            link(v.tensor_tensor(i2, i2, bc(m2, E), ALU.mult))
            v.tensor_tensor(tw, i1, i2, ALU.add).then_inc(S("tw_ready"), 1)
            v.wait_ge(S("tw_turned"), 1)
            v.tensor_copy(twT, psum[0:E, 6:8, :].rearrange("p a b -> p (a b)")).then_inc(S("twT_ready"), 1)
            for i in range(2 * NF):
                f = i % NF
                v.wait_ge(S("silu_done"), i + 1)
                v.wait_ge(S("gate_up"), 2 * i + 2)
                v.tensor_tensor(h1[:, i % 2, :], sg[:, i % 2, :], bank(3 * (i % 2) + 1), ALU.mult)\
                 .then_inc(S("gu_done"), 1)
                v.wait_ge(S("gu_done"), i + 1)
                v.wait_ge(S("tw_spread"), i + 1)
                if i == NF:
                    v.wait_ge(S("down"), 2)
                v.tensor_tensor(hid[:, f, :], h1[:, i % 2, :], bank(3 * (i % 2) + 2), ALU.mult)\
                 .then_inc(S("hid_ready"), 1)
                if i == NF:
                    residual(2, "down", 6, 2, "x2", 0)
            residual(2, "down", 6, 2, "x2", 4)
            norm_stats(2, ready="x2")
            norm_apply(2, "xn2")
            evacuate("n2_turned", "n2_out")
            for k in range(2):
                v.wait_ge(S("q_proj"), k + 1)
                v.tensor_tensor(qr[:, k, :], bank(2 * k, 2), cosT[:, :], ALU.mult)
                v.wait_ge(S("q_proj"), k + 3)
                tmp = attn[:, 4 * k:4 * k + 4, :].rearrange("p a b -> p (a b)")
                link(v.tensor_tensor(tmp, bank(4 + 2 * k, 2), sinT[:, :], ALU.mult))
                v.tensor_tensor(qr[:, k, :], qr[:, k, :], tmp, ALU.add).then_inc(S("q_rotated"), 1)
                v.wait_ge(S("q_rotated"), k + 1)
                for j in range(2, 4):
                    v.tensor_scalar(qm[:, k, j, :], qr[:, k, :], hm1[:, j:j + 1], None, ALU.mult)\
                     .then_inc(S("q_masked"), 1)
            for g in range(T * 8):
                t = g // 8
                v.wait_ge(S("logit1"), g + 1)
                v.tensor_reduce(mx[:, t, 4 * (g % 8):4 * (g % 8) + 4],
                                bank(2 * (g % 4), 2).rearrange("p (j k) -> p j k", j=4), AX.X, ALU.max)\
                 .then_inc(S("max1"), 1)
            v.wait_ge(S("max1"), T * 8)

            def split_maxima(n):
                v.tensor_copy(mx[:, :, 32:64], mx[:, :, 0:32]).then_inc(S(f"mx_dup{n}"), 1)
                v.wait_ge(S(f"m_hi{n}"), 1)
                link(v.tensor_tensor(mlow[32:64, :], psum[32:64, 0:2, :].rearrange("p a b -> p (a b)"),
                                     mTb[32:64, :], ALU.subtract))
                v.tensor_copy(mTb[32:64, :], mlow[32:64, :]).then_inc(S(f"m_split{n}"), 1)

            split_maxima(1)

            def heads_out(tag, per, finish):
                for g in range(B * per):
                    v.wait_ge(S("o_sum" + tag), g + 1)
                    if g >= per and g % per == 0:
                        v.wait_ge(S("o_turned" + tag), 2 * (g // per))
                    v.tensor_copy(osb[:, g % per, :], psum[:, 4 + g % 2, 0:256]).then_inc(S("o_copied" + tag), 1)
                    if g % per == per - 1:
                        for qt in range(2):
                            finish(2 * (g // per) + qt)

            def finish1(t):
                v.wait_ge(S("o_turned1"), t + 1)
                o = bank(6, 2).rearrange("p (h e) -> p h e", e=32)
                link(v.reciprocal(rec[:, t, :], o[:, :, D1]))
                v.tensor_tensor(attn[:, t, :].rearrange("p (h e) -> p h e", e=D1), o[:, :, 0:D1],
                                rec[:, t, :].unsqueeze(2).to_broadcast([P, H1, D1]), ALU.mult)\
                 .then_inc(S("o_norm1"), 1)

            heads_out("1", 8, finish1)
            evacuate("attn_turned", "attnT_out")
            residual(4, "proj1", 4, 1, "x3")
            norm_stats(3, ready="x3")
            norm_apply(3, "xn3")
            evacuate("n3_turned", "n3_out")
            v.wait_ge(S("gate_logit"), 1)
            link(v.tensor_copy(gl[:, :, 0:H2], psum[:, 4, 0:T * H2].rearrange("p (t e) -> p t e", t=T)))
            first_best(gl[:, :, 0:H2], gm[:, :], gi[:, :, :], gt[:, :, :], gs[:, :], rank16[:, :], H2)
            v.tensor_tensor(gt[:, :, :], gl[:, :, 0:H2], bc(gm[:, :], H2), ALU.subtract).then_inc(S("gdiff"), 1)
            v.wait_ge(S("gexp"), 1)
            link(v.tensor_reduce(gs[:, :], gt[:, :, :], AX.X, ALU.add))
            link(v.reciprocal(gm[:, :], gs[:, :]))
            for t in range(T):
                v.wait_ge(S("kv_proj"), t + 1)
                g4 = kvp[:, t % 2, :].rearrange("p (s h e) -> p s h e", s=2, h=H2)
                for s in range(2):
                    m = v.tensor_tensor(g4[:, s], bank(5 + t % 2)[:, 256 * s:256 * s + 256].rearrange("p (h e) -> p h e", h=H2),
                                        gi[:, t, :].unsqueeze(2).to_broadcast([P, H2, D2]), ALU.mult)
                m.then_inc(S("kv_read"), 1)
                v.wait_ge(S("kv_read"), t + 1)
                for s in range(2):
                    m = v.tensor_reduce(ksv[:, t, s, :], g4[:, s].rearrange("p h e -> p e h"), AX.X, ALU.add)
                link(m)
                v.tensor_scalar(va2[:, t, 0:D2], ksv[:, t, 1, :], gm[:, t:t + 1], None, ALU.mult)
                v.memset(va2[:, t, D2:32], 1.0)
                last = v.tensor_copy(krep[:, t, :].rearrange("p (r e) -> p r e", r=8),
                                     ksv[:, t, 0, :].unsqueeze(1).to_broadcast([P, 8, D2]))
            last.then_inc(S("krep_ready"), 1)
            v.memset(mx[:, :, 16:32], 0.0)
            for g in range(2 * T):
                t, half = g // 2, g % 2
                n = P * (t % 2 + 1)
                v.wait_ge(S("logit2"), g + 1)
                src = psum[:, 4 * (g % 2):4 * (g % 2) + 4, 0:2 * n].rearrange("p a (j k) -> p a j k", j=2)
                v.tensor_reduce(mx[:, t, 8 * half:8 * half + 8].rearrange("p (a j) -> p a j", a=4), src, AX.X, ALU.max).then_inc(S("max2"), 1)
            v.wait_ge(S("max2"), 2 * T)
            split_maxima(2)

            def finish2(t):
                v.wait_ge(S("o_turned2"), t + 1)
                o = bank(6).rearrange("p (h e) -> p h e", e=32)
                link(v.reciprocal(rec[:, t, 0:H2], o[:, :, D2]))
                f = fin[:, t % 2, :]
                v.tensor_tensor(f.rearrange("p (h e) -> p h e", e=D2), o[:, :, 0:D2],
                                rec[:, t, 0:H2].unsqueeze(2).to_broadcast([P, H2, D2]), ALU.mult)\
                 .then_inc(S("o_norm2"), 1)
                v.wait_ge(S("o_norm2"), t + 1)
                m = v.scalar_tensor_tensor(x[:, t, :], f, tg[:, 3:4], x[:, t, :], ALU.mult, ALU.add)
                if t % 2:
                    m.then_inc(S("fin_ready"), 1)

            heads_out("2", 4, finish2)


def kernel(**inputs):
    import ml_dtypes
    import numpy as np
    import concourse.bacc as bacc
    from concourse.bass_utils import run_bass_kernel_spmd as run

    bf = ml_dtypes.bfloat16
    g = {k: np.ascontiguousarray(v) for k, v in inputs.items()}
    a = {}

    def rows(w_t, k=2):
        return w_t.reshape(k, P, -1).transpose(1, 0, 2)

    a["x"] = g["x"]
    a["ctxT"] = g["ctx_1024"].reshape(NT, CTX).T
    a["win"] = g["L0_xattn_in_proj_w"].T
    a["pos"] = g["fside_BxSx2_0"].reshape(T, P, 2).transpose(1, 0, 2)
    a["convw"] = rows(g["L0_xattn_conv_w"].reshape(C, KCONV))
    a["convb"] = g["L0_xattn_conv_b"].reshape(2, P).T
    order = list(range(RANK, RANK + 2 * NS))
    a["xproj"] = rows(g["L0_xattn_x_proj_w"][order * 3 + list(range(RANK))].T)
    a["dtw"] = g["L0_xattn_dt_proj_w"].T
    a["dtb"] = g["L0_xattn_dt_proj_b"].reshape(2, P).T
    a["alog"] = rows(g["L0_xattn_A_log"])
    a["dp"] = g["L0_xattn_D"].reshape(2, P).T
    gates = np.stack([g["g_xattn"][0], g["g_xattn"][1], g["g_ffn"][0], g["g_ffn"][1]])
    a["gates"] = np.broadcast_to(gates, (P, 4))
    swap = np.arange(C).reshape(-1, 2)[:, ::-1].reshape(-1)
    wkv = g["L1_xattn_Wkv"]
    a["wk1"] = wkv[:, :C]
    a["wk2"] = wkv[:, :C][:, swap]
    a["wv"] = wkv[:, C:]
    a["wq1"] = rows(g["L1_xattn_Wq"])
    a["wq2"] = rows(g["L1_xattn_Wq"][:, swap])
    a["wout"] = rows(g["L1_xattn_Wout"])
    a["bout"] = g["L1_xattn_bout"].reshape(1, C)
    a["wqkv"] = rows(g["L1_ffn_W_qkv"].T)
    a["wg16"] = rows(g["L1_ffn_W_gate"].T)
    a["wg8"] = rows(g["L0_ffn_gate_w"].T)
    a["gateT"] = rows(g["L0_ffn_gate_proj"].reshape(E * FD, C).T)
    a["upT"] = rows(g["L0_ffn_up_proj"].reshape(E * FD, C).T)
    a["downT"] = g["L0_ffn_down_proj"].transpose(0, 2, 1).reshape(NF, P, C).transpose(1, 0, 2)
    p = np.arange(P)
    a["ident"] = np.eye(P, dtype=np.float32)
    a["identb"] = np.eye(P, dtype=bf)
    sel = np.zeros((96, 2 * NS, P), bf)
    negsel = np.zeros((64, H1, P), bf)
    for n in range(32):
        sel[[n, 32 + n, 64 + n], n] = 1
        negsel[[n, 32 + n], n] = -1
    a["sel"], a["negsel"] = sel, negsel
    a["hm1"] = (p[:, None] // D1 % 4 == np.arange(4)).astype(np.float32)
    a["hm2"] = (p[:, None] // D2 % 2 == np.arange(2)).astype(np.float32)
    ex = np.zeros((E, NF, P), np.float32)
    for f in range(NF):
        ex[(f * P + p) // FD, f, p] = 1
    a["ex8"] = ex
    ecs = np.zeros((8, 2, P), np.float32)
    pair = p % D1 // 4 * 2 + p % 4 // 2
    ecs[pair, 0, p] = 1
    ecs[4 + pair, 1, p] = np.where(p % 2, 1, -1)
    a["ecs"] = ecs
    mA = np.zeros((P, 2, 256), bf)
    mB = np.zeros((P, 2, 256), bf)
    mA[:, :, 128:] = np.where(p[None, :] > p[:, None], -1e30, 0)[:, None, :]
    mB[:, :, :128] = np.where(p[:, None] > p[None, :], -1e30, 0)[:, None, :]
    a["maskA"], a["maskB"] = mA, mB
    a["rank8"] = np.broadcast_to(np.arange(E, 0, -1, dtype=np.float32), (P, E))
    a["rank16"] = np.broadcast_to(np.arange(H2, 0, -1, dtype=np.float32), (P, H2))
    a["onesr"] = np.ones((1, P), np.float32)
    a["consts"] = np.broadcast_to(np.array([EPS, 1, 0, 0], np.float32), (P, 4))

    nc = bacc.Bacc("TRN2", target_bir_lowering=False, num_devices=1)
    arrays, d = {}, {}
    for name, v in a.items():
        v = np.ascontiguousarray(v)
        arrays["in_" + name] = v
        d[name] = nc.dram_tensor("in_" + name, v.shape, mybir.dt.from_np(v.dtype), kind="ExternalInput").ap()
    out = nc.dram_tensor("out_y", (B, L, C), F32, kind="ExternalOutput").ap()
    flamingo_program(nc, d, out)
    r = run(nc, [arrays], core_ids=[0])
    return r.results[0]["out_y"]
```

```python
from contextlib import ExitStack

import concourse.bass as bass
from concourse import mybir

F32 = mybir.dt.float32
BF16 = mybir.dt.bfloat16
I32 = mybir.dt.int32
ALU = mybir.AluOpType
ACT = mybir.ActivationFunctionType
AX = mybir.AxisListType

P = 128
B, L, C = 4, 256, 256
T = B * L // P
NT = B * L
CTX = 128
NS, RANK, KCONV = 16, 8, 4
E, FD = 8, 176
NF = E * FD // P
H1, D1 = 32, 8
H2, D2 = 16, 16
EPS = 1e-5
SMALL = 0.05
TWO_PI_HI = 6.28125
TWO_PI_LO = 2.0 * 3.141592653589793 - 6.28125
ROUND = 12582912.0
PI_IN = 3.1415925
RING = 4
UNITS = 2 * B
LAG = 2


def flamingo_program(nc, d, out):
    ctx = ExitStack()
    with ctx:
        def sb(name, shape, dt=F32):
            return ctx.enter_context(nc.sbuf_tensor(name, shape, dt))

        sems = {}

        def S(name):
            if name not in sems:
                sems[name] = ctx.enter_context(nc.semaphore(name))
            return sems[name]

        x = sb("x", [P, T, C])
        xn = sb("xn", [P, T, C])
        xnT = sb("xnT", [P, 2, NT])
        stats = sb("stats", [P, T, 6])
        mv = sb("mv", [P, T, 2])
        lnv = sb("lnv", [P, T])
        rstd = sb("rstd", [P, T])
        gates = sb("gates", [P, 4])
        tg = sb("tg", [P, 4])
        consts = sb("consts", [P, 4])
        ident = sb("ident", [P, P])
        identb = sb("identb", [P, P], BF16)
        maskA = sb("maskA", [P, 2, 256], BF16)
        maskB = sb("maskB", [P, 2, 256], BF16)
        rank8 = sb("rank8", [P, E])
        rank16 = sb("rank16", [P, H2])
        onesr = sb("onesr", [1, P])
        wq1 = sb("wq1", [P, 2, C])
        wq2 = sb("wq2", [P, 2, C])
        wout = sb("wout", [P, 2, C])
        bout = sb("bout", [1, C])
        wqkv = sb("wqkv", [P, 2, 3 * C])
        wg16 = sb("wg16", [P, 2, H2])
        wg8 = sb("wg8", [P, 2, E])
        ex8 = sb("ex8", [96, NF, P], BF16)
        tw3 = sb("tw3", [P, T, 96])
        twT = sb("twT", [96, NT], BF16)
        k1T = sb("k1T", [P, 2, NT])
        k2T = sb("k2T", [P, 2, NT])
        vaug = sb("vaug", [P, T, H1, 32])
        cosT = sb("cosT", [P, NT])
        sinT = sb("sinT", [P, NT])
        area = sb("area", [P, 21520])
        used = [0]

        def part(shape, dt=F32, rows=P):
            n = 1
            for s in shape:
                n *= s
            w = n if dt != BF16 else n // 2
            a = area[0:rows, used[0]:used[0] + w]
            used[0] += w
            if dt != F32:
                a = a.bitcast(dt)
            if len(shape) == 2:
                a = a.rearrange("p (a b) -> p a b", a=shape[0])
            elif len(shape) == 3:
                a = a.rearrange("p (a b c) -> p a b c", a=shape[0], b=shape[1])
            return a

        wk1 = part([C]); wk2 = part([C]); wv = part([C]); win = part([C])
        ctxT = part([NT])
        xproj = part([2, 104]); dtw = part([C]); convw = part([2, KCONV]); convb = part([2])
        dtb = part([2]); negA = part([2, NS]); Dp = part([2])
        pos = part([T, 2]); ang = part([T, 8]); rnd = part([T, 8]); trig = part([T, 8])
        ecs = part([2, P], rows=8); csT = part([NT], rows=8)
        sel = part([2 * NS, P], BF16, rows=96)
        dsplit = part([NT], BF16, rows=96)
        zg = part([2, NT]); u = part([2, NT]); dt = part([2, NT]); w = part([2, NT])
        scan0 = used[0]
        xin = part([2, B * (L + 3)]); mid3 = part([NT], rows=P); conv = part([2, NT])
        midb = part([NT], BF16, rows=96); lob = part([NT], BF16, rows=96); hib = part([NT], BF16, rows=96)
        end0 = used[0]
        xp = xin.rearrange("p a (b l) -> p a b l", b=B)
        spare = sb("parts", [P, 3, 2, NT], BF16)
        parts = spare
        second = spare[:, :, :, :].rearrange("p c k t -> p c (k t)").bitcast(F32)
        absx = [xin[:, 0, 0:NT], second[:, 0, :]]
        expx = [conv[:, 0, :], second[:, 1, :]]
        used[0] = scan0
        dA = [part([NT]) for _ in range(2)]
        end0 = max(end0, used[0])
        used[0] = scan0
        dA = [part([NT]) for _ in range(2)]
        Bsb = [area[:, 0:NT], area[:, NT:2 * NT]]
        dBu = part([2, NT]); hst = part([2, NT])
        prod = xn[:, :, :].rearrange("p (a t) c -> p a (t c)", a=2)
        assert max(end0, used[0]) <= 21520, (end0, used[0])
        yT = xnT
        used[0] = 0
        gateT = part([2, E * FD]); upT = part([2, E * FD]); downT = part([NF, C])
        hid = part([NF, 512])
        sg = part([2, 512]); h1 = part([2, 512])
        rl = part([T, E]); i1 = part([T, E]); i2 = part([T, E]); tmp8 = part([T, E]); tw = part([T, E])
        m1 = part([T]); m2 = part([T]); mi = part([T]); w1 = part([T]); w2 = part([T]); twb = part([T, E], BF16)
        assert used[0] <= 21520, used[0]
        used[0] = 0
        Pb = [part([4 * 256]) for _ in range(4)]
        both = used[0]
        qs = [part([16, 256], BF16, rows=75) for _ in range(RING)]
        ks = [part([16, 256], BF16, rows=75) for _ in range(RING)]
        assert used[0] <= 21520, used[0]
        used[0] = both
        qs2 = [part([H2, 256], BF16) for _ in range(B)]
        qx2 = [part([H2, 256], BF16, rows=19) for _ in range(B)]
        ks2 = part([NT], BF16); kx2 = part([NT], BF16, rows=19)
        assert used[0] <= 21520, used[0]
        mx = sb("mx", [P, 2, 2, 16])
        mb = sb("mb", [P, 2, 16], BF16)
        mr = sb("mr", [P, 2, 16])
        m3 = sb("m3", [P, 2, 2, 48])
        mrow = sb("mrow", [48, 2, 256], BF16)
        rec = sb("rec", [P, T, 16])
        kt = xn[:, :, :].rearrange("p t c -> p (t c)")[:, 0:T * 147].rearrange("p (t r) -> p t r", t=T)
        kb = sb("kb", [P, T, D2], BF16)
        qr, tmpq, osb, attn = k1T, k2T, k2T, xn
        kd = nc.dram_tensor("kd", (3, C, NT), BF16, kind="Internal").ap()
        qd = nc.dram_tensor("qd", (3, C, NT), BF16, kind="Internal").ap()
        q2d = nc.dram_tensor("q2d", (3, C, NT), BF16, kind="Internal").ap()
        gl = sb("gl", [P, T, H2])
        va2 = vaug[:, :, 0, :]
        gi = sb("gi", [P, T, H2]); gm = sb("gm", [P, T]); gt = sb("gt", [P, T, H2]); gs = sb("gs", [P, T])
        kvp = k2T[:, 0, :].rearrange("p (a b) -> p a b", a=2)
        ksv = sb("ksv", [P, T, 2, D2])
        fin = sinT[:, 0:2 * C].rearrange("p (a b) -> p a b", a=2)

        psum = ctx.enter_context(nc.psum_tensor("psum", [P, 8, 512], F32))

        def bank(i, n=1):
            return psum[:, i:i + n, :].rearrange("p a b -> p (a b)")

        dqs = []

        block = ctx.enter_context(nc.Block())
        xt = d["x"].rearrange("b (t p) c -> p (b t) c", p=P)
        ot = out.rearrange("b (t p) c -> p (b t) c", p=P)

        @block.sync
        def _(sp):
            def load(dst, name, s):
                sp.dma_start(dst, d[name]).then_inc(S(s), 16)

            load(ctxT, "ctxT", "ld_in")
            load(win, "win", "ld_in")
            sp.dma_start(x[:, :, :], xt).then_inc(S("ld_x"), 16)
            load(pos, "pos", "ld_pos")
            for dst, name in ((convw, "convw"), (convb, "convb"), (xproj, "xproj"), (dtb, "dtb"),
                              (negA, "alog"), (Dp, "dp"), (gates[:, :], "gates"), (ident[:, :], "ident"), (ecs, "ecs"),
                              (sel, "sel"), (consts[:, :], "consts")):
                load(dst, name, "ld_small")
            sp.dma_start(dtw[96:104, :], d["dtw"]).then_inc(S("ld_small"), 16)
            for dst, name in ((wv, "wv"), (wk1, "wk1"), (wk2, "wk2")):
                load(dst, name, "ld_kv")
            for dst, name in ((identb[:, :], "identb"), (maskA[:, :, :], "maskA"),
                              (maskB[:, :, :], "maskB"), (rank8[:, :], "rank8"), (rank16[:, :], "rank16"),
                              (wq1[:, :, :], "wq1"), (wq2[:, :, :], "wq2"), (wout[:, :, :], "wout"),
                              (bout[:, :], "bout"), (wqkv[:, :, :], "wqkv"), (wg16[:, :, :], "wg16"),
                              (wg8[:, :, :], "wg8"), (ex8[:, :, :], "ex8"), (onesr[:, :], "onesr")):
                load(dst, name, "ld_late")
            sp.wait_ge(S("y_gated"), 2)
            for dst, name in ((gateT, "gateT"), (upT, "upT")):
                load(dst, name, "ld_moe")
            load(downT, "downT", "ld_down")

            def store(src, dst, c, k):
                return sp.dma_start(dst[c, P * k:P * k + P, :], src)

            def stack(dst, src, a, c, part, k, b, n):
                r = n * (3 * a + c)
                return sp.dma_start(dst[r:r + n, :, :],
                                    src[part].rearrange("(h e) t -> e h t", e=n)[:, k:k + 16, L * b:L * b + L])

            sp.wait_ge(S("k_parts"), 6)
            for c in range(3):
                for k in range(2):
                    store(parts[:, c, k, :], kd, c, k).then_inc(S("k_stored"), 16)
            sp.wait_ge(S("k_stored"), 96)
            sp.wait_ge(S("x2"), 4)
            for n in range(RING):
                sp.dma_start(ks[n][72:75, :, :], d["ones3"]).then_inc(S(f"k_slot{n}"), 16)

            def load_k(u):
                for a in range(3):
                    for c in range(3):
                        stack(ks[u % RING], kd, a, c, c, 16 * (u // B), u % B, D1).then_inc(S(f"k_slot{u % RING}"), 16)

            def load_q(u):
                for a in range(3):
                    for c in range(3):
                        stack(qs[u % RING], qd, a, c, a, 16 * (u // B), u % B, D1).then_inc(S(f"q_slot{u % RING}"), 16)

            for u in range(RING):
                load_k(u)
            for k in range(2):
                for c in range(3):
                    if c < 2:
                        sp.wait_ge(S("q_high"), 2 * k + c + 1)
                    else:
                        sp.wait_ge(S("q_low"), k + 1)
                    store(parts[:, c, k, :], qd, c, k).then_inc(S("q_stored"), 16)
                sp.wait_ge(S("q_stored"), 48 * (k + 1))
                if k == 0:
                    for u in range(RING):
                        load_q(u)
            for u in range(UNITS):
                if u >= LAG and u + LAG < UNITS:
                    sp.wait_ge(S("lt1"), 8 * (u - LAG + 1))
                    sp.wait_ge(S("logit1"), 16 * (u - LAG + 1))
                    load_k(u + LAG)
                    load_q(u + LAG)
                sp.wait_ge(S("m_copied1"), u + 1)
                for c in range(3):
                    sp.dma_start(qs[u % RING][72 + c:73 + c, :, :], mrow[16 * c:16 * c + 16, u % 2, :])\
                      .then_inc(S(f"m_slot{u % RING}"), 16)
            for k in range(2):
                for c in range(3):
                    if c < 2:
                        sp.wait_ge(S("q2_high"), 2 * k + c + 1)
                    else:
                        sp.wait_ge(S("q2_low"), k + 1)
                    store(parts[:, c, k, :], q2d, c, k).then_inc(S("q2_stored"), 16)
            sp.wait_ge(S("q2_stored"), 96)
            sp.wait_ge(S("lt1"), 8 * UNITS)
            for b in range(B):
                for a in range(3):
                    for c in range(3):
                        if a == c == 2:
                            sp.dma_start(qx2[b][0:16, :, :],
                                         q2d[2].rearrange("(h e) t -> e h t", e=D2)[:, :, L * b:L * b + L])\
                              .then_inc(S(f"q2_slot{b}"), 16)
                        else:
                            stack(qs2[b], q2d, a, c, a, 0, b, D2).then_inc(S(f"q2_slot{b}"), 16)
            for b in range(B):
                sp.wait_ge(S("m_copied2"), b + 1)
                for c in range(3):
                    sp.dma_start(qx2[b][16 + c:17 + c, :, :], mrow[16 * c:16 * c + 16, b % 2, :])\
                      .then_inc(S(f"m2_slot{b}"), 16)
            for t in range(T // 2):
                sp.wait_ge(S("fin_ready"), t + 1)
                sp.dma_start(ot[:, 2 * t:2 * t + 2, :], x[:, 2 * t:2 * t + 2, :]).then_inc(S("stored"), 16)
            sp.wait_ge(S("stored"), 16 * (T // 2))

        @block.tensor
        def _(pe):
            def turn_tiles(src_of, at, ready, done):
                for t in range(T):
                    if ready:
                        pe.wait_ge(S(ready), t + 1)
                    for k in range(2):
                        m = pe.transpose(psum[:, at + 2 * k + t // 4, P * (t % 4):P * (t % 4) + P],
                                         src_of(t, k), ident[:, :])
                    m.then_inc(S(done), 1)

            pe.wait_ge(S("ld_in"), 32)
            for k in range(2):
                for c in range(2):
                    m = pe.matmul(bank(2 * k + c), win[:, P * k:P * k + P], ctxT[:, 512 * c:512 * c + 512],
                                  start=True, stop=True)
            m.then_inc(S("inproj"), 1)
            pe.wait_ge(S("ld_small"), 16 * 12)
            pe.wait_ge(S("xin_copied"), 2)
            pe.wait_ge(S("u_ready"), 2)
            for c in range(2):
                for k in range(2):
                    m = pe.matmul(psum[0:104, c, :], xproj[:, k, :], u[:, k, 512 * c:512 * c + 512],
                                  start=(k == 0), stop=(k == 1))
            m.then_inc(S("xdbl"), 1)
            pe.wait_ge(S("dtlow"), 1)
            for k in range(2):
                for c in range(2):
                    m = pe.matmul(bank(4 + 2 * k + c), dtw[96:104, P * k:P * k + P],
                                  mid3[96:104, 512 * c:512 * c + 512], start=True, stop=True)
                m.then_inc(S("dtpre"), 1)
            pe.wait_ge(S("trig_ready"), 1)
            for t in range(T):
                m = pe.transpose(psum[0:8, 2 + t // 4, P * (t % 4):P * (t % 4) + P], trig[:, t, :], ident[:, :])
            m.then_inc(S("cs_turned"), 1)
            pe.wait_ge(S("cs_copied"), 1)
            pe.wait_ge(S("hi_ready"), 1)
            pe.wait_ge(S("split_read"), 1)
            for i in range(2):
                for c in range(2):
                    m = pe.matmul(bank(2 * i + c), ecs[:, i, :], csT[:, 512 * c:512 * c + 512],
                                  start=True, stop=True)
                m.then_inc(S("cs_spread"), 1)
            pe.wait_ge(S("ld_kv"), 48)
            for n, wk in enumerate((wk1, wk2)):
                if n == 0:
                    pe.wait_ge(S("dtpre_read"), 4)
                else:
                    pe.wait_ge(S("cs_out"), 2)
                for k in range(2):
                    for c in range(2):
                        m = pe.matmul(bank(4 - 4 * n + 2 * k + c), wk[:, P * k:P * k + P],
                                      ctxT[:, 512 * c:512 * c + 512], start=True, stop=True)
                m.then_inc(S("k_proj"), 1)
            pe.wait_ge(S("k_out"), 2)
            for t in range(T):
                m = pe.matmul(psum[:, 4 + t // 2, C * (t % 2):C * (t % 2) + C], ctxT[:, P * t:P * t + P], wv[:, :],
                              start=True, stop=True)
            m.then_inc(S("v_proj"), 1)
            units = 2 * NS
            pe.wait_ge(S("split_done"), 1)
            pe.wait_ge(S("k_out"), 4)

            def spread(at, row):
                for c in range(2):
                    m = pe.matmul(bank(at + c), sel[:, row, :], dsplit[:, 512 * c:512 * c + 512],
                                  start=True, stop=True)
                return m

            def add_state(i):
                pe.wait_ge(S("prod_ready"), i + 1)
                if i == NS:
                    pe.wait_ge(S("y_taken"), 1)
                for c in range(2):
                    m = pe.matmul(bank(6 + c), ident[:, :], prod[:, i % 2, 512 * c:512 * c + 512],
                                  start=(i % NS == 0), stop=(i % NS == NS - 1))
                m.then_inc(S("y_sum"), 1)

            def spread_b(i):
                if i >= 2:
                    pe.wait_ge(S("b_copied"), i - 1)
                spread(2 * (i % 2), i % NS).then_inc(S("b_spread"), 1)

            spread_b(0)
            spread_b(1)
            pe.wait_ge(S("v_out"), 4)
            for i in range(units):
                if i >= 1:
                    pe.wait_ge(S("prod_ready"), i)
                spread(4, NS + i % NS).then_inc(S("c_spread"), 1)
                if i + 2 < units:
                    spread_b(i + 2)
                if i >= 1:
                    add_state(i - 1)
            add_state(units - 1)
            pe.wait_ge(S("b_copied"), units)
            pe.wait_ge(S("y_gated"), 2)
            for t in range(T):
                for k in range(2):
                    m = pe.transpose(psum[:, t // 2, C * (t % 2) + P * k:C * (t % 2) + P * k + P],
                                     yT[:, k, P * t:P * t + P], ident[:, :])
                if t % 2:
                    m.then_inc(S("y_turned"), 1)

            pe.wait_ge(S("ld_late"), 16 * 14)
            pe.wait_ge(S("x1"), 4)
            turn_tiles(lambda t, k: xn[:, t, P * k:P * k + P], 0, "xn1", "n1_turned")
            pe.wait_ge(S("n1_out"), 4)
            for t in range(T):
                for k in range(2):
                    m = pe.matmul(psum[:, 4, E * t:E * t + E], xnT[:, k, P * t:P * t + P], wg8[:, k, :],
                                  start=(k == 0), stop=(k == 1))
            m.then_inc(S("router"), 1)
            pe.wait_ge(S("ld_moe"), 32)

            def weights_of(i):
                c = i // NF
                if i == 0:
                    pe.wait_ge(S("tw_ready"), 1)
                    for t in range(T):
                        m = pe.transpose(psum[0:96, 6 + t // 4, P * (t % 4):P * (t % 4) + P], tw3[:, t, :],
                                         ident[:, :])
                    m.then_inc(S("tw_turned"), 1)
                    pe.wait_ge(S("twT_ready"), 1)
                if i >= 2:
                    pe.wait_ge(S("hid_ready"), i - 1)
                pe.matmul(bank(3 * (i % 2) + 2), ex8[:, i % NF, :], twT[:, 512 * c:512 * c + 512],
                          start=True, stop=True).then_inc(S("tw_spread"), 1)

            def down(c):
                pe.wait_ge(S("hid_ready"), NF * (c + 1))
                if c:
                    pe.wait_ge(S("x2"), 2)
                for t in range(4):
                    for f in range(NF):
                        m = pe.matmul(psum[:, 6 + t // 2, C * (t % 2):C * (t % 2) + C],
                                      hid[:, f, P * t:P * t + P], downT[:, f, :],
                                      start=(f == 0), stop=(f == NF - 1))
                    if t % 2:
                        m.then_inc(S("down"), 1)

            for i in range(2 * NF):
                c, f = i // NF, i % NF
                if i == 1:
                    pe.wait_ge(S("router_read"), 1)
                if i >= 2:
                    pe.wait_ge(S("silu_done"), i - 1)
                    pe.wait_ge(S("gu_done"), i - 1)
                for n, wt in enumerate((gateT, upT)):
                    for k in range(2):
                        m = pe.matmul(bank(3 * (i % 2) + n), wt[:, k, P * f:P * f + P],
                                      xnT[:, k, 512 * c:512 * c + 512], start=(k == 0), stop=(k == 1))
                    m.then_inc(S("gate_up"), 1)
                if i >= 1:
                    weights_of(i - 1)
                if i == NF:
                    pe.wait_ge(S("ld_down"), 16)
                    down(0)
            weights_of(2 * NF - 1)
            down(1)

            pe.wait_ge(S("x2"), 4)
            turn_tiles(lambda t, k: xn[:, t, P * k:P * k + P], 0, "xn2", "n2_turned")
            pe.wait_ge(S("n2_out"), 4)
            for n, wt in enumerate((wq1, wq2)):
                for k in range(2):
                    for c in range(2):
                        for kk in range(2):
                            m = pe.matmul(bank(4 * n + 2 * k + c), wt[:, kk, P * k:P * k + P],
                                          xnT[:, kk, 512 * c:512 * c + 512], start=(kk == 0), stop=(kk == 1))
                    m.then_inc(S("q_proj"), 1)
            def attention(tag, units, slots_ready, maxima, probs, values):

                def some_maxima(s, i, jj):
                    n = 16 * s + 2 * i + jj
                    if n >= 2:
                        pe.wait_ge(S("max" + tag), n - 1)
                    maxima(s, i, jj).then_inc(S("logit" + tag), 1)

                for s in range(units + LAG + 1):
                    for i in range(8):
                        if s < units:
                            if i == 0:
                                slots_ready(s)
                            some_maxima(s, i, 0)
                        if i == 1 and 1 <= s <= units:
                            pe.wait_ge(S("m_parts" + tag), s)
                            if s > LAG + 1:
                                pe.wait_ge(S("o_norm" + tag), 2 * (s - LAG - 1))
                            for qt in range(2):
                                m = pe.transpose(psum[0:48, 7, P * qt:P * qt + P], m3[:, (s - 1) % 2, qt, :],
                                                 ident[:, :])
                            m.then_inc(S("m_turned" + tag), 1)
                        u = s - LAG
                        if 0 <= u < units:
                            n = 8 * u + i
                            if i == 0:
                                pe.wait_ge(S(f"m_slot{u % RING}" if tag == "1" else f"m2_slot{u}"),
                                           48 * (u // RING + 1))
                            if n >= 2:
                                pe.wait_ge(S("prob" + tag), n - 1)
                            probs(u, i // 2, i % 2, 2 + 2 * (i % 2)).then_inc(S("lt" + tag), 1)
                        if s < units:
                            some_maxima(s, i, 1)
                        if i % 2 == 0:
                            G = 4 * u + i // 2 - 1
                            if 0 <= G < 4 * units:
                                pe.wait_ge(S("prob" + tag), 2 * G + 2)
                                if G:
                                    pe.wait_ge(S("o_copied" + tag), G)
                                for kt in range(2):
                                    q0 = P * kt if tag == "2" else 0
                                    for j in range(4):
                                        m = pe.matmul(psum[32 * j:32 * j + 32, 6, q0:256], values(G, kt, j),
                                                      Pb[2 * (G % 2) + kt][:, (256 - q0) * j:(256 - q0) * (j + 1)],
                                                      start=(kt == 0), stop=(kt == 1), skip_group_check=True,
                                                      tile_position=(0, 32 * j))
                                m.then_inc(S("o_sum" + tag), 1)
                        if i in (2, 4) and 0 <= u - 1 < units:
                            qt = i // 2 - 1
                            pe.wait_ge(S("o_copied" + tag), 4 * u)
                            pe.wait_ge(S("m_copied" + tag), min(s, units))
                            if qt or u >= 2:
                                pe.wait_ge(S("o_norm" + tag), 2 * (u - 1) + qt)
                            for g in range(4):
                                m = pe.transpose(psum[:, 7, P * g:P * g + P],
                                                 osb[:, (u - 1) % 2, 256 * g + P * qt:256 * g + P * qt + P],
                                                 ident[:, :])
                            m.then_inc(S("o_turned" + tag), 1)

            def ready1(u):
                pe.wait_ge(S(f"k_slot{u % RING}"), 16 + 144 * (u // RING + 1))
                pe.wait_ge(S(f"q_slot{u % RING}"), 144 * (u // RING + 1))

            def maxima1(u, i, jj):
                qt, g = i // 4, i % 4
                for j in range(2):
                    h = 4 * g + 2 * jj + j
                    m = pe.matmul(psum[:, jj, 256 * j:256 * j + 256],
                                  qs[u % RING][0:72, h, P * qt:P * qt + P],
                                  ks[u % RING][0:72, h, :], start=True, stop=True)
                return m

            def probs1(u, g, kt, at):
                for j in range(4):
                    m = pe.matmul(psum[:, at + j // 2, 256 * (j % 2):256 * (j % 2) + 256],
                                  ks[u % RING][:, 4 * g + j, P * kt:P * kt + P],
                                  qs[u % RING][:, 4 * g + j, :], start=True, stop=True)
                return m

            attention("1", UNITS, ready1, maxima1, probs1,
                      lambda G, kt, j: vaug[:, 2 * (G // 4 % B) + kt, 16 * (G // 16) + 4 * (G % 4) + j, :])
            pe.wait_ge(S("o_norm1"), 2 * UNITS)
            turn_tiles(lambda t, k: attn[:, t, P * k:P * k + P], 0, None, "attn_turned")
            pe.wait_ge(S("attnT_out"), 4)
            for t in range(T):
                dst = psum[:, 4 + t // 2, C * (t % 2):C * (t % 2) + C]
                for k in range(2):
                    pe.matmul(dst, xnT[:, k, P * t:P * t + P], wout[:, k, :], start=(k == 0), stop=False)
                m = pe.matmul(dst, onesr[:, :], bout[:, :], start=False, stop=True)
                if t % 2:
                    m.then_inc(S("proj1"), 1)

            pe.wait_ge(S("x3"), 4)
            turn_tiles(lambda t, k: xn[:, t, P * k:P * k + P], 0, "xn3", "n3_turned")
            pe.wait_ge(S("n3_out"), 4)
            for t in range(T):
                for k in range(2):
                    m = pe.matmul(psum[:, 4, H2 * t:H2 * t + H2], xnT[:, k, P * t:P * t + P], wg16[:, k, :],
                                  start=(k == 0), stop=(k == 1))
            m.then_inc(S("gate_logit"), 1)
            for k in range(2):
                for c in range(2):
                    for kk in range(2):
                        m = pe.matmul(bank(2 * k + c), wqkv[:, kk, P * k:P * k + P],
                                      xnT[:, kk, 512 * c:512 * c + 512], start=(kk == 0), stop=(kk == 1))
                m.then_inc(S("q2_proj"), 1)
            for t in range(T):
                if t >= 2:
                    pe.wait_ge(S("kv_read"), t - 1)
                for kk in range(2):
                    m = pe.matmul(bank(5 + t % 2), xnT[:, kk, P * t:P * t + P], wqkv[:, kk, C:3 * C],
                                  start=(kk == 0), stop=(kk == 1))
                m.then_inc(S("kv_proj"), 1)
            pe.wait_ge(S("kt_ready"), 1)
            pe.wait_ge(S("kv_read"), T)
            for t in range(T):
                pe.transpose(psum[:, 6 + t // 4, P * (t % 4):P * (t % 4) + P], kt[:, t, 0:P], ident[:, :])
                m = pe.transpose(psum[0:19, 4 + t // 4, P * (t % 4):P * (t % 4) + P], kt[:, t, P:P + 19], ident[:, :])
            m.then_inc(S("ks_turned"), 1)
            pe.wait_ge(S("ks_out"), 2)
            pe.wait_ge(S("q2_low"), 2)

            def ready2(b):
                pe.wait_ge(S(f"q2_slot{b}"), 144)

            def maxima2(b, i, jj):
                qt, g = i // 4, i % 4
                n = P * (qt + 1)
                o = psum[:, jj, 0:2 * n]
                pe.matmul(o, identb[:, :], maskA[:, :, 256 - n:256], start=True, stop=False,
                          skip_group_check=True)
                for j in range(2):
                    h = 4 * g + 2 * jj + j
                    pe.matmul(o[:, n * j:n * j + n], qs2[b][:, h, P * qt:P * qt + P],
                              ks2[:, L * b:L * b + n], start=False, stop=False, skip_group_check=True)
                    m = pe.matmul(o[:, n * j:n * j + n], qx2[b][0:16, h, P * qt:P * qt + P],
                                  kx2[0:16, L * b:L * b + n], start=False, stop=(j == 1), skip_group_check=True)
                return m

            def probs2(b, g, kt, at):
                q0 = P * kt
                n = 256 - q0
                for jj in range(2):
                    h = 4 * g + 2 * jj
                    o = psum[:, at + jj, 0:2 * n]
                    pe.matmul(o, identb[:, :], maskB[:, :, 0:n], start=True, stop=False, skip_group_check=True)
                    pe.matmul(o, ks2[:, L * b + q0:L * b + q0 + P], qs2[b][:, h:h + 2, q0:256],
                              start=False, stop=False, skip_group_check=True)
                    m = pe.matmul(o, kx2[:, L * b + q0:L * b + q0 + P], qx2[b][:, h:h + 2, q0:256],
                                  start=False, stop=True, skip_group_check=True)
                return m

            attention("2", B, ready2, maxima2, probs2, lambda G, kt, j: va2[:, 2 * (G // 4) + kt, :])

        @block.scalar
        def _(act):
            chain = [0]

            def link(ins):
                chain[0] += 1
                ins.then_inc(S("act_chain"), 1)
                act.wait_ge(S("act_chain"), chain[0])

            def rstd_of(n):
                act.wait_ge(S("mv"), n + 1)
                link(act.activation(lnv[:, :], mv[:, :, 1], ACT.Ln, bias=consts[:, 0:1]))
                act.activation(rstd[:, :], lnv[:, :], ACT.Exp, scale=-0.5).then_inc(S("rstd"), 1)

            def evacuate(turned, done):
                act.wait_ge(S(turned), 4)
                act.activation(xnT[:, 0, 0:512], bank(0), ACT.Copy).then_inc(S(done), 1)
                act.wait_ge(S(turned), 8)
                act.activation(xnT[:, 0, 512:1024], bank(1), ACT.Copy).then_inc(S(done), 1)

            act.wait_ge(S("inproj"), 1)
            act.wait_ge(S("xin_zero"), 1)
            for k in range(2):
                act.activation(xp[:, k, :, 3:3 + L], bank(2 * k, 2).rearrange("p (b l) -> p b l", b=B),
                               ACT.Copy).then_inc(S("xin_copied"), 1)
            act.wait_ge(S("ld_small"), 16 * 12)
            act.activation(tg[:, :], gates[:, :], ACT.Tanh).then_inc(S("tg"), 1)
            act.activation(negA, negA, ACT.Exp).then_inc(S("expA"), 1)
            rstd_of(0)
            act.wait_ge(S("ang_ready"), 1)
            act.activation(trig, ang, ACT.Sin).then_inc(S("trig_ready"), 1)
            for k in range(2):
                act.wait_ge(S("conv_done"), k + 1)
                act.activation(u[:, k, :], conv[:, k, :], ACT.Silu, bias=convb[:, k:k + 1]).then_inc(S("u_ready"), 1)
            act.wait_ge(S("xn0"), T)
            for k in range(2):
                act.activation(zg[:, k, :].rearrange("p (b l) -> p b l", b=B), xn[:, k:T:2, :], ACT.Silu)\
                   .then_inc(S("z_out"), 1)
            act.wait_ge(S("xdbl"), 1)
            act.activation(mid3[96:104, :], psum[96:104, 0:2, :].rearrange("p a b -> p (a b)"), ACT.Copy)\
               .then_inc(S("dtlow"), 1)
            act.activation(hib, psum[0:96, 0:2, :].rearrange("p a b -> p (a b)"), ACT.Copy).then_inc(S("hi_ready"), 1)
            for k in range(2):
                act.wait_ge(S("dtpre"), k + 1)
                act.activation(absx[k], bank(4 + 2 * k, 2), ACT.Abs, bias=dtb[:, k:k + 1])\
                   .then_inc(S("dtpre_read"), 1)
                act.activation(dt[:, k, :], bank(4 + 2 * k, 2), ACT.Relu, bias=dtb[:, k:k + 1])\
                   .then_inc(S("dtpre_read"), 1)
            act.wait_ge(S("dtpre_read"), 3)
            for k in range(2):
                act.activation(expx[k], absx[k], ACT.Exp, scale=-1.0).then_inc(S("exp_ready"), 1)
            for k in range(2):
                act.wait_ge(S("exp_ready"), k + 1)
                act.activation(w[:, k, :], expx[k], ACT.Ln, bias=consts[:, 1:2]).then_inc(S("ln_ready"), 1)
            act.wait_ge(S("cs_turned"), 1)
            act.activation(csT, psum[0:8, 2:4, :].rearrange("p a b -> p (a b)"), ACT.Copy).then_inc(S("cs_copied"), 1)
            for i, dst in enumerate((cosT, sinT)):
                act.wait_ge(S("cs_spread"), i + 1)
                act.activation(dst[:, :], bank(2 * i, 2), ACT.Copy).then_inc(S("cs_out"), 1)
            act.wait_ge(S("k_proj"), 1)
            for k in range(2):
                act.activation(k1T[:, k, :], bank(4 + 2 * k, 2), ACT.Copy).then_inc(S("k_out"), 1)
            act.wait_ge(S("k_proj"), 2)
            for k in range(2):
                act.activation(k2T[:, k, :], bank(2 * k, 2), ACT.Copy).then_inc(S("k_out"), 1)
            act.wait_ge(S("v_proj"), 1)
            act.wait_ge(S("vaug_ones"), 1)
            for n in range(4):
                act.activation(vaug[:, 2 * n:2 * n + 2, :, 0:D1],
                               bank(4 + n).rearrange("p (t h e) -> p t h e", t=2, h=H1), ACT.Copy)\
                   .then_inc(S("v_out"), 1)
            for i in range(2 * NS):
                k, n = i // NS, i % NS
                act.wait_ge(S("b_spread"), i + 1)
                if i >= 2:
                    act.wait_ge(S("dBu_ready"), i - 1)
                act.activation(Bsb[i % 2], bank(2 * (i % 2), 2), ACT.Copy).then_inc(S("b_copied"), 1)
                if n == 0:
                    act.wait_ge(S("w_ready"), k + 1)
                if i == 0:
                    act.wait_ge(S("negA"), 1)
                    act.wait_ge(S("dA_zero"), 1)
                if i >= 2:
                    act.wait_ge(S("scanned"), i - 1)
                act.activation(dA[i % 2].rearrange("p (b l) -> p b l", b=B)[:, :, 1:L],
                               dt[:, k, :].rearrange("p (b l) -> p b l", b=B)[:, :, 1:L], ACT.Exp,
                               scale=negA[:, k, n:n + 1]).then_inc(S("dA_ready"), 1)
            rstd_of(1)
            evacuate("n1_turned", "n1_out")
            act.wait_ge(S("m_diff"), 1)
            act.activation(w1, w2, ACT.Exp).then_inc(S("e2"), 1)
            for i in range(2 * NF):
                act.wait_ge(S("gate_up"), 2 * i + 1)
                if i >= 2:
                    act.wait_ge(S("gu_done"), i - 1)
                act.activation(sg[:, i % 2, :], bank(3 * (i % 2)), ACT.Silu).then_inc(S("silu_done"), 1)
            rstd_of(2)
            evacuate("n2_turned", "n2_out")
            act.wait_ge(S("k_stored"), 96)
            for k in range(2):
                act.wait_ge(S("q_rotated"), k + 1)
                act.activation(parts[:, 0, k, :], qr[:, k, :], ACT.Copy).then_inc(S("q_high"), 1)
                act.wait_ge(S("q_rest"), k + 1)
                act.activation(parts[:, 1, k, :], qr[:, k, :], ACT.Copy).then_inc(S("q_high"), 1)

            def attention(tag, units, scale):
                for s in range(units + LAG + 1):
                    u = s - LAG
                    for i in range(8):
                        if i == 1 and 1 <= s <= units:
                            act.wait_ge(S("m_turned" + tag), s)
                            if s >= 3 and tag == "1":
                                act.wait_ge(S(f"m_slot{(s - 3) % RING}"), 48 * ((s - 3) // RING + 1))
                            if s >= 3 and tag == "2":
                                act.wait_ge(S(f"m2_slot{s - 3}"), 48)
                            act.activation(mrow[:, (s - 1) % 2, :], psum[0:48, 7, 0:256], ACT.Copy)\
                               .then_inc(S("m_copied" + tag), 1)
                        if 0 <= u < units:
                            n, g, kt = 8 * u + i, 4 * u + i // 2, i % 2
                            act.wait_ge(S("lt" + tag), n + 1)
                            if g >= 2:
                                act.wait_ge(S("o_sum" + tag), g - 1)
                            w2n = 512 - 256 * kt if tag == "2" else 512
                            act.activation(Pb[2 * (g % 2) + kt][:, 0:2 * w2n].rearrange("p (a b) -> p a b", a=2),
                                           psum[:, 2 + 2 * kt:4 + 2 * kt, 0:w2n], ACT.Exp, scale=scale)\
                               .then_inc(S("prob" + tag), 1)
                        G = 4 * u + i // 2 - 1
                        if i % 2 == 0 and 0 <= G < 4 * units:
                            act.wait_ge(S("o_sum" + tag), G + 1)
                            if G >= 8 and G % 4 == 0:
                                act.wait_ge(S("o_turned" + tag), 2 * (G // 4 - 1))
                            act.activation(osb[:, G // 4 % 2, 256 * (G % 4):256 * (G % 4) + 256], psum[:, 6, 0:256],
                                           ACT.Copy).then_inc(S("o_copied" + tag), 1)

            attention("1", UNITS, float(D1) ** -0.5)
            evacuate("attn_turned", "attnT_out")
            rstd_of(3)
            evacuate("n3_turned", "n3_out")
            for k in range(2):
                act.wait_ge(S("q2_proj"), k + 1)
                act.activation(parts[:, 0, k, :], bank(2 * k, 2), ACT.Copy).then_inc(S("q2_high"), 1)
                act.wait_ge(S("q2_rest"), k + 1)
                act.activation(parts[:, 1, k, :], qr[:, k, :], ACT.Copy).then_inc(S("q2_high"), 1)
            act.wait_ge(S("gdiff"), 1)
            act.activation(gt[:, :, :], gt[:, :, :], ACT.Exp).then_inc(S("gexp"), 1)
            act.wait_ge(S("ks_turned"), 1)
            act.activation(ks2, bank(6, 2), ACT.Copy).then_inc(S("ks_out"), 1)
            act.activation(kx2, psum[0:19, 4:6, :].rearrange("p a b -> p (a b)"), ACT.Copy).then_inc(S("ks_out"), 1)
            attention("2", B, float(D2) ** -0.5)

        @block.gpsimd
        def _(pool):
            pool.memset(vaug[:, :, :, :], 1.0).then_inc(S("vaug_ones"), 1)
            pool.memset(tw3[:, :, :], 0.0).then_inc(S("tw3_zero"), 1)
            for i in range(2 * NS):
                k = i // NS
                if i % NS == 0:
                    pool.wait_ge(S("w_ready"), k + 1)
                pool.wait_ge(S("b_copied"), i + 1)
                if i >= 2:
                    pool.wait_ge(S("scanned"), i - 1)
                pool.tensor_tensor(dBu[:, i % 2, :], w[:, k, :], Bsb[i % 2], ALU.mult).then_inc(S("dBu_ready"), 1)
            pool.wait_ge(S("k_out"), 4)
            pool.wait_ge(S("cs_out"), 2)
            for k in range(2):
                pool.tensor_tensor(k1T[:, k, :], k1T[:, k, :], cosT[:, :], ALU.mult).then_inc(S("k_rot"), 1)
                pool.tensor_tensor(k2T[:, k, :], k2T[:, k, :], sinT[:, :], ALU.mult).then_inc(S("k_rot"), 1)
            pool.wait_ge(S("k_rot"), 4)
            done = 4
            for k in range(2):
                pool.tensor_tensor(k1T[:, k, :], k1T[:, k, :], k2T[:, k, :], ALU.add).then_inc(S("k_rot"), 1)
                pool.wait_ge(S("k_rot"), 5 + 2 * k)
                pool.tensor_copy(parts[:, 0, k, :], k1T[:, k, :]).then_inc(S("k_parts"), 1)
                pool.wait_ge(S("k_parts"), 3 * k + 1)
                pool.tensor_tensor(k1T[:, k, :], k1T[:, k, :], parts[:, 0, k, :], ALU.subtract).then_inc(S("k_rot"), 1)
                pool.wait_ge(S("k_rot"), 6 + 2 * k)
                pool.tensor_copy(parts[:, 1, k, :], k1T[:, k, :]).then_inc(S("k_parts"), 1)
                pool.wait_ge(S("k_parts"), 3 * k + 2)
                pool.tensor_tensor(parts[:, 2, k, :], k1T[:, k, :], parts[:, 1, k, :], ALU.subtract)\
                    .then_inc(S("k_parts"), 1)

            def maxima_parts(tag, units):
                for u in range(units):
                    pool.wait_ge(S("max" + tag), 16 * (u + 1))
                    if u >= 2:
                        pool.wait_ge(S("m_turned" + tag), u - 1)
                    c = 4 * u
                    o = m3[:, u % 2, :, :]

                    def step(ins, n):
                        ins.then_inc(S("m_step" + tag), 1)
                        pool.wait_ge(S("m_step" + tag), c + n)

                    step(pool.tensor_scalar(mr[:, :, :], mx[:, u % 2, :, :], -1.0, 0.0, ALU.mult, ALU.add), 1)
                    step(pool.tensor_copy(mb[:, :, :], mr[:, :, :]), 2)
                    pool.tensor_copy(o[:, :, 0:16], mb[:, :, :])
                    step(pool.tensor_tensor(mr[:, :, :], mr[:, :, :], mb[:, :, :], ALU.subtract), 3)
                    step(pool.tensor_copy(mb[:, :, :], mr[:, :, :]), 4)
                    pool.tensor_copy(o[:, :, 16:32], mb[:, :, :])
                    pool.tensor_tensor(o[:, :, 32:48], mr[:, :, :], mb[:, :, :], ALU.subtract)\
                        .then_inc(S("m_parts" + tag), 1)
                    pool.wait_ge(S("m_parts" + tag), u + 1)

            maxima_parts("1", UNITS)
            maxima_parts("2", B)

        @block.vector
        def _(v):
            chain = [0]

            def link(ins):
                chain[0] += 1
                ins.then_inc(S("dve_chain"), 1)
                v.wait_ge(S("dve_chain"), chain[0])

            def norm_stats(n, tiles=range(T), ready=None):
                for t in range(T):
                    if ready:
                        v.wait_ge(S(ready), t // 2 + 1)
                    last = v.bn_stats(stats[:, t, :], x[:, t, :])
                link(last)
                for t in range(T):
                    last = v.bn_aggr(mv[:, t, :], stats[:, t, :])
                last.then_inc(S("mv"), 1)

            def norm_apply(n, name):
                v.wait_ge(S("rstd"), n + 1)
                for t in range(T):
                    v.tensor_scalar(xn[:, t, :], x[:, t, :], mv[:, t, 0:1], rstd[:, t:t + 1],
                                    ALU.subtract, ALU.mult).then_inc(S(name), 1)

            def evacuate(turned, done):
                v.wait_ge(S(turned), 4)
                v.tensor_copy(xnT[:, 1, 0:512], bank(2)).then_inc(S(done), 1)
                v.wait_ge(S(turned), 8)
                v.tensor_copy(xnT[:, 1, 512:1024], bank(3)).then_inc(S(done), 1)

            v.memset(xp[:, :, :, 0:3], 0.0).then_inc(S("xin_zero"), 1)
            v.wait_ge(S("ld_pos"), 16)
            a4 = ang.rearrange("p t (s a i) -> p t s a i", s=2, a=2)
            for s in range(2):
                for i in range(2):
                    last = v.tensor_scalar(a4[:, :, s, :, i], pos, 10000.0 ** (-i / 2), None, ALU.mult)
            link(last)
            for s in range(2):
                c8 = slice(4 * s, 4 * s + 4)
                last = v.tensor_scalar(rnd[:, :, c8], ang[:, :, c8], 1.0 / 6.283185307179586,
                                       0.25 if s == 0 else 0.0, ALU.mult, ALU.add)
            link(last)
            link(v.tensor_scalar(rnd, rnd, ROUND, None, ALU.add))
            link(v.tensor_scalar(rnd, rnd, ROUND, None, ALU.subtract))
            link(v.scalar_tensor_tensor(ang, rnd, -TWO_PI_HI, ang, ALU.mult, ALU.add))
            link(v.scalar_tensor_tensor(ang, rnd, -TWO_PI_LO, ang, ALU.mult, ALU.add))
            link(v.tensor_scalar(ang[:, :, 0:4], ang[:, :, 0:4], 1.5707963267948966, None, ALU.add))
            v.tensor_scalar(ang, ang, PI_IN, -PI_IN, ALU.min, ALU.max).then_inc(S("ang_ready"), 1)
            v.wait_ge(S("ld_x"), 16)
            norm_stats(0)
            v.wait_ge(S("ld_small"), 16 * 12)
            for k in range(2):
                v.wait_ge(S("xin_copied"), k + 1)
                cv = conv[:, k, :].rearrange("p (b l) -> p b l", b=B)
                link(v.tensor_scalar(cv, xp[:, k, :, 0:L], convw[:, k, 0:1], None, ALU.mult))
                for j in range(1, KCONV):
                    m = v.scalar_tensor_tensor(cv, xp[:, k, :, j:j + L], convw[:, k, j:j + 1], cv,
                                               ALU.mult, ALU.add)
                    if j < KCONV - 1:
                        link(m)
                m.then_inc(S("conv_done"), 1)
            norm_apply(0, "xn0")
            v.wait_ge(S("expA"), 1)
            v.tensor_scalar(negA, negA, -1.0, None, ALU.mult).then_inc(S("negA"), 1)
            v.wait_ge(S("hi_ready"), 1)
            xd = psum[0:96, 0:2, :].rearrange("p a b -> p (a b)")
            rest = mid3[0:96, :]
            v.tensor_tensor(rest, xd, hib, ALU.subtract).then_inc(S("split_read"), 1)
            v.wait_ge(S("split_read"), 1)
            link(v.tensor_copy(midb, rest))
            link(v.tensor_tensor(rest, rest, midb, ALU.subtract))
            link(v.tensor_copy(lob, rest))
            v.tensor_copy(dsplit[0:32, :], hib[0:32, :])
            v.tensor_copy(dsplit[32:64, :], midb[32:64, :])
            v.tensor_copy(dsplit[64:96, :], lob[64:96, :]).then_inc(S("split_done"), 1)
            def softplus(k, n):
                e, s, small = expx[k], absx[k], (prod[:, 0, :] if k == 0 else second[:, 2, :]).bitcast(I32)
                if n == 0:
                    v.wait_ge(S("exp_ready"), k + 1)
                    link(v.tensor_scalar(s, e, 0.2, -0.25, ALU.mult, ALU.add))
                if n == 1:
                    link(v.tensor_tensor(s, s, e, ALU.mult))
                if n == 2:
                    link(v.scalar_tensor_tensor(s, s, 1.0 / 3.0, e, ALU.add, ALU.mult))
                if n == 3:
                    link(v.scalar_tensor_tensor(s, s, -0.5, e, ALU.add, ALU.mult))
                if n == 4:
                    link(v.scalar_tensor_tensor(s, s, 1.0, e, ALU.add, ALU.mult))
                    if k == 0:
                        v.wait_ge(S("z_out"), 2)
                    link(v.tensor_scalar(small, e, SMALL, None, ALU.is_lt))
                if n == 5:
                    v.wait_ge(S("ln_ready"), k + 1)
                    link(v.copy_predicated(w[:, k, :], small, s))
                if n == 6:
                    link(v.tensor_tensor(dt[:, k, :], dt[:, k, :], w[:, k, :], ALU.add))
                if n == 7:
                    v.tensor_tensor(w[:, k, :], dt[:, k, :], u[:, k, :], ALU.mult).then_inc(S("w_ready"), 1)

            for n in range(8):
                softplus(0, n)
            for i in range(2):
                last = v.memset(dA[i].rearrange("p (b l) -> p b l", b=B)[:, :, 0:1], 0.0)
            last.then_inc(S("dA_zero"), 1)

            def take_y(k):
                v.wait_ge(S("y_sum"), NS * (k + 1))
                v.scalar_tensor_tensor(yT[:, k, :], u[:, k, :], Dp[:, k:k + 1], bank(6, 2),
                                       ALU.mult, ALU.add).then_inc(S("y_taken"), 1)
                v.wait_ge(S("y_taken"), k + 1)
                v.tensor_tensor(yT[:, k, :], yT[:, k, :], zg[:, k, :], ALU.mult).then_inc(S("y_gated"), 1)

            for i in range(2 * NS):
                v.wait_ge(S("dA_ready"), i + 1)
                v.wait_ge(S("dBu_ready"), i + 1)
                v.tensor_tensor_scan(hst[:, i % 2, :], dA[i % 2], dBu[:, i % 2, :], 0.0, ALU.mult, ALU.add)\
                 .then_inc(S("scanned"), 1)
                if i == NS:
                    take_y(0)
                v.wait_ge(S("scanned"), i + 1)
                v.wait_ge(S("c_spread"), i + 1)
                if i >= 2:
                    v.wait_ge(S("y_sum"), i - 1)
                v.tensor_tensor(prod[:, i % 2, :], hst[:, i % 2, :], bank(4, 2), ALU.mult)\
                 .then_inc(S("prod_ready"), 1)
                if i < 8:
                    softplus(1, i)
            take_y(1)
            v.wait_ge(S("tg"), 1)

            def residual(n, turned, banks, gate, name, t0=0):
                for c in range(n):
                    v.wait_ge(S(turned), t0 // 2 + c + 1)
                    xs = x[:, t0 + 2 * c:t0 + 2 * c + 2, :].rearrange("p a b -> p (a b)")
                    v.scalar_tensor_tensor(xs, bank(banks + c), tg[:, gate:gate + 1], xs, ALU.mult, ALU.add)\
                     .then_inc(S(name), 1)

            residual(4, "y_turned", 0, 0, "x1")
            norm_stats(1, ready="x1")
            norm_apply(1, "xn1")
            evacuate("n1_turned", "n1_out")
            v.wait_ge(S("tw3_zero"), 1)
            v.wait_ge(S("router"), 1)
            v.tensor_copy(rl, psum[:, 4, 0:T * E].rearrange("p (t e) -> p t e", t=T)).then_inc(S("router_read"), 1)
            v.wait_ge(S("router_read"), 1)

            def bc(a, n):
                return a.unsqueeze(2).to_broadcast([P, T, n])

            def first_best(val, m, ind, work, best, rank, n):
                link(v.tensor_reduce(m, val, AX.X, ALU.max))
                link(v.tensor_tensor(work, val, bc(m, n), ALU.is_equal))
                link(v.tensor_tensor(work, work, rank.unsqueeze(1).to_broadcast([P, T, n]), ALU.mult))
                link(v.tensor_reduce(best, work, AX.X, ALU.max))
                link(v.tensor_tensor(ind, work, bc(best, n), ALU.is_equal))

            first_best(rl, m1, i1, tmp8, mi, rank8[:, :], E)
            link(v.scalar_tensor_tensor(rl, i1, -1e30, rl, ALU.mult, ALU.add))
            first_best(rl, m2, i2, tmp8, mi, rank8[:, :], E)
            v.tensor_tensor(w2, m2, m1, ALU.subtract).then_inc(S("m_diff"), 1)
            v.wait_ge(S("e2"), 1)
            link(v.tensor_scalar(w2, w1, 1.0, None, ALU.add))
            link(v.reciprocal(m1, w2))
            link(v.tensor_tensor(m2, m1, w1, ALU.mult))
            link(v.tensor_tensor(i1, i1, bc(m1, E), ALU.mult))
            link(v.tensor_tensor(i2, i2, bc(m2, E), ALU.mult))
            link(v.tensor_tensor(tw, i1, i2, ALU.add))
            link(v.tensor_copy(twb, tw))
            v.tensor_copy(tw3[:, :, 0:E], twb)
            link(v.tensor_tensor(tw, tw, twb, ALU.subtract))
            link(v.tensor_copy(twb, tw))
            v.tensor_copy(tw3[:, :, 32:32 + E], twb)
            v.tensor_tensor(tw3[:, :, 64:64 + E], tw, twb, ALU.subtract).then_inc(S("tw_ready"), 1)
            v.wait_ge(S("tw_turned"), 1)
            v.tensor_copy(twT[:, :], psum[0:96, 6:8, :].rearrange("p a b -> p (a b)")).then_inc(S("twT_ready"), 1)
            for i in range(2 * NF):
                f = i % NF
                v.wait_ge(S("silu_done"), i + 1)
                v.wait_ge(S("gate_up"), 2 * i + 2)
                v.tensor_tensor(h1[:, i % 2, :], sg[:, i % 2, :], bank(3 * (i % 2) + 1), ALU.mult)\
                 .then_inc(S("gu_done"), 1)
                v.wait_ge(S("gu_done"), i + 1)
                v.wait_ge(S("tw_spread"), i + 1)
                if i == NF:
                    v.wait_ge(S("down"), 2)
                v.tensor_tensor(hid[:, f, :], h1[:, i % 2, :], bank(3 * (i % 2) + 2), ALU.mult)\
                 .then_inc(S("hid_ready"), 1)
                if i == NF:
                    residual(2, "down", 6, 2, "x2", 0)
            residual(2, "down", 6, 2, "x2", 4)
            norm_stats(2, ready="x2")
            norm_apply(2, "xn2")
            evacuate("n2_turned", "n2_out")
            v.wait_ge(S("k_parts"), 6)
            for k in range(2):
                v.wait_ge(S("q_proj"), k + 1)
                v.tensor_tensor(qr[:, k, :], bank(2 * k, 2), cosT[:, :], ALU.mult)
                v.wait_ge(S("q_proj"), k + 3)
                link(v.tensor_tensor(tmpq[:, k, :], bank(4 + 2 * k, 2), sinT[:, :], ALU.mult))
                v.tensor_tensor(qr[:, k, :], qr[:, k, :], tmpq[:, k, :], ALU.add).then_inc(S("q_rotated"), 1)
                v.wait_ge(S("q_high"), 2 * k + 1)
                v.tensor_tensor(qr[:, k, :], qr[:, k, :], parts[:, 0, k, :], ALU.subtract).then_inc(S("q_rest"), 1)
                v.wait_ge(S("q_high"), 2 * k + 2)
                v.tensor_tensor(parts[:, 2, k, :], qr[:, k, :], parts[:, 1, k, :], ALU.subtract)\
                 .then_inc(S("q_low"), 1)

            def attention(tag, units, finish):
                for s in range(units + LAG + 1):
                    u = s - LAG
                    for i in range(8):
                        if s < units:
                            qt, g = i // 4, i % 4
                            n = P * (qt + 1) if tag == "2" else 256
                            for jj in range(2):
                                v.wait_ge(S("logit" + tag), 16 * s + 2 * i + jj + 1)
                                if s >= 2 and i == jj == 0:
                                    v.wait_ge(S("m_parts" + tag), s - 1)
                                h = 4 * g + 2 * jj
                                v.tensor_reduce(mx[:, s % 2, qt, h:h + 2],
                                                psum[:, jj, 0:2 * n].rearrange("p (j k) -> p j k", j=2),
                                                AX.X, ALU.max).then_inc(S("max" + tag), 1)
                        if i in (3, 5) and 0 <= u - 1 < units:
                            finish(u - 1, (i - 3) // 2)

            def finish1(u, qt):
                t, k = 2 * (u % B) + qt, u // B
                v.wait_ge(S("o_turned1"), 2 * u + qt + 1)
                o = bank(7).rearrange("p (h e) -> p h e", e=32)
                link(v.reciprocal(rec[:, t, :], o[:, :, D1]))
                v.tensor_tensor(attn[:, t, P * k:P * k + P].rearrange("p (h e) -> p h e", e=D1), o[:, :, 0:D1],
                                rec[:, t, :].unsqueeze(2).to_broadcast([P, 16, D1]), ALU.mult)\
                 .then_inc(S("o_norm1"), 1)

            attention("1", UNITS, finish1)
            evacuate("attn_turned", "attnT_out")
            residual(4, "proj1", 4, 1, "x3")
            norm_stats(3, ready="x3")
            norm_apply(3, "xn3")
            evacuate("n3_turned", "n3_out")
            v.wait_ge(S("gate_logit"), 1)
            link(v.tensor_copy(gl[:, :, :], psum[:, 4, 0:T * H2].rearrange("p (t e) -> p t e", t=T)))
            for k in range(2):
                v.wait_ge(S("q2_high"), 2 * k + 1)
                v.tensor_tensor(qr[:, k, :], bank(2 * k, 2), parts[:, 0, k, :], ALU.subtract).then_inc(S("q2_rest"), 1)
                v.wait_ge(S("q2_high"), 2 * k + 2)
                v.tensor_tensor(parts[:, 2, k, :], qr[:, k, :], parts[:, 1, k, :], ALU.subtract)\
                 .then_inc(S("q2_low"), 1)
            first_best(gl[:, :, :], gm[:, :], gi[:, :, :], gt[:, :, :], gs[:, :], rank16[:, :], H2)
            v.tensor_tensor(gt[:, :, :], gl[:, :, :], bc(gm[:, :], H2), ALU.subtract).then_inc(S("gdiff"), 1)
            v.wait_ge(S("gexp"), 1)
            link(v.tensor_reduce(gs[:, :], gt[:, :, :], AX.X, ALU.add))
            link(v.reciprocal(gm[:, :], gs[:, :]))
            for t in range(T):
                v.wait_ge(S("kv_proj"), t + 1)
                g4 = kvp[:, t % 2, :].rearrange("p (s h e) -> p s h e", s=2, h=H2)
                for s in range(2):
                    m = v.tensor_tensor(g4[:, s], bank(5 + t % 2)[:, 256 * s:256 * s + 256].rearrange("p (h e) -> p h e", h=H2),
                                        gi[:, t, :].unsqueeze(2).to_broadcast([P, H2, D2]), ALU.mult)
                m.then_inc(S("kv_read"), 1)
                v.wait_ge(S("kv_read"), t + 1)
                for s in range(2):
                    m = v.tensor_reduce(ksv[:, t, s, :], g4[:, s].rearrange("p h e -> p e h"), AX.X, ALU.add)
                link(m)
                v.tensor_scalar(va2[:, t, 0:D2], ksv[:, t, 1, :], gm[:, t:t + 1], None, ALU.mult)
                v.memset(va2[:, t, D2:32], 1.0)
            key = ksv[:, :, 0, :]
            for c in range(3):
                if c < 2:
                    link(v.tensor_copy(kb[:, :, :], key))
                    src = kb[:, :, :]
                else:
                    src = key
                for a in range(3):
                    r = D2 * (3 * a + c)
                    v.tensor_copy(kt[:, :, r:r + D2], src)
                if c < 2:
                    link(v.tensor_tensor(key, key, kb[:, :, :], ALU.subtract))
            v.memset(kt[:, :, 144:147], 1.0).then_inc(S("kt_ready"), 1)

            def finish2(b, qt):
                t = 2 * b + qt
                v.wait_ge(S("o_turned2"), t + 1)
                o = bank(7).rearrange("p (h e) -> p h e", e=32)
                link(v.reciprocal(rec[:, t, :], o[:, :, D2]))
                f = fin[:, t % 2, :]
                v.tensor_tensor(f.rearrange("p (h e) -> p h e", e=D2), o[:, :, 0:D2],
                                rec[:, t, :].unsqueeze(2).to_broadcast([P, H2, D2]), ALU.mult)\
                 .then_inc(S("o_norm2"), 1)
                v.wait_ge(S("o_norm2"), t + 1)
                m = v.scalar_tensor_tensor(x[:, t, :], f, tg[:, 3:4], x[:, t, :], ALU.mult, ALU.add)
                if t % 2:
                    m.then_inc(S("fin_ready"), 1)

            attention("2", B, finish2)


def kernel(**inputs):
    import ml_dtypes
    import numpy as np
    import concourse.bacc as bacc
    from concourse.bass_utils import run_bass_kernel_spmd as run

    bf = ml_dtypes.bfloat16
    g = {k: np.ascontiguousarray(v) for k, v in inputs.items()}
    a = {}

    def rows(w_t, k=2):
        return w_t.reshape(k, P, -1).transpose(1, 0, 2)

    a["x"] = g["x"]
    a["ctxT"] = g["ctx_1024"].reshape(NT, CTX).T
    a["win"] = g["L0_xattn_in_proj_w"].T
    a["pos"] = g["fside_BxSx2_0"].reshape(T, P, 2).transpose(1, 0, 2)
    a["convw"] = rows(g["L0_xattn_conv_w"].reshape(C, KCONV))
    a["convb"] = g["L0_xattn_conv_b"].reshape(2, P).T
    order = list(range(RANK, RANK + 2 * NS))
    a["xproj"] = rows(g["L0_xattn_x_proj_w"][order * 3 + list(range(RANK))].T)
    a["dtw"] = g["L0_xattn_dt_proj_w"].T
    a["dtb"] = g["L0_xattn_dt_proj_b"].reshape(2, P).T
    a["alog"] = rows(g["L0_xattn_A_log"])
    a["dp"] = g["L0_xattn_D"].reshape(2, P).T
    gates = np.stack([g["g_xattn"][0], g["g_xattn"][1], g["g_ffn"][0], g["g_ffn"][1]])
    a["gates"] = np.broadcast_to(gates, (P, 4))
    swap = np.arange(C).reshape(-1, 2)[:, ::-1].reshape(-1)
    wkv = g["L1_xattn_Wkv"]
    a["wk1"] = wkv[:, :C]
    a["wk2"] = wkv[:, :C][:, swap]
    a["wv"] = wkv[:, C:]
    a["wq1"] = rows(g["L1_xattn_Wq"])
    a["wq2"] = rows(g["L1_xattn_Wq"][:, swap])
    a["wout"] = rows(g["L1_xattn_Wout"])
    a["bout"] = g["L1_xattn_bout"].reshape(1, C)
    a["wqkv"] = rows(g["L1_ffn_W_qkv"].T)
    a["wg16"] = rows(g["L1_ffn_W_gate"].T)
    a["wg8"] = rows(g["L0_ffn_gate_w"].T)
    a["gateT"] = rows(g["L0_ffn_gate_proj"].reshape(E * FD, C).T)
    a["upT"] = rows(g["L0_ffn_up_proj"].reshape(E * FD, C).T)
    a["downT"] = g["L0_ffn_down_proj"].transpose(0, 2, 1).reshape(NF, P, C).transpose(1, 0, 2)
    p = np.arange(P)
    a["ident"] = np.eye(P, dtype=np.float32)
    a["identb"] = np.eye(P, dtype=bf)
    sel = np.zeros((96, 2 * NS, P), bf)
    for n in range(32):
        sel[[n, 32 + n, 64 + n], n] = 1
    a["sel"] = sel
    a["ones3"] = np.ones((3, 16, 256), bf)
    ex = np.zeros((96, NF, P), bf)
    for f in range(NF):
        for part in range(3):
            ex[32 * part + (f * P + p) // FD, f, p] = 1
    a["ex8"] = ex
    ecs = np.zeros((8, 2, P), np.float32)
    pair = p % D1 // 4 * 2 + p % 4 // 2
    ecs[pair, 0, p] = 1
    ecs[4 + pair, 1, p] = np.where(p % 2, 1, -1)
    a["ecs"] = ecs
    mA = np.zeros((P, 2, 256), bf)
    mB = np.zeros((P, 2, 256), bf)
    mA[:, :, 128:] = np.where(p[None, :] > p[:, None], -1e30, 0)[:, None, :]
    mB[:, :, :128] = np.where(p[:, None] > p[None, :], -1e30, 0)[:, None, :]
    a["maskA"], a["maskB"] = mA, mB
    a["rank8"] = np.broadcast_to(np.arange(E, 0, -1, dtype=np.float32), (P, E))
    a["rank16"] = np.broadcast_to(np.arange(H2, 0, -1, dtype=np.float32), (P, H2))
    a["onesr"] = np.ones((1, P), np.float32)
    a["consts"] = np.broadcast_to(np.array([EPS, 1, 0, 0], np.float32), (P, 4))

    nc = bacc.Bacc("TRN2", target_bir_lowering=False, num_devices=1)
    arrays, d = {}, {}
    for name, v in a.items():
        v = np.ascontiguousarray(v)
        arrays["in_" + name] = v
        d[name] = nc.dram_tensor("in_" + name, v.shape, mybir.dt.from_np(v.dtype), kind="ExternalInput").ap()
    out = nc.dram_tensor("out_y", (B, L, C), F32, kind="ExternalOutput").ap()
    flamingo_program(nc, d, out)
    r = run(nc, [arrays], core_ids=[0])
    return r.results[0]["out_y"]
```

```python
from contextlib import ExitStack

import concourse.bass as bass
from concourse import mybir

F32 = mybir.dt.float32
BF16 = mybir.dt.bfloat16
I32 = mybir.dt.int32
ALU = mybir.AluOpType
ACT = mybir.ActivationFunctionType
AX = mybir.AxisListType

P = 128
B, L, C = 4, 256, 256
T = B * L // P
NT = B * L
CTX = 128
NS, RANK, KCONV = 16, 8, 4
E, FD = 8, 176
NF = E * FD // P
H1, D1 = 32, 8
H2, D2 = 16, 16
EPS = 1e-5
SMALL = 0.05
TWO_PI_HI = 6.28125
TWO_PI_LO = 2.0 * 3.141592653589793 - 6.28125
ROUND = 12582912.0
PI_IN = 3.1415925
RING = 4
UNITS = 2 * B
TURN0 = 15
MAX0 = 18
LAG = 2


def flamingo_program(nc, d, out):
    ctx = ExitStack()
    with ctx:
        def sb(name, shape, dt=F32):
            return ctx.enter_context(nc.sbuf_tensor(name, shape, dt))

        sems = {}

        def S(name):
            if name not in sems:
                sems[name] = ctx.enter_context(nc.semaphore(name))
            return sems[name]

        x = sb("x", [P, T, C])
        xn = sb("xn", [P, T, C])
        xnT = sb("xnT", [P, 2, NT])
        stats = sb("stats", [P, T, 6])
        mv = sb("mv", [P, T, 2])
        lnv = sb("lnv", [P, T])
        rstd = sb("rstd", [P, T])
        gates = sb("gates", [P, 4])
        tg = sb("tg", [P, 4])
        consts = sb("consts", [P, 4])
        ident = sb("ident", [P, P])
        identb = sb("identb", [P, P], BF16)
        maskA = sb("maskA", [P, 2, 256], BF16)
        maskB = sb("maskB", [P, 2, 256], BF16)
        rank8 = sb("rank8", [P, E])
        rank16 = sb("rank16", [P, H2])
        onesr = sb("onesr", [1, P])
        wq1 = sb("wq1", [P, 2, C])
        wq2 = sb("wq2", [P, 2, C])
        wout = sb("wout", [P, 2, C])
        bout = sb("bout", [1, C])
        wqkv = sb("wqkv", [P, 2, 3 * C])
        wg16 = sb("wg16", [P, 2, H2])
        wg8 = sb("wg8", [P, 2, E])
        ex8 = sb("ex8", [96, NF, P], BF16)
        tw3 = sb("tw3", [P, T, 96])
        twT = sb("twT", [96, NT], BF16)
        k1T = sb("k1T", [P, 2, NT])
        k2T = sb("k2T", [P, 2, NT])
        vaug = sb("vaug", [P, T, H1, 32])
        cosT = sb("cosT", [P, NT])
        sinT = sb("sinT", [P, NT])
        area = sb("area", [P, 21520])
        used = [0]

        def part(shape, dt=F32, rows=P):
            n = 1
            for s in shape:
                n *= s
            w = n if dt != BF16 else n // 2
            a = area[0:rows, used[0]:used[0] + w]
            used[0] += w
            if dt != F32:
                a = a.bitcast(dt)
            if len(shape) == 2:
                a = a.rearrange("p (a b) -> p a b", a=shape[0])
            elif len(shape) == 3:
                a = a.rearrange("p (a b c) -> p a b c", a=shape[0], b=shape[1])
            return a

        wk1 = part([C]); wk2 = part([C]); wv = part([C]); win = part([C])
        ctxT = part([NT])
        xproj = part([2, 104]); dtw = part([C]); convw = part([2, KCONV]); convb = part([2])
        dtb = part([2]); negA = part([2, NS]); Dp = part([2])
        pos = part([T, 2]); ang = part([T, 8]); rnd = part([T, 8]); trig = part([T, 8])
        ecs = part([2, P], rows=8); csT = part([NT], rows=8)
        sel = part([2 * NS, P], BF16, rows=96)
        dsplit = part([NT], BF16, rows=96)
        zg = part([2, NT]); u = part([2, NT]); dt = part([2, NT]); w = part([2, NT])
        scan0 = used[0]
        xin = part([2, B * (L + 3)]); mid3 = part([NT], rows=P); conv = part([2, NT])
        midb = part([NT], BF16, rows=96); lob = part([NT], BF16, rows=96); hib = part([NT], BF16, rows=96)
        end0 = used[0]
        xp = xin.rearrange("p a (b l) -> p a b l", b=B)
        spare = sb("parts", [P, 3, 2, NT], BF16)
        parts = spare
        second = spare[:, :, :, :].rearrange("p c k t -> p c (k t)").bitcast(F32)
        absx = [xin[:, 0, 0:NT], second[:, 0, :]]
        expx = [conv[:, 0, :], second[:, 1, :]]
        used[0] = scan0
        dA = [part([NT]) for _ in range(2)]
        end0 = max(end0, used[0])
        used[0] = scan0
        dA = [part([NT]) for _ in range(2)]
        dBu = part([2, NT]); hst = part([2, NT])
        prod = xn[:, :, :].rearrange("p (a t) c -> p a (t c)", a=2)
        assert max(end0, used[0]) <= 21520, (end0, used[0])
        yT = xnT

        def b_rows(i):
            return xnT[:, i, :] if i < 2 else area[:, NT * (i % 2):NT * (i % 2) + NT]

        used[0] = 0
        rl = part([T, E]); i1 = part([T, E]); i2 = part([T, E]); tmp8 = part([T, E]); tw = part([T, E])
        m1 = part([T]); m2 = part([T]); mi = part([T]); w1 = part([T]); w2 = part([T]); twb = part([T, E], BF16)
        downT = part([NF, C])
        hid = part([NF, 512])
        free_late = used[0]
        sg = part([2, 512]); h1 = part([2, 512])
        free_sooner = used[0]
        gateT = part([2, E * FD]); upT = part([2, E * FD])
        free_now = used[0]
        used[0] = 0
        Pb = [part([4 * 256]) for _ in range(4)]
        both = used[0]
        PAIR = 2 * 16 * 256 // 2
        slot_at = [21520 - PAIR, 21520 - 2 * PAIR, 21520 - 3 * PAIR, both]
        assert slot_at[0] >= free_now and slot_at[1] >= free_sooner and slot_at[2] >= free_late
        assert both + PAIR <= slot_at[2]
        qs, ks = [], []
        for at in slot_at:
            used[0] = at
            qs.append(part([16, 256], BF16))
            ks.append(part([16, 256], BF16))
        qs2, qx2 = [], []
        for at in slot_at:
            used[0] = at
            qs2.append(part([H2, 256], BF16))
            qx2.append(part([H2, 256], BF16, rows=19))
        ks2 = tw3[:, :, :].rearrange("p a b -> p (a b)")[:, 0:NT // 2].bitcast(BF16)
        kx2 = twT[0:19, :]
        mx = sb("mx", [P, 2, 2, 16])
        mb = sb("mb", [P, 2, 16], BF16)
        mr = sb("mr", [P, 2, 16])
        tmpq_of = [k2T[:, :, 0:512], xn[:, 4:8, :].rearrange("p (k a) c -> p k (a c)", k=2)]
        m3 = sb("m3", [P, 2, 2, 48])
        mrow = sb("mrow", [48, 2, 256], BF16)
        rec = sb("rec", [P, T, 16])
        kt = [xn[:, 4 * h:4 * h + 4, :].rearrange("p t c -> p (t c)")[:, 0:4 * 147]
              .rearrange("p (t r) -> p t r", t=4) for h in range(2)]
        kb = sb("kb", [P, T, D2], BF16)
        qr, osb, attn = k1T, k2T, xn
        kd = nc.dram_tensor("kd", (H1, 3, 3, D1, NT), BF16, kind="Internal").ap()
        qd = nc.dram_tensor("qd", (H1, 3, D1, NT), BF16, kind="Internal").ap()
        q2d = nc.dram_tensor("q2d", (H2, 3, D2, NT), BF16, kind="Internal").ap()
        gl = sb("gl", [P, T, H2])
        va2 = vaug[:, :, 0, :]
        gi = sb("gi", [P, T, H2]); gm = sb("gm", [P, T]); gt = sb("gt", [P, T, H2]); gs = sb("gs", [P, T])
        kvp = cosT[:, :].rearrange("p (a b) -> p a b", a=2)
        ksv = sb("ksv", [P, T, 2, D2])
        fin = sinT[:, 0:2 * C].rearrange("p (a b) -> p a b", a=2)

        psum = ctx.enter_context(nc.psum_tensor("psum", [P, 8, 512], F32))

        def bank(i, n=1):
            return psum[:, i:i + n, :].rearrange("p a b -> p (a b)")

        block = ctx.enter_context(nc.Block())
        xt = d["x"].rearrange("b (t p) c -> p (b t) c", p=P)
        ot = out.rearrange("b (t p) c -> p (b t) c", p=P)

        def batch_of(u):
            return 2 * (u // 4) + u % 2

        def half_of(u):
            return u // 2 % 2

        def m_loaded(tag, u):
            return 48 * (u // RING + 1 if tag == "1" else UNITS // RING + 1)

        @block.sync
        def _(sp):
            def load(dst, name, s):
                sp.dma_start(dst, d[name]).then_inc(S(s), 16)

            load(ctxT, "ctxT", "ld_in")
            load(win, "win", "ld_in")
            sp.dma_start(x[:, :, :], xt).then_inc(S("ld_x"), 16)
            load(pos, "pos", "ld_pos")
            load(wk1, "wk1", "ld_kv")
            load(wk2, "wk2", "ld_kv")
            for dst, name in ((convw, "convw"), (convb, "convb"), (xproj, "xproj"), (dtb, "dtb"),
                              (negA, "alog"), (Dp, "dp"), (gates[:, :], "gates"), (ident[:, :], "ident"), (ecs, "ecs"),
                              (sel, "sel"), (consts[:, :], "consts")):
                load(dst, name, "ld_small")
            sp.dma_start(dtw[96:104, :], d["dtw"]).then_inc(S("ld_small"), 16)
            load(wv, "wv", "ld_v")
            for dst, name in ((identb[:, :], "identb"), (maskA[:, :, :], "maskA"),
                              (maskB[:, :, :], "maskB"), (rank8[:, :], "rank8"), (rank16[:, :], "rank16"),
                              (wq1[:, :, :], "wq1"), (wq2[:, :, :], "wq2"), (wout[:, :, :], "wout"),
                              (bout[:, :], "bout"), (wqkv[:, :, :], "wqkv"), (wg16[:, :, :], "wg16"),
                              (wg8[:, :, :], "wg8"), (ex8[:, :, :], "ex8"), (onesr[:, :], "onesr")):
                load(dst, name, "ld_late")
            sp.wait_ge(S("y_gated"), 4)
            for name, part_of in (("ld_moe", slice(0, 3 * P)), ("ld_moe_rest", slice(3 * P, E * FD))):
                for dst, src in ((gateT, "gateT"), (upT, "upT")):
                    sp.dma_start(dst[:, :, part_of], d[src][:, :, part_of]).then_inc(S(name), 16)
            load(downT, "downT", "ld_down")
            sp.wait_ge(S("k_parts"), 6)
            for c in range(3):
                for a in range(3):
                    for k in range(2):
                        sp.dma_start(kd[16 * k:16 * k + 16, c, a, :, :], parts[:, c, k, :])\
                          .then_inc(S("k_stored"), 16)
            sp.wait_ge(S("k_stored"), 288)

            def load_k(u):
                k, b = 16 * half_of(u), batch_of(u)
                sp.dma_start(ks[u % RING][0:72, :, :],
                             kd.rearrange("h c a e t -> (c a e) h t")[:, k:k + 16, L * b:L * b + L])\
                  .then_inc(S(f"k_slot{u % RING}"), 16)

            def load_q(u):
                k, b = 16 * half_of(u), batch_of(u)
                for c in range(3):
                    sp.dma_start(qs[u % RING][24 * c:24 * c + 24, :, :],
                                 qd.rearrange("h a e t -> (a e) h t")[:, k:k + 16, L * b:L * b + L])\
                      .then_inc(S(f"q_slot{u % RING}"), 16)

            def first_k(u):
                sp.wait_ge(S("slot_zero"), u + 1)
                sp.dma_start(ks[u][P - 3:P, :, :], d["ones3"]).then_inc(S(f"k_slot{u}"), 16)
                load_k(u)

            def store_q(half, k):
                for c in range(3):
                    sp.wait_ge(S(f"q_parts{k}"), 3 * half + c + 1)
                    sp.dma_start(qd[16 * k:16 * k + 16, c, :, 512 * half:512 * half + 512],
                                 parts[:, c, k, 512 * half:512 * half + 512]).then_inc(S("q_stored"), 16)
                sp.wait_ge(S("q_stored"), 48 * (2 * half + k + 1))

            def load_m(u):
                sp.wait_ge(S("m_copied1"), u + 1)
                for c in range(3):
                    sp.dma_start(qs[u % RING][P - 3 + c:P - 2 + c, :, :], mrow[16 * c:16 * c + 16, u % 2, :])\
                      .then_inc(S(f"m_slot{u % RING}"), 16)

            first_k(0)
            store_q(0, 0)
            load_q(0)
            store_q(0, 1)
            sp.wait_ge(S("gate_up"), 4 * NF)
            first_k(1)
            load_q(1)
            sp.wait_ge(S("hid_ready"), 2 * NF)
            first_k(2)
            load_q(2)
            load_m(0)
            sp.wait_ge(S("down"), 4)
            first_k(3)
            load_q(3)
            load_m(1)
            for u in range(LAG, UNITS):
                if u + LAG < UNITS:
                    sp.wait_ge(S("lt1"), 8 * (u - LAG + 1))
                    sp.wait_ge(S("logit1"), 16 * (u - LAG + 1))
                    load_k(u + LAG)
                    if u == LAG:
                        load_m(u)
                        store_q(1, 0)
                    load_q(u + LAG)
                    if u == LAG:
                        store_q(1, 1)
                if u > LAG:
                    load_m(u)

            def store_q2(half):
                for k in range(2):
                    for c, name in enumerate(("q2_high", "q2_mid", "q2_low")):
                        sp.wait_ge(S(name), 2 * half + k + 1)
                        sp.dma_start(q2d[8 * k:8 * k + 8, c, :, 512 * half:512 * half + 512],
                                     parts[:, c, k, 512 * half:512 * half + 512]).then_inc(S("q2_stored"), 16)
                sp.wait_ge(S("q2_stored"), 96 * (half + 1))

            def load_q2(b):
                rows_of = q2d.rearrange("h a e t -> (a e) h t")[:, :, L * b:L * b + L]
                for r, n in ((0, 48), (48, 48), (96, 32)):
                    sp.dma_start(qs2[b][r:r + n, :, :], rows_of[0:n]).then_inc(S(f"q_slot{b}"), 16)
                sp.dma_start(qx2[b][0:16, :, :], rows_of[32:48]).then_inc(S(f"q_slot{b}"), 16)

            def load_m2(b):
                sp.wait_ge(S("m_copied2"), b + 1)
                for c in range(3):
                    sp.dma_start(qx2[b][16 + c:17 + c, :, :], mrow[16 * c:16 * c + 16, b % 2, :])\
                      .then_inc(S(f"m_slot{b}"), 16)

            store_q2(0)
            for b in range(2):
                sp.wait_ge(S("lt1"), 8 * (b + RING + 1))
                load_q2(b)
            load_m2(0)
            store_q2(1)
            for b in range(2, B):
                sp.wait_ge(S("lt1"), 8 * (b + RING + 1))
                load_q2(b)
            for b in range(1, B):
                load_m2(b)
            for t in range(T // 2):
                sp.wait_ge(S("fin_ready"), t + 1)
                sp.dma_start(ot[:, 2 * t:2 * t + 2, :], x[:, 2 * t:2 * t + 2, :]).then_inc(S("stored"), 16)
            sp.wait_ge(S("stored"), 16 * (T // 2))

        @block.tensor
        def _(pe):
            pe.wait_ge(S("ld_in"), 32)
            for k in range(2):
                for c in range(2):
                    m = pe.matmul(bank(2 * k + c), win[:, P * k:P * k + P], ctxT[:, 512 * c:512 * c + 512],
                                  start=True, stop=True)
            m.then_inc(S("inproj"), 1)
            pe.wait_ge(S("ld_kv"), 32)
            for n, wk in enumerate((wk1, wk2)):
                if n:
                    pe.wait_ge(S("xin_copied"), 2)
                for k in range(2):
                    for c in range(2):
                        m = pe.matmul(bank(4 - 4 * n + 2 * k + c), wk[:, P * k:P * k + P],
                                      ctxT[:, 512 * c:512 * c + 512], start=True, stop=True)
                m.then_inc(S("k_proj"), 1)
            pe.wait_ge(S("ld_small"), 16 * 12)
            pe.wait_ge(S("u_ready"), 2)
            pe.wait_ge(S("k1_out"), 2)
            for c in range(2):
                for k in range(2):
                    m = pe.matmul(psum[0:104, 4 + c, :], xproj[:, k, :], u[:, k, 512 * c:512 * c + 512],
                                  start=(k == 0), stop=(k == 1))
            m.then_inc(S("xdbl"), 1)
            pe.wait_ge(S("trig_ready"), 1)
            pe.wait_ge(S("k2_out"), 2)
            for t in range(T):
                m = pe.transpose(psum[0:8, 2 + t // 4, P * (t % 4):P * (t % 4) + P], trig[:, t, :], ident[:, :])
            m.then_inc(S("cs_turned"), 1)
            pe.wait_ge(S("dtlow"), 1)
            for k in range(2):
                for c in range(2):
                    m = pe.matmul(bank((6, 0)[k] + c), dtw[96:104, P * k:P * k + P],
                                  mid3[96:104, 512 * c:512 * c + 512], start=True, stop=True)
                m.then_inc(S("dtpre"), 1)

            def values(t0):
                for t in range(t0, t0 + 4):
                    m = pe.matmul(psum[:, 6 + t // 2 % 2, C * (t % 2):C * (t % 2) + C], ctxT[:, P * t:P * t + P],
                                  wv[:, :], start=True, stop=True)
                m.then_inc(S("v_proj"), 1)

            pe.wait_ge(S("ld_v"), 16)
            pe.wait_ge(S("dtpre_read"), 2)
            values(0)
            units = 2 * NS
            pe.wait_ge(S("split_done"), 1)
            pe.wait_ge(S("dtpre_read"), 4)

            def spread(at, row):
                for c in range(2):
                    m = pe.matmul(bank(at + c), sel[:, row, :], dsplit[:, 512 * c:512 * c + 512],
                                  start=True, stop=True)
                return m

            def add_state(i):
                pe.wait_ge(S("prod_ready"), i + 1)
                if i == 0:
                    pe.wait_ge(S("v_out"), 4)
                if i == NS:
                    pe.wait_ge(S("y_taken"), 2)
                for c in range(2):
                    m = pe.matmul(bank(6 + c), ident[:, :], prod[:, i % 2, 512 * c:512 * c + 512],
                                  start=(i % NS == 0), stop=(i % NS == NS - 1))
                m.then_inc(S("y_sum"), 1)

            def spread_b(i):
                if i >= 2:
                    pe.wait_ge(S("b_copied"), i - 1)
                spread(2 * (i % 2), i % NS).then_inc(S("b_spread"), 1)

            spread_b(0)
            pe.wait_ge(S("cs_copied"), 1)
            pe.wait_ge(S("hi_ready"), 1)
            pe.wait_ge(S("split_read"), 1)
            for i in range(2):
                for c in range(2):
                    m = pe.matmul(bank(4 - 2 * i + c), ecs[:, i, :], csT[:, 512 * c:512 * c + 512],
                                  start=True, stop=True)
                m.then_inc(S("cs_spread"), 1)
            pe.wait_ge(S("v_out"), 2)
            values(4)
            for i in range(units):
                if i >= 1:
                    pe.wait_ge(S("prod_ready"), i)
                else:
                    pe.wait_ge(S("cs_out"), 1)
                spread(4, NS + i % NS).then_inc(S("c_spread"), 1)
                if i == 0:
                    pe.wait_ge(S("cs_out"), 2)
                    spread_b(1)
                if i + 2 < units:
                    spread_b(i + 2)
                if i >= 1:
                    add_state(i - 1)
            add_state(units - 1)
            pe.wait_ge(S("b_copied"), units)
            for t in range(T):
                pe.wait_ge(S("y_gated"), 3 + t // 4)
                for k in range(2):
                    m = pe.transpose(psum[:, t // 2, C * (t % 2) + P * k:C * (t % 2) + P * k + P],
                                     yT[:, k, P * t:P * t + P], ident[:, :])
                if t % 2:
                    m.then_inc(S("y_turned"), 1)

            pe.wait_ge(S("ld_late"), 16 * 14)
            pe.wait_ge(S("x1"), 2)
            def turn_half(half, k, at, ready="xn2", turned="n2_turned"):
                for t in range(4 * half, 4 * half + 4):
                    if k == 0 and ready:
                        pe.wait_ge(S(ready), t + 1)
                    m = pe.transpose(psum[:, at, P * (t % 4):P * (t % 4) + P], xn[:, t, P * k:P * k + P], ident[:, :])
                m.then_inc(S(turned), 1)

            def router(tiles, at):
                for t in tiles:
                    for k in range(2):
                        m = pe.matmul(psum[:, at, E * (t % 4):E * (t % 4) + E], xnT[:, k, P * t:P * t + P],
                                      wg8[:, k, :], start=(k == 0), stop=(k == 1))
                m.then_inc(S("router"), 1)

            for k in range(2):
                turn_half(0, k, k, "xn1", "n1_turned")
            pe.wait_ge(S("n1_out"), 2)
            pe.wait_ge(S("ld_moe"), 32)

            def turn_weights(half):
                pe.wait_ge(S("tw_ready"), half + 1)
                for t in range(4 * half, 4 * half + 4):
                    m = pe.transpose(psum[0:96, 6, P * (t % 4):P * (t % 4) + P], tw3[:, t, :], ident[:, :])
                m.then_inc(S("tw_turned"), 1)

            def weights_of(i):
                c = i // NF
                if i == 0:
                    turn_weights(0)
                    pe.wait_ge(S("twT_ready"), 1)
                if i == NF:
                    pe.wait_ge(S("twT_ready"), 2)
                if i >= 2:
                    pe.wait_ge(S("hid_ready"), i - 1)
                pe.matmul(bank(3 * (i % 2) + 2), ex8[:, i % NF, :], twT[:, 512 * c:512 * c + 512],
                          start=True, stop=True).then_inc(S("tw_spread"), 1)

            def down(c):
                pe.wait_ge(S("hid_ready"), NF * (c + 1))
                if c:
                    pe.wait_ge(S("x2"), 2)
                if c:
                    pe.wait_ge(S("max1"), 14)
                    pe.wait_ge(S("silu_done"), 2 * NF)
                    pe.wait_ge(S("gu_done"), 2 * NF)
                for t in range(4):
                    if c and t == 1:
                        turn_m(0, 5)
                    for f in range(NF):
                        n = 6 * (t - 1) + f // 2
                        if c and f % 2 == 0 and 0 <= n < 16:
                            if n == 0:
                                ready1(1)
                            some_maxima("1", maxima1, 1, n // 2, n % 2)
                        m = pe.matmul(psum[:, 6 + t // 2, C * (t % 2):C * (t % 2) + C],
                                      hid[:, f, P * t:P * t + P], downT[:, f, :],
                                      start=(f == 0), stop=(f == NF - 1))
                    if t % 2:
                        m.then_inc(S("down"), 1)

            def some_maxima(tag, maxima, s, i, jj, at=0):
                n = 16 * s + 2 * i + jj
                if n >= 2:
                    pe.wait_ge(S("max" + tag), n - 1)
                maxima(s, i, jj, at).then_inc(S("logit" + tag), 1)

            def ready1(u):
                pe.wait_ge(S(f"k_slot{u % RING}"), 16 + 16 * (u // RING + 1))
                pe.wait_ge(S(f"q_slot{u % RING}"), 48 * (u // RING + 1))

            def maxima1(u, i, jj, at):
                qt, g = i // 4, i % 4
                for j in range(2):
                    h = 4 * g + 2 * jj + j
                    m = pe.matmul(psum[:, at + jj, 256 * j:256 * j + 256],
                                  qs[u % RING][0:P - 3, h, P * qt:P * qt + P],
                                  ks[u % RING][0:P - 3, h, :], start=True, stop=True)
                return m

            def turn_m(u, at, tag="1"):
                pe.wait_ge(S("m_parts" + tag), u + 1)
                for qt in range(2):
                    m = pe.transpose(psum[0:48, at, P * qt:P * qt + P], m3[:, u % 2, qt, :], ident[:, :])
                m.then_inc(S("m_turned" + tag), 1)

            def q_half(half, n, k, at):
                for kk in range(2):
                    m = pe.matmul(bank(at), (wq1, wq2)[n][:, kk, P * k:P * k + P],
                                  xnT[:, kk, 512 * half:512 * half + 512], start=(kk == 0), stop=(kk == 1))
                m.then_inc(S("q_proj"), 1)

            def unit0_maxima(n, at=6):
                if n == 0:
                    ready1(0)
                    pe.wait_ge(S("q_out"), 4)
                some_maxima("1", maxima1, 0, n // 2, n % 2, at)

            for i in range(2 * NF):
                c, f = i // NF, i % NF
                if i == 1:
                    pe.wait_ge(S("x1"), 4)
                    for k in range(2):
                        turn_half(1, k, 2 + k, "xn1", "n1_turned")
                    pe.wait_ge(S("n1_out"), 4)
                if i >= 2:
                    pe.wait_ge(S("silu_done"), i - 1)
                    pe.wait_ge(S("gu_done"), i - 1)
                if i == 3:
                    pe.wait_ge(S("ld_moe_rest"), 32)
                for n, wt in enumerate((gateT, upT)):
                    for k in range(2):
                        m = pe.matmul(bank(3 * (i % 2) + n), wt[:, k, P * f:P * f + P],
                                      xnT[:, k, 512 * c:512 * c + 512], start=(k == 0), stop=(k == 1))
                    m.then_inc(S("gate_up"), 1)
                    if n == 0 and i >= MAX0 + 1:
                        for nn in (4 * (i - MAX0) - 2, 4 * (i - MAX0) - 1):
                            unit0_maxima(nn)
                if i == 0:
                    router(range(4), 5)
                if i == 2:
                    weights_of(0)
                if i >= 2:
                    weights_of(i - 1)
                if 1 <= i <= 4:
                    router([3 + i], 7)
                if i == 9:
                    turn_weights(1)
                if i == NF:
                    pe.wait_ge(S("ld_down"), 16)
                    down(0)
                if i == TURN0:
                    for k in range(2):
                        turn_half(0, k, 6 + k)
                if i in (TURN0 + 1, TURN0 + 2):
                    k = i - TURN0 - 1
                    pe.wait_ge(S("n2_out"), 2)
                    if k:
                        pe.wait_ge(S("q_out"), 2)
                    for n in range(2):
                        q_half(0, n, k, 6 + n)
                if i >= MAX0:
                    for nn in (4 * (i - MAX0), 4 * (i - MAX0) + 1):
                        unit0_maxima(nn)
            weights_of(2 * NF - 1)
            pe.wait_ge(S("silu_done"), 2 * NF - 1)
            pe.wait_ge(S("gu_done"), 2 * NF - 1)
            for nn in (14, 15):
                unit0_maxima(nn, 0)
            down(1)

            def attention(tag, units, first, slots_ready, maxima, probs, values, side):

                for s in range(first, units + LAG + 1):
                    for i in range(8):
                        if s < units:
                            if i == 0:
                                slots_ready(s)
                            some_maxima(tag, maxima, s, i, 0)
                        if i == 1 and 1 <= s <= units:
                            if s > LAG + 1:
                                pe.wait_ge(S("o_norm" + tag), 2 * (s - LAG - 1))
                            if tag == "1" and s == LAG + 1:
                                pe.wait_ge(S("q_out"), 8)
                            if tag == "1" and s == LAG:
                                pe.wait_ge(S("x2"), 4)
                            turn_m(s - 1, 7, tag)
                        u = s - LAG
                        if 0 <= u < units:
                            n = 8 * u + i
                            if i == 0:
                                pe.wait_ge(S(f"m_slot{u % RING}"), m_loaded(tag, u))
                            if n >= 2:
                                pe.wait_ge(S("prob" + tag), n - 1)
                            probs(u, i // 2, i % 2, 2 + 2 * (i % 2)).then_inc(S("lt" + tag), 1)
                        if s < units:
                            some_maxima(tag, maxima, s, i, 1)
                        if i % 2 == 0:
                            G = 4 * u + i // 2 - 1
                            if 0 <= G < 4 * units:
                                pe.wait_ge(S("prob" + tag), 2 * G + 2)
                                if G:
                                    pe.wait_ge(S("o_copied" + tag), G)
                                for kt in range(2):
                                    q0 = P * kt if tag == "2" else 0
                                    for j in range(4):
                                        m = pe.matmul(psum[32 * j:32 * j + 32, 6, q0:256], values(G, kt, j),
                                                      Pb[2 * (G % 2) + kt][:, (256 - q0) * j:(256 - q0) * (j + 1)],
                                                      start=(kt == 0), stop=(kt == 1), skip_group_check=True,
                                                      tile_position=(0, 32 * j))
                                m.then_inc(S("o_sum" + tag), 1)
                        if i in (2, 4) and 0 <= u - 1 < units:
                            qt = i // 2 - 1
                            pe.wait_ge(S("o_copied" + tag), 4 * u)
                            pe.wait_ge(S("m_copied" + tag), min(s, units))
                            if qt or u >= 2:
                                pe.wait_ge(S("o_norm" + tag), 2 * (u - 1) + qt)
                            for g in range(4):
                                m = pe.transpose(psum[:, 7, P * g:P * g + P],
                                                 osb[:, (u - 1) % 2, 256 * g + P * qt:256 * g + P * qt + P],
                                                 ident[:, :])
                            m.then_inc(S("o_turned" + tag), 1)
                        if side:
                            side(s, i)

            def project(half, c, at):
                for t in range(4 * half + 2 * c, 4 * half + 2 * c + 2):
                    dst = psum[:, at, C * (t % 2):C * (t % 2) + C]
                    for k in range(2):
                        pe.matmul(dst, xnT[:, k, P * t:P * t + P], wout[:, k, :], start=(k == 0), stop=False)
                    m = pe.matmul(dst, onesr[:, :], bout[:, :], start=False, stop=True)
                m.then_inc(S("proj1"), 1)

            def gate_logits(half, at):
                for t in range(4 * half, 4 * half + 4):
                    for k in range(2):
                        m = pe.matmul(psum[:, at, H2 * (t % 4):H2 * (t % 4) + H2], xnT[:, k, P * t:P * t + P],
                                      wg16[:, k, :], start=(k == 0), stop=(k == 1))
                m.then_inc(S("gate_logit"), 1)

            def q2_half(half, k, at):
                for kk in range(2):
                    m = pe.matmul(bank(at), wqkv[:, kk, P * k:P * k + P], xnT[:, kk, 512 * half:512 * half + 512],
                                  start=(kk == 0), stop=(kk == 1))
                m.then_inc(S("q2_proj"), 1)

            def keys_values(t, at):
                for kk in range(2):
                    m = pe.matmul(bank(at), xnT[:, kk, P * t:P * t + P], wqkv[:, kk, C:3 * C],
                                  start=(kk == 0), stop=(kk == 1))
                m.then_inc(S("kv_proj"), 1)

            def turn_keys(half, at):
                pe.wait_ge(S("kt_ready"), half + 1)
                for t in range(4):
                    pe.transpose(psum[:, at, P * t:P * t + P], kt[half][:, t, 0:P], ident[:, :])
                    m = pe.transpose(psum[0:19, at + 1, P * t:P * t + P], kt[half][:, t, P:P + 19], ident[:, :])
                m.then_inc(S("ks_turned"), 1)

            def side1(s, i):
                j = 8 * (s - UNITS) + i
                if j in (-3, -2):
                    if j == -3:
                        pe.wait_ge(S("o_norm1"), 2 * (UNITS - 3))
                    else:
                        pe.wait_ge(S("a_out0"), 1)
                    turn_half(0, j + 3, 7, None, "a_turned")
                if j == 0:
                    pe.wait_ge(S("max1"), 16 * UNITS)
                    pe.wait_ge(S("a_out0"), 2)
                    for c in range(2):
                        project(0, c, c)
                if j == 6:
                    pe.wait_ge(S("x3"), 2)
                    for k in range(2):
                        turn_half(0, k, k, "xn3", "n3_turned")
                if j == 7:
                    pe.wait_ge(S("n3_out0"), 2)
                    gate_logits(0, 1)
                    q2_half(0, 0, 0)
                if j == 8:
                    pe.wait_ge(S("gl_read"), 1)
                    q2_half(0, 1, 1)
                if 9 <= j < 13:
                    t = j - 9
                    if t < 2:
                        pe.wait_ge(S("q2_read"), t + 1)
                    else:
                        pe.wait_ge(S("kv_read"), t - 1)
                    keys_values(t, t % 2)
                job = 8 * (s - LAG) + i - 2
                if 0 <= job < 6:
                    if job == 0:
                        pe.wait_ge(S("m_copied1"), 2)
                    if job == 1:
                        pe.wait_ge(S("n2_out"), 3)
                    if job == 2:
                        pe.wait_ge(S("n2_out"), 4)
                    if job > 2:
                        pe.wait_ge(S("q_out"), 4 + job - 2)
                    if job < 2:
                        turn_half(1, job, 7)
                    else:
                        q_half(1, job % 2, (job - 2) // 2, 7)

            def probs1(u, g, kt, at):
                for j in range(4):
                    m = pe.matmul(psum[:, at + j // 2, 256 * (j % 2):256 * (j % 2) + 256],
                                  ks[u % RING][:, 4 * g + j, P * kt:P * kt + P],
                                  qs[u % RING][:, 4 * g + j, :], start=True, stop=True)
                return m

            attention("1", UNITS, LAG, ready1, maxima1, probs1,
                      lambda G, kt, j: vaug[:, 2 * batch_of(G // 4) + kt, 16 * half_of(G // 4) + 4 * (G % 4) + j, :],
                      side1)
            pe.wait_ge(S("kv_read"), 4)
            turn_keys(0, 0)
            pe.wait_ge(S("o_norm1"), 2 * UNITS)
            pe.wait_ge(S("prob1"), 8 * UNITS)
            for k in range(2):
                turn_half(1, k, 2 + k, None, "a_turned")

            def side2(s, i):
                j = 8 * s + i
                if j == 1:
                    pe.wait_ge(S("a_out1"), 2)
                    for c in range(2):
                        project(1, c, 2 + c)
                if j == 6:
                    for k in range(2):
                        turn_half(1, k, 4 + k, "xn3", "n3_turned")
                if j == 7:
                    pe.wait_ge(S("n3_out1"), 2)
                    pe.wait_ge(S("x3"), 4)
                    gate_logits(1, 2)
                    q2_half(1, 0, 3)
                if j == 8:
                    q2_half(1, 1, 4)
                if 9 <= j < 13:
                    t = j - 5
                    if t == 5:
                        pe.wait_ge(S("gl_read"), 2)
                    if t > 5:
                        pe.wait_ge(S("kv_read"), t - 1)
                    keys_values(t, 5 - 3 * (t % 2))
                if j == 14:
                    pe.wait_ge(S("q2_read"), 4)
                    turn_keys(1, 3)
                if j == 15:
                    pe.wait_ge(S("ks_out"), 4)
                    pe.wait_ge(S("kv_read"), T)

            def ready2(b):
                pe.wait_ge(S("ks_out"), 2 * (b // 2) + 2)
                pe.wait_ge(S(f"q_slot{b}"), 48 * (UNITS // RING) + 64)

            def maxima2(b, i, jj, at):
                qt, g = i // 4, i % 4
                n = P * (qt + 1)
                o = psum[:, jj, 0:2 * n]
                for j in range(2):
                    h = 4 * g + 2 * jj + j
                    pe.matmul(o[:, n * j:n * j + n], qs2[b][:, h, P * qt:P * qt + P],
                              ks2[:, L * b:L * b + n], start=(j == 0), stop=False, skip_group_check=True)
                m = pe.matmul(o.rearrange("p (j k) -> p j k", j=2)[:, :, n - P:n], identb[:, :], maskA[:, :, P:2 * P],
                              start=False, stop=True, skip_group_check=True)
                return m

            def probs2(b, g, kt, at):
                q0 = P * kt
                n = 256 - q0
                for jj in range(2):
                    h = 4 * g + 2 * jj
                    o = psum[:, at + jj, 0:2 * n]
                    pe.matmul(o, ks2[:, L * b + q0:L * b + q0 + P], qs2[b][:, h:h + 2, q0:256],
                              start=True, stop=False, skip_group_check=True)
                    pe.matmul(o, kx2[:, L * b + q0:L * b + q0 + P], qx2[b][:, h:h + 2, q0:256],
                              start=False, stop=False, skip_group_check=True)
                    m = pe.matmul(o.rearrange("p (j k) -> p j k", j=2)[:, :, 0:P], identb[:, :], maskB[:, :, 0:P],
                                  start=False, stop=True, skip_group_check=True)
                return m

            attention("2", B, 0, ready2, maxima2, probs2, lambda G, kt, j: va2[:, 2 * (G // 4) + kt, :], side2)

        def rotate(eng, step, half, k):
            hs = slice(512 * half, 512 * half + 512)
            q, p2, n = qr[:, k, hs], tmpq_of[half][:, k, :], 4 * half

            def done(ins, c):
                ins.then_inc(S(f"q_parts{k}"), 1)
                eng.wait_ge(S(f"q_parts{k}"), 3 * half + c + 1)

            eng.wait_ge(S("k_stored"), 288)
            eng.wait_ge(S("q_out"), 4 * half + 2 * k + 2)
            step(eng.tensor_tensor(q, q, cosT[:, hs], ALU.mult))
            step(eng.tensor_tensor(p2, p2, sinT[:, hs], ALU.mult))
            step(eng.tensor_tensor(q, q, p2, ALU.add))
            done(eng.tensor_copy(parts[:, 0, k, hs], q), 0)
            step(eng.tensor_tensor(q, q, parts[:, 0, k, hs], ALU.subtract))
            done(eng.tensor_copy(parts[:, 1, k, hs], q), 1)
            eng.tensor_tensor(parts[:, 2, k, hs], q, parts[:, 1, k, hs], ALU.subtract)\
                .then_inc(S(f"q_parts{k}"), 1)

        @block.scalar
        def _(act):
            chain = [0]

            def link(ins):
                chain[0] += 1
                ins.then_inc(S("act_chain"), 1)
                act.wait_ge(S("act_chain"), chain[0])

            def rstd_all():
                act.wait_ge(S("mv0"), 1)
                link(act.activation(lnv[:, :], mv[:, :, 1], ACT.Ln, bias=consts[:, 0:1]))
                act.activation(rstd[:, :], lnv[:, :], ACT.Exp, scale=-0.5).then_inc(S("rstd0"), 1)

            def rstd_half(half, n=2):
                hs = slice(4 * half, 4 * half + 4)
                act.wait_ge(S(f"mv{n}"), half + 1)
                link(act.activation(lnv[:, hs], mv[:, hs, 1], ACT.Ln, bias=consts[:, 0:1]))
                act.activation(rstd[:, hs], lnv[:, hs], ACT.Exp, scale=-0.5).then_inc(S(f"rstd{n}"), 1)

            def turned_out(half, k, at):
                act.wait_ge(S("n2_turned"), 2 * half + k + 1)
                act.activation(xnT[:, k, 512 * half:512 * half + 512], bank(at), ACT.Copy).then_inc(S("n2_out"), 1)

            def q_out(half, n, k, at):
                act.wait_ge(S("q_proj"), 4 * half + 2 * k + n + 1)
                if half == n == k == 0:
                    act.wait_ge(S("k_parts"), 6)
                dst = tmpq_of[half][:, k, :] if n else qr[:, k, 512 * half:512 * half + 512]
                act.activation(dst, bank(at), ACT.Copy).then_inc(S("q_out"), 1)

            def m_out(u, tag, at):
                act.wait_ge(S("m_turned" + tag), u + 1)
                if u >= 2:
                    act.wait_ge(S(f"m_slot{(u - 2) % RING}"), m_loaded(tag, u - 2))
                act.activation(mrow[:, u % 2, :], psum[0:48, at, 0:256], ACT.Copy).then_inc(S("m_copied" + tag), 1)

            act.wait_ge(S("inproj"), 1)
            act.wait_ge(S("xin_zero"), 1)
            for k in range(2):
                act.activation(xp[:, k, :, 3:3 + L], bank(2 * k, 2).rearrange("p (b l) -> p b l", b=B),
                               ACT.Copy).then_inc(S("xin_copied"), 1)
            act.wait_ge(S("ld_small"), 16 * 12)
            act.activation(tg[:, :], gates[:, :], ACT.Tanh).then_inc(S("tg"), 1)
            rstd_all()
            act.activation(negA, negA, ACT.Exp).then_inc(S("expA"), 1)
            act.wait_ge(S("k_proj"), 1)
            for k in range(2):
                act.activation(k1T[:, k, :], bank(4 + 2 * k, 2), ACT.Copy).then_inc(S("k1_out"), 1)
            for k in range(2):
                act.wait_ge(S("conv_done"), k + 1)
                act.activation(u[:, k, :], conv[:, k, :], ACT.Silu, bias=convb[:, k:k + 1]).then_inc(S("u_ready"), 1)
            act.wait_ge(S("xn0"), T)
            for k in range(2):
                act.activation(zg[:, k, :].rearrange("p (b l) -> p b l", b=B), xn[:, k:T:2, :], ACT.Silu)\
                   .then_inc(S("z_out"), 1)
            act.wait_ge(S("ang_ready"), 1)
            act.activation(trig, ang, ACT.Sin).then_inc(S("trig_ready"), 1)
            act.wait_ge(S("xdbl"), 1)
            act.activation(mid3[96:104, :], psum[96:104, 4:6, :].rearrange("p a b -> p (a b)"), ACT.Copy)\
               .then_inc(S("dtlow"), 1)
            act.activation(hib, psum[0:96, 4:6, :].rearrange("p a b -> p (a b)"), ACT.Copy).then_inc(S("hi_ready"), 1)
            for k in range(2):
                act.wait_ge(S("dtpre"), k + 1)
                act.activation(absx[k], bank((6, 0)[k], 2), ACT.Abs, bias=dtb[:, k:k + 1])\
                   .then_inc(S("dtpre_read"), 1)
                act.activation(dt[:, k, :], bank((6, 0)[k], 2), ACT.Relu, bias=dtb[:, k:k + 1])\
                   .then_inc(S("dtpre_read"), 1)
            act.wait_ge(S("dtpre_read"), 3)
            for k in range(2):
                act.activation(expx[k], absx[k], ACT.Exp, scale=-1.0).then_inc(S("exp_ready"), 1)
            act.wait_ge(S("cs_turned"), 1)
            act.activation(csT, psum[0:8, 2:4, :].rearrange("p a b -> p (a b)"), ACT.Copy).then_inc(S("cs_copied"), 1)
            for k in range(2):
                act.wait_ge(S("exp_ready"), k + 1)
                act.activation(w[:, k, :], expx[k], ACT.Ln, bias=consts[:, 1:2]).then_inc(S("ln_ready"), 1)

            def values_out(half):
                act.wait_ge(S("v_proj"), half + 1)
                act.wait_ge(S("vaug_ones"), 1)
                for n in range(2):
                    t = 4 * half + 2 * n
                    act.activation(vaug[:, t:t + 2, :, 0:D1],
                                   bank(6 + n).rearrange("p (t h e) -> p t h e", t=2, h=H1), ACT.Copy)\
                       .then_inc(S("v_out"), 1)

            values_out(0)

            def cos_sin_out(i):
                act.wait_ge(S("cs_spread"), i + 1)
                act.activation((cosT, sinT)[i][:, :], bank(4 - 2 * i, 2), ACT.Copy).then_inc(S("cs_out"), 1)

            for i in range(2 * NS):
                k, n = i // NS, i % NS
                act.wait_ge(S("b_spread"), i + 1)
                if i >= 2:
                    act.wait_ge(S("dBu_ready"), i - 1)
                act.activation(b_rows(i), bank(2 * (i % 2), 2), ACT.Copy).then_inc(S("b_copied"), 1)
                if i == 0:
                    cos_sin_out(0)
                if n == 0:
                    act.wait_ge(S("w_ready"), k + 1)
                if i == 0:
                    act.wait_ge(S("negA"), 1)
                    act.wait_ge(S("dA_zero"), 1)
                if i >= 2:
                    act.wait_ge(S("scanned"), i - 1)
                act.activation(dA[i % 2].rearrange("p (b l) -> p b l", b=B)[:, :, 1:L],
                               dt[:, k, :].rearrange("p (b l) -> p b l", b=B)[:, :, 1:L], ACT.Exp,
                               scale=negA[:, k, n:n + 1]).then_inc(S("dA_ready"), 1)
                if i == 0:
                    cos_sin_out(1)
                    values_out(1)
            def n1_out(half, k, at):
                act.wait_ge(S("n1_turned"), 2 * half + k + 1)
                act.activation(xnT[:, k, 512 * half:512 * half + 512], bank(at), ACT.Copy).then_inc(S("n1_out"), 1)

            def second_weight(half):
                act.wait_ge(S("m_diff"), half + 1)
                hs = slice(4 * half, 4 * half + 4)
                act.activation(w1[:, hs], w2[:, hs], ACT.Exp).then_inc(S("e2"), 1)

            rstd_half(0, 1)
            for k in range(2):
                n1_out(0, k, k)
            rstd_half(1, 1)
            for i in range(2 * NF):
                act.wait_ge(S("gate_up"), 2 * i + 1)
                if i >= 2:
                    act.wait_ge(S("gu_done"), i - 1)
                act.activation(sg[:, i % 2, :], bank(3 * (i % 2)), ACT.Silu).then_inc(S("silu_done"), 1)
                if i == 0:
                    for k in range(2):
                        n1_out(1, k, 2 + k)
                    second_weight(0)
                if i == 6:
                    second_weight(1)
                if i == NF + 1:
                    rstd_half(0)
                if i == TURN0:
                    for k in range(2):
                        turned_out(0, k, 6 + k)
                if i in (TURN0 + 1, TURN0 + 2):
                    for n in range(2):
                        q_out(0, n, i - TURN0 - 1, 6 + n)
            m_out(0, "1", 5)
            rstd_half(1)

            def attention(tag, units, first, scale, side):
                for s in range(first, units + LAG + 1):
                    u = s - LAG
                    for i in range(8):
                        if i == 1 and 1 <= s <= units:
                            m_out(s - 1, tag, 7)
                        if 0 <= u < units:
                            n, g, kt = 8 * u + i, 4 * u + i // 2, i % 2
                            act.wait_ge(S("lt" + tag), n + 1)
                            if g >= 2:
                                act.wait_ge(S("o_sum" + tag), g - 1)
                            w2n = 512 - 256 * kt if tag == "2" else 512
                            act.activation(Pb[2 * (g % 2) + kt][:, 0:2 * w2n].rearrange("p (a b) -> p a b", a=2),
                                           psum[:, 2 + 2 * kt:4 + 2 * kt, 0:w2n], ACT.Exp, scale=scale)\
                               .then_inc(S("prob" + tag), 1)
                        G = 4 * u + i // 2 - 1
                        if i % 2 == 0 and 0 <= G < 4 * units:
                            act.wait_ge(S("o_sum" + tag), G + 1)
                            if G >= 8 and G % 4 == 0:
                                act.wait_ge(S("o_turned" + tag), 2 * (G // 4 - 1))
                            act.activation(osb[:, G // 4 % 2, 256 * (G % 4):256 * (G % 4) + 256], psum[:, 6, 0:256],
                                           ACT.Copy).then_inc(S("o_copied" + tag), 1)
                        side(s, i)

            def side1(s, i):
                job = 8 * (s - LAG) + i - 2
                if 0 <= job < 2:
                    turned_out(1, job, 7)
                if 2 <= job < 6:
                    q_out(1, job % 2, (job - 2) // 2, 7)
                j = 8 * (s - UNITS) + i
                if j == 4:
                    rstd_half(0, 3)
                if j == 8:
                    gate_exp(0)

            def gate_exp(half):
                act.wait_ge(S("gdiff"), half + 1)
                hs = slice(4 * half, 4 * half + 4)
                act.activation(gt[:, hs, :], gt[:, hs, :], ACT.Exp).then_inc(S("gexp"), 1)

            def keys_out(half, at):
                act.wait_ge(S("ks_turned"), half + 1)
                hs = slice(512 * half, 512 * half + 512)
                act.activation(ks2[:, hs], bank(at), ACT.Copy).then_inc(S("ks_out"), 1)
                act.activation(kx2[:, hs], psum[0:19, at + 1, :], ACT.Copy).then_inc(S("ks_out"), 1)

            def half_out(turned, at, done):
                for k in range(2):
                    act.wait_ge(S(turned), k + 3)
                    act.activation(xnT[:, k, 512:1024], bank(at + k), ACT.Copy).then_inc(S(done), 1)

            def side2(s, i):
                j = 8 * s + i
                if j == 4:
                    rstd_half(1, 3)
                if j == 6:
                    half_out("n3_turned", 4, "n3_out1")
                if j in (7, 8):
                    k = j - 7
                    act.wait_ge(S("q2_proj"), k + 3)
                    act.activation(parts[:, 0, k, 512:1024], bank(3 + k), ACT.Copy).then_inc(S("q2_high"), 1)
                if j == 8:
                    gate_exp(1)
                if j == 14:
                    keys_out(1, 3)

            attention("1", UNITS, LAG, float(D1) ** -0.5, side1)
            keys_out(0, 0)
            half_out("a_turned", 2, "a_out1")
            attention("2", B, 0, float(D2) ** -0.5, side2)

        @block.gpsimd
        def _(pool):
            chain = [0]

            def link(ins):
                chain[0] += 1
                ins.then_inc(S("pool_chain"), 1)
                pool.wait_ge(S("pool_chain"), chain[0])

            pool.memset(vaug[:, :, :, :], 1.0).then_inc(S("vaug_ones"), 1)
            pool.memset(tw3[:, :, :], 0.0).then_inc(S("tw3_zero"), 1)
            e, s = expx[1], absx[1]
            pool.wait_ge(S("exp_ready"), 2)
            link(pool.tensor_scalar(s, e, 0.2, -0.25, ALU.mult, ALU.add))
            link(pool.tensor_tensor(s, s, e, ALU.mult))
            link(pool.tensor_scalar(s, s, 1.0, 1.0 / 3.0, ALU.mult, ALU.add))
            link(pool.tensor_tensor(s, s, e, ALU.mult))
            link(pool.tensor_scalar(s, s, 1.0, -0.5, ALU.mult, ALU.add))
            pool.tensor_tensor(s, s, e, ALU.mult).then_inc(S("series"), 1)
            for i in range(2 * NS):
                k = i // NS
                if i % NS == 0:
                    pool.wait_ge(S("w_ready"), k + 1)
                pool.wait_ge(S("b_copied"), i + 1)
                if i >= 2:
                    pool.wait_ge(S("scanned"), i - 1)
                pool.tensor_tensor(dBu[:, i % 2, :], w[:, k, :], b_rows(i), ALU.mult).then_inc(S("dBu_ready"), 1)
            pool.wait_ge(S("k1_out"), 2)
            pool.wait_ge(S("k2_out"), 2)
            pool.wait_ge(S("cs_out"), 2)
            for k in range(2):
                link(pool.tensor_tensor(k1T[:, k, :], k1T[:, k, :], cosT[:, :], ALU.mult))
                link(pool.tensor_tensor(k2T[:, k, :], k2T[:, k, :], sinT[:, :], ALU.mult))
            for k in range(2):
                link(pool.tensor_tensor(k1T[:, k, :], k1T[:, k, :], k2T[:, k, :], ALU.add))
                pool.tensor_copy(parts[:, 0, k, :], k1T[:, k, :]).then_inc(S("k_parts"), 1)
                pool.wait_ge(S("k_parts"), 3 * k + 1)
                link(pool.tensor_tensor(k1T[:, k, :], k1T[:, k, :], parts[:, 0, k, :], ALU.subtract))
                pool.tensor_copy(parts[:, 1, k, :], k1T[:, k, :]).then_inc(S("k_parts"), 1)
                pool.wait_ge(S("k_parts"), 3 * k + 2)
                pool.tensor_tensor(parts[:, 2, k, :], k1T[:, k, :], parts[:, 1, k, :], ALU.subtract)\
                    .then_inc(S("k_parts"), 1)

            def maxima_parts(tag, first, last):
                for u in range(first, last):
                    pool.wait_ge(S("max" + tag), 16 * (u + 1))
                    if u >= 2:
                        pool.wait_ge(S("m_turned" + tag), u - 1)
                    o = m3[:, u % 2, :, :]

                    link(pool.tensor_scalar(mr[:, :, :], mx[:, u % 2, :, :], -1.0, 0.0, ALU.mult, ALU.add))
                    link(pool.tensor_copy(mb[:, :, :], mr[:, :, :]))
                    pool.tensor_copy(o[:, :, 0:16], mb[:, :, :])
                    link(pool.tensor_tensor(mr[:, :, :], mr[:, :, :], mb[:, :, :], ALU.subtract))
                    link(pool.tensor_copy(mb[:, :, :], mr[:, :, :]))
                    pool.tensor_copy(o[:, :, 16:32], mb[:, :, :])
                    pool.tensor_tensor(o[:, :, 32:48], mr[:, :, :], mb[:, :, :], ALU.subtract)\
                        .then_inc(S("m_parts" + tag), 1)
                    pool.wait_ge(S("m_parts" + tag), u + 1)

            def zero_slot(n):
                pool.memset(area[64:P, slot_at[n]:slot_at[n] + PAIR], 0.0).then_inc(S("slot_zero"), 1)
                pool.wait_ge(S("slot_zero"), n + 1)

            pool.wait_ge(S("y_gated"), 4)
            pool.wait_ge(S("k_parts"), 6)
            zero_slot(0)
            rotate(pool, link, 0, 1)
            pool.wait_ge(S("q_parts1"), 3)
            pool.wait_ge(S("gate_up"), 4 * NF)
            zero_slot(1)
            pool.wait_ge(S("hid_ready"), 2 * NF)
            zero_slot(2)
            maxima_parts("1", 0, 2)
            pool.wait_ge(S("rstd2"), 2)
            for t in range(4, 8):
                pool.tensor_scalar(xn[:, t, :], x[:, t, :], mv[:, t, 0:1], rstd[:, t:t + 1],
                                   ALU.subtract, ALU.mult).then_inc(S("xn2"), 1)
            pool.wait_ge(S("xn2"), T)
            zero_slot(3)
            maxima_parts("1", 2, 3)
            rotate(pool, link, 1, 1)
            maxima_parts("1", 3, UNITS)

            def q2_parts(half, k):
                hs = slice(512 * half, 512 * half + 512)
                pool.wait_ge(S("q2_read"), 2 * half + k + 1)
                pool.tensor_copy(parts[:, 1, k, hs], qr[:, k, hs]).then_inc(S("q2_mid"), 1)
                pool.wait_ge(S("q2_mid"), 2 * half + k + 1)
                pool.tensor_tensor(parts[:, 2, k, hs], qr[:, k, hs], parts[:, 1, k, hs], ALU.subtract)\
                    .then_inc(S("q2_low"), 1)

            for k in range(2):
                q2_parts(0, k)
            maxima_parts("2", 0, 1)
            for k in range(2):
                q2_parts(1, k)
            maxima_parts("2", 1, B)

        @block.vector
        def _(v):
            chain = [0]

            def link(ins):
                chain[0] += 1
                ins.then_inc(S("dve_chain"), 1)
                v.wait_ge(S("dve_chain"), chain[0])

            def norm_stats():
                for t in range(T):
                    last = v.bn_stats(stats[:, t, :], x[:, t, :])
                link(last)
                for t in range(T):
                    last = v.bn_aggr(mv[:, t, :], stats[:, t, :])
                last.then_inc(S("mv0"), 1)

            def norm_apply():
                v.wait_ge(S("rstd0"), 1)
                for t in range(T):
                    v.tensor_scalar(xn[:, t, :], x[:, t, :], mv[:, t, 0:1], rstd[:, t:t + 1],
                                    ALU.subtract, ALU.mult).then_inc(S("xn0"), 1)

            v.memset(xp[:, :, :, 0:3], 0.0).then_inc(S("xin_zero"), 1)
            v.wait_ge(S("ld_pos"), 16)
            a4 = ang.rearrange("p t (s a i) -> p t s a i", s=2, a=2)
            for s in range(2):
                for i in range(2):
                    last = v.tensor_scalar(a4[:, :, s, :, i], pos, 10000.0 ** (-i / 2), None, ALU.mult)
            link(last)
            for s in range(2):
                c8 = slice(4 * s, 4 * s + 4)
                last = v.tensor_scalar(rnd[:, :, c8], ang[:, :, c8], 1.0 / 6.283185307179586,
                                       0.25 if s == 0 else 0.0, ALU.mult, ALU.add)
            link(last)
            link(v.tensor_scalar(rnd, rnd, ROUND, None, ALU.add))
            link(v.tensor_scalar(rnd, rnd, ROUND, None, ALU.subtract))
            link(v.scalar_tensor_tensor(ang, rnd, -TWO_PI_HI, ang, ALU.mult, ALU.add))
            link(v.scalar_tensor_tensor(ang, rnd, -TWO_PI_LO, ang, ALU.mult, ALU.add))
            link(v.tensor_scalar(ang[:, :, 0:4], ang[:, :, 0:4], 1.5707963267948966, None, ALU.add))
            v.tensor_scalar(ang, ang, PI_IN, -PI_IN, ALU.min, ALU.max).then_inc(S("ang_ready"), 1)
            v.wait_ge(S("ld_x"), 16)
            norm_stats()
            v.wait_ge(S("ld_small"), 16 * 12)
            for k in range(2):
                v.wait_ge(S("xin_copied"), k + 1)
                cv = conv[:, k, :].rearrange("p (b l) -> p b l", b=B)
                link(v.tensor_scalar(cv, xp[:, k, :, 0:L], convw[:, k, 0:1], None, ALU.mult))
                for j in range(1, KCONV):
                    m = v.scalar_tensor_tensor(cv, xp[:, k, :, j:j + L], convw[:, k, j:j + 1], cv,
                                               ALU.mult, ALU.add)
                    if j < KCONV - 1:
                        link(m)
                m.then_inc(S("conv_done"), 1)
            v.wait_ge(S("k_proj"), 2)
            for k in range(2):
                v.tensor_copy(k2T[:, k, :], bank(2 * k, 2)).then_inc(S("k2_out"), 1)
            norm_apply()
            v.wait_ge(S("expA"), 1)
            v.tensor_scalar(negA, negA, -1.0, None, ALU.mult).then_inc(S("negA"), 1)
            v.wait_ge(S("hi_ready"), 1)
            xd = psum[0:96, 4:6, :].rearrange("p a b -> p (a b)")
            rest = mid3[0:96, :]
            v.tensor_tensor(rest, xd, hib, ALU.subtract).then_inc(S("split_read"), 1)
            v.wait_ge(S("split_read"), 1)
            link(v.tensor_copy(midb, rest))
            link(v.tensor_tensor(rest, rest, midb, ALU.subtract))
            link(v.tensor_copy(lob, rest))
            v.tensor_copy(dsplit[0:32, :], hib[0:32, :])
            v.tensor_copy(dsplit[32:64, :], midb[32:64, :])
            v.tensor_copy(dsplit[64:96, :], lob[64:96, :]).then_inc(S("split_done"), 1)
            def softplus(k, n):
                e, s, small = expx[k], absx[k], (prod[:, 0, :] if k == 0 else second[:, 2, :]).bitcast(I32)
                if n < 4 and k:
                    return
                if n == 0:
                    v.wait_ge(S("exp_ready"), k + 1)
                    link(v.tensor_scalar(s, e, 0.2, -0.25, ALU.mult, ALU.add))
                if n == 1:
                    link(v.tensor_tensor(s, s, e, ALU.mult))
                if n == 2:
                    link(v.scalar_tensor_tensor(s, s, 1.0 / 3.0, e, ALU.add, ALU.mult))
                if n == 3:
                    link(v.scalar_tensor_tensor(s, s, -0.5, e, ALU.add, ALU.mult))
                if n == 4:
                    if k:
                        v.wait_ge(S("series"), 1)
                    link(v.scalar_tensor_tensor(s, s, 1.0, e, ALU.add, ALU.mult))
                    if k == 0:
                        v.wait_ge(S("z_out"), 2)
                    link(v.tensor_scalar(small, e, SMALL, None, ALU.is_lt))
                if n == 5:
                    v.wait_ge(S("ln_ready"), k + 1)
                    link(v.copy_predicated(w[:, k, :], small, s))
                if n == 6:
                    link(v.tensor_tensor(dt[:, k, :], dt[:, k, :], w[:, k, :], ALU.add))
                if n == 7:
                    v.tensor_tensor(w[:, k, :], dt[:, k, :], u[:, k, :], ALU.mult).then_inc(S("w_ready"), 1)

            for n in range(8):
                softplus(0, n)
            for i in range(2):
                last = v.memset(dA[i].rearrange("p (b l) -> p b l", b=B)[:, :, 0:1], 0.0)
            last.then_inc(S("dA_zero"), 1)

            def take_y(k):
                v.wait_ge(S("y_sum"), NS * (k + 1))
                for c in range(2):
                    cs = slice(512 * c, 512 * c + 512)
                    v.scalar_tensor_tensor(yT[:, k, cs], u[:, k, cs], Dp[:, k:k + 1], bank(6 + c),
                                           ALU.mult, ALU.add).then_inc(S("y_taken"), 1)
                    v.wait_ge(S("y_taken"), 2 * k + c + 1)
                    v.tensor_tensor(yT[:, k, cs], yT[:, k, cs], zg[:, k, cs], ALU.mult).then_inc(S("y_gated"), 1)

            for i in range(2 * NS):
                v.wait_ge(S("dA_ready"), i + 1)
                v.wait_ge(S("dBu_ready"), i + 1)
                v.tensor_tensor_scan(hst[:, i % 2, :], dA[i % 2], dBu[:, i % 2, :], 0.0, ALU.mult, ALU.add)\
                 .then_inc(S("scanned"), 1)
                v.wait_ge(S("scanned"), i + 1)
                v.wait_ge(S("c_spread"), i + 1)
                if i >= 2:
                    v.wait_ge(S("y_sum"), i - 1)
                v.tensor_tensor(prod[:, i % 2, :], hst[:, i % 2, :], bank(4, 2), ALU.mult)\
                 .then_inc(S("prod_ready"), 1)
                if i < 8:
                    softplus(1, i)
                if i == NS:
                    take_y(0)
            take_y(1)
            v.wait_ge(S("tg"), 1)

            def residual(n, turned, banks, gate, name, t0=0):
                for c in range(n):
                    v.wait_ge(S(turned), t0 // 2 + c + 1)
                    xs = x[:, t0 + 2 * c:t0 + 2 * c + 2, :].rearrange("p a b -> p (a b)")
                    v.scalar_tensor_tensor(xs, bank(banks + c), tg[:, gate:gate + 1], xs, ALU.mult, ALU.add)\
                     .then_inc(S(name), 1)

            def bc(a, n, tiles=T):
                return a.unsqueeze(2).to_broadcast([P, tiles, n])

            def first_best(val, m, ind, work, best, rank, n, tiles=T):
                link(v.tensor_reduce(m, val, AX.X, ALU.max))
                link(v.tensor_tensor(work, val, bc(m, n, tiles), ALU.is_equal))
                link(v.tensor_tensor(work, work, rank.unsqueeze(1).to_broadcast([P, tiles, n]), ALU.mult))
                link(v.tensor_reduce(best, work, AX.X, ALU.max))
                link(v.tensor_tensor(ind, work, bc(best, n, tiles), ALU.is_equal))

            def half_stats(half, n=2):
                for t in range(4 * half, 4 * half + 4):
                    v.wait_ge(S(f"x{n}"), t // 2 + 1)
                    last = v.bn_stats(stats[:, t, :], x[:, t, :])
                link(last)
                for t in range(4 * half, 4 * half + 4):
                    last = v.bn_aggr(mv[:, t, :], stats[:, t, :])
                last.then_inc(S(f"mv{n}"), 1)

            def half_apply(half, n=2):
                v.wait_ge(S(f"rstd{n}"), half + 1)
                for t in range(4 * half, 4 * half + 4):
                    v.tensor_scalar(xn[:, t, :], x[:, t, :], mv[:, t, 0:1], rstd[:, t:t + 1],
                                    ALU.subtract, ALU.mult).then_inc(S(f"xn{n}"), 1)

            def some_maxima(tag, s, i, jj, at=0):
                qt, g = i // 4, i % 4
                n = P * (qt + 1) if tag == "2" else 256
                v.wait_ge(S("logit" + tag), 16 * s + 2 * i + jj + 1)
                if s >= 2 and i == jj == 0:
                    v.wait_ge(S("m_parts" + tag), s - 1)
                h = 4 * g + 2 * jj
                v.tensor_reduce(mx[:, s % 2, qt, h:h + 2],
                                psum[:, at + jj, 0:2 * n].rearrange("p (j k) -> p j k", j=2),
                                AX.X, ALU.max).then_inc(S("max" + tag), 1)

            def best_two(half, at):
                hs = slice(4 * half, 4 * half + 4)
                l_, a1, a2, work = rl[:, hs, :], i1[:, hs, :], i2[:, hs, :], tmp8[:, hs, :]
                v.wait_ge(S("router"), (1, 5)[half])
                v.tensor_copy(l_, psum[:, at, 0:4 * E].rearrange("p (t e) -> p t e", t=4)).then_inc(S("router_read"), 1)
                v.wait_ge(S("router_read"), half + 1)
                first_best(l_, m1[:, hs], a1, work, mi[:, hs], rank8[:, :], E, 4)
                link(v.scalar_tensor_tensor(l_, a1, -1e30, l_, ALU.mult, ALU.add))
                first_best(l_, m2[:, hs], a2, work, mi[:, hs], rank8[:, :], E, 4)
                v.tensor_tensor(w2[:, hs], m2[:, hs], m1[:, hs], ALU.subtract).then_inc(S("m_diff"), 1)

            def weights_of_two(half):
                hs = slice(4 * half, 4 * half + 4)
                a1, a2 = i1[:, hs, :], i2[:, hs, :]
                v.wait_ge(S("e2"), half + 1)
                link(v.tensor_scalar(w2[:, hs], w1[:, hs], 1.0, None, ALU.add))
                link(v.reciprocal(m1[:, hs], w2[:, hs]))
                link(v.tensor_tensor(m2[:, hs], m1[:, hs], w1[:, hs], ALU.mult))
                link(v.tensor_tensor(a1, a1, bc(m1[:, hs], E, 4), ALU.mult))
                link(v.tensor_tensor(a2, a2, bc(m2[:, hs], E, 4), ALU.mult))
                both_w, high = tw[:, hs, :], twb[:, hs, :]
                link(v.tensor_tensor(both_w, a1, a2, ALU.add))
                link(v.tensor_copy(high, both_w))
                v.tensor_copy(tw3[:, hs, 0:E], high)
                link(v.tensor_tensor(both_w, both_w, high, ALU.subtract))
                link(v.tensor_copy(high, both_w))
                v.tensor_copy(tw3[:, hs, 32:32 + E], high)
                v.tensor_tensor(tw3[:, hs, 64:64 + E], both_w, high, ALU.subtract).then_inc(S("tw_ready"), 1)

            def weights_out(half):
                v.wait_ge(S("tw_turned"), half + 1)
                v.tensor_copy(twT[:, 512 * half:512 * half + 512], psum[0:96, 6, :]).then_inc(S("twT_ready"), 1)

            residual(2, "y_turned", 0, 0, "x1", 0)
            half_stats(0, 1)
            residual(2, "y_turned", 2, 0, "x1", 4)
            half_apply(0, 1)
            half_stats(1, 1)
            half_apply(1, 1)
            v.wait_ge(S("tw3_zero"), 1)
            def hidden(i):
                f = i % NF
                v.wait_ge(S("gu_done"), i + 1)
                v.wait_ge(S("tw_spread"), i + 1)
                if i == NF:
                    v.wait_ge(S("down"), 2)
                v.tensor_tensor(hid[:, f, :], h1[:, i % 2, :], bank(3 * (i % 2) + 2), ALU.mult)\
                 .then_inc(S("hid_ready"), 1)
                if i == 5:
                    best_two(1, 7)
                if i == 7:
                    weights_of_two(1)
                if i == 9:
                    weights_out(1)
                if i == NF:
                    residual(2, "down", 6, 2, "x2", 0)
                    half_stats(0)
                if i == NF + 1:
                    half_apply(0)
                if i == TURN0:
                    rotate(v, link, 0, 0)
                if MAX0 - 1 <= i < MAX0 + 3:
                    for n in range(4 * (i - MAX0 + 1), min(4 * (i - MAX0 + 1) + 4, 14)):
                        some_maxima("1", 0, n // 2, n % 2, 6)

            for i in range(2 * NF):
                v.wait_ge(S("silu_done"), i + 1)
                v.wait_ge(S("gate_up"), 2 * i + 2)
                if i >= 2:
                    v.wait_ge(S("hid_ready"), i - 1)
                v.tensor_tensor(h1[:, i % 2, :], sg[:, i % 2, :], bank(3 * (i % 2) + 1), ALU.mult)\
                 .then_inc(S("gu_done"), 1)
                if i == 0:
                    best_two(0, 5)
                    weights_of_two(0)
                if i == 1:
                    weights_out(0)
                if i:
                    hidden(i - 1)
            hidden(2 * NF - 1)
            for n in (14, 15):
                some_maxima("1", 0, n // 2, n % 2, 0)
            for n in range(16):
                some_maxima("1", 1, n // 2, n % 2)
                if n in (5, 15):
                    residual(1, "down", 6 + n // 15, 2, "x2", 4 + 2 * (n // 15))
            half_stats(1)
            def attention(tag, units, first, finish, side):
                for s in range(first, units + LAG + 1):
                    u = s - LAG
                    for i in range(8):
                        if s < units:
                            for jj in range(2):
                                some_maxima(tag, s, i, jj)
                        if i in (3, 5) and 0 <= u - 1 < units:
                            finish(u - 1, (i - 3) // 2)
                        side(s, i)

            def finish1(u, qt):
                t, k = 2 * batch_of(u) + qt, half_of(u)
                v.wait_ge(S("o_turned1"), 2 * u + qt + 1)
                o = bank(7).rearrange("p (h e) -> p h e", e=32)
                link(v.reciprocal(rec[:, t, :], o[:, :, D1]))
                v.tensor_tensor(attn[:, t, P * k:P * k + P].rearrange("p (h e) -> p h e", e=D1), o[:, :, 0:D1],
                                rec[:, t, :].unsqueeze(2).to_broadcast([P, 16, D1]), ALU.mult)\
                 .then_inc(S("o_norm1"), 1)

            def half_out(half, k, at, turned, done):
                v.wait_ge(S(turned), 2 * half + k + 1)
                v.tensor_copy(xnT[:, k, 512 * half:512 * half + 512], bank(at)).then_inc(S(done), 1)

            def best_head(half, at):
                hs = slice(4 * half, 4 * half + 4)
                v.wait_ge(S("gate_logit"), half + 1)
                v.tensor_copy(gl[:, hs, :], psum[:, at, 0:4 * H2].rearrange("p (t e) -> p t e", t=4))\
                 .then_inc(S("gl_read"), 1)
                v.wait_ge(S("gl_read"), half + 1)
                first_best(gl[:, hs, :], gm[:, hs], gi[:, hs, :], gt[:, hs, :], gs[:, hs], rank16[:, :], H2, 4)
                v.tensor_tensor(gt[:, hs, :], gl[:, hs, :], bc(gm[:, hs], H2, 4), ALU.subtract)\
                 .then_inc(S("gdiff"), 1)

            def best_weight(half):
                hs = slice(4 * half, 4 * half + 4)
                v.wait_ge(S("gexp"), half + 1)
                link(v.tensor_reduce(gs[:, hs], gt[:, hs, :], AX.X, ALU.add))
                link(v.reciprocal(gm[:, hs], gs[:, hs]))

            def q2_high(half, k, at):
                hs = slice(512 * half, 512 * half + 512)
                v.wait_ge(S("q2_proj"), 2 * half + k + 1)
                if half == k == 0:
                    v.wait_ge(S("q_stored"), 192)
                if half == 0:
                    v.tensor_copy(parts[:, 0, k, hs], bank(at)).then_inc(S("q2_high"), 1)
                v.wait_ge(S("q2_high"), 2 * half + k + 1)
                v.tensor_tensor(qr[:, k, hs], bank(at), parts[:, 0, k, hs], ALU.subtract).then_inc(S("q2_read"), 1)

            def keys_values(t, at):
                g4 = kvp[:, t % 2, :].rearrange("p (s h e) -> p s h e", s=2, h=H2)
                v.wait_ge(S("kv_proj"), t + 1)
                v.tensor_tensor(g4, bank(at).rearrange("p (s h e) -> p s h e", s=2, h=H2),
                                gi[:, t, :].unsqueeze(1).unsqueeze(3).to_broadcast([P, 2, H2, D2]), ALU.mult)\
                 .then_inc(S("kv_read"), 1)
                v.wait_ge(S("kv_read"), t + 1)
                v.tensor_reduce(ksv[:, t, :, :], g4.rearrange("p s h e -> p s e h"), AX.X, ALU.add)\
                 .then_inc(S("kv_summed"), 1)
                v.wait_ge(S("kv_summed"), t + 1)
                v.tensor_scalar(va2[:, t, 0:D2], ksv[:, t, 1, :], gm[:, t:t + 1], None, ALU.mult)

            def key_stack(half):
                hs = slice(4 * half, 4 * half + 4)
                v.memset(va2[:, hs, D2:32], 1.0)
                key = ksv[:, hs, 0, :]
                for c in range(3):
                    if c < 2:
                        link(v.tensor_copy(kb[:, hs, :], key))
                        src = kb[:, hs, :]
                    else:
                        src = key
                    for a in range(3):
                        r = D2 * (3 * c + a)
                        v.tensor_copy(kt[half][:, :, r:r + D2], src)
                    if c < 2:
                        link(v.tensor_tensor(key, key, kb[:, hs, :], ALU.subtract))
                v.memset(kt[half][:, :, 144:147], 1.0).then_inc(S("kt_ready"), 1)

            def side1(s, i):
                if s == LAG and i == 7:
                    rotate(v, link, 1, 0)
                j = 8 * (s - UNITS) + i
                if j in (-3, -2):
                    half_out(0, j + 3, 7, "a_turned", "a_out0")
                if j == 1:
                    residual(2, "proj1", 0, 1, "x3", 0)
                    half_stats(0, 3)
                if j == 5:
                    half_apply(0, 3)
                if j == 6:
                    for k in range(2):
                        half_out(0, k, k, "n3_turned", "n3_out0")
                if j == 7:
                    best_head(0, 1)
                    q2_high(0, 0, 0)
                if j == 8:
                    q2_high(0, 1, 1)
                if j == 9:
                    best_weight(0)
                if 9 <= j < 13:
                    keys_values(j - 9, (j - 9) % 2)
                if j == 13:
                    key_stack(0)

            def side2(s, i):
                j = 8 * s + i
                if j == 2:
                    residual(2, "proj1", 2, 1, "x3", 4)
                    half_stats(1, 3)
                if j == 5:
                    half_apply(1, 3)
                if j == 7:
                    best_head(1, 2)
                    q2_high(1, 0, 3)
                if j == 8:
                    q2_high(1, 1, 4)
                if j == 9:
                    best_weight(1)
                if 9 <= j < 13:
                    t = j - 5
                    keys_values(t, 5 - 3 * (t % 2))
                if j == 13:
                    key_stack(1)

            attention("1", UNITS, LAG, finish1, side1)

            def finish2(b, qt):
                t = 2 * b + qt
                v.wait_ge(S("o_turned2"), t + 1)
                o = bank(7).rearrange("p (h e) -> p h e", e=32)
                link(v.reciprocal(rec[:, t, :], o[:, :, D2]))
                f = fin[:, t % 2, :]
                v.tensor_tensor(f.rearrange("p (h e) -> p h e", e=D2), o[:, :, 0:D2],
                                rec[:, t, :].unsqueeze(2).to_broadcast([P, H2, D2]), ALU.mult)\
                 .then_inc(S("o_norm2"), 1)
                v.wait_ge(S("o_norm2"), t + 1)
                m = v.scalar_tensor_tensor(x[:, t, :], f, tg[:, 3:4], x[:, t, :], ALU.mult, ALU.add)
                if t % 2:
                    m.then_inc(S("fin_ready"), 1)

            attention("2", B, 0, finish2, side2)


def kernel(**inputs):
    import ml_dtypes
    import numpy as np
    import concourse.bacc as bacc
    from concourse.bass_utils import run_bass_kernel_spmd as run

    bf = ml_dtypes.bfloat16
    g = {k: np.ascontiguousarray(v) for k, v in inputs.items()}
    a = {}

    def rows(w_t, k=2):
        return w_t.reshape(k, P, -1).transpose(1, 0, 2)

    a["x"] = g["x"]
    a["ctxT"] = g["ctx_1024"].reshape(NT, CTX).T
    a["win"] = g["L0_xattn_in_proj_w"].T
    a["pos"] = g["fside_BxSx2_0"].reshape(T, P, 2).transpose(1, 0, 2)
    a["convw"] = rows(g["L0_xattn_conv_w"].reshape(C, KCONV))
    a["convb"] = g["L0_xattn_conv_b"].reshape(2, P).T
    order = list(range(RANK, RANK + 2 * NS))
    a["xproj"] = rows(g["L0_xattn_x_proj_w"][order * 3 + list(range(RANK))].T)
    a["dtw"] = g["L0_xattn_dt_proj_w"].T
    a["dtb"] = g["L0_xattn_dt_proj_b"].reshape(2, P).T
    a["alog"] = rows(g["L0_xattn_A_log"])
    a["dp"] = g["L0_xattn_D"].reshape(2, P).T
    gates = np.stack([g["g_xattn"][0], g["g_xattn"][1], g["g_ffn"][0], g["g_ffn"][1]])
    a["gates"] = np.broadcast_to(gates, (P, 4))
    swap = np.arange(C).reshape(-1, 2)[:, ::-1].reshape(-1)
    wkv = g["L1_xattn_Wkv"]
    a["wk1"] = wkv[:, :C]
    a["wk2"] = wkv[:, :C][:, swap]
    a["wv"] = wkv[:, C:]
    a["wq1"] = rows(g["L1_xattn_Wq"])
    a["wq2"] = rows(g["L1_xattn_Wq"][:, swap])
    a["wout"] = rows(g["L1_xattn_Wout"])
    a["bout"] = g["L1_xattn_bout"].reshape(1, C)
    a["wqkv"] = rows(g["L1_ffn_W_qkv"].T)
    a["wg16"] = rows(g["L1_ffn_W_gate"].T)
    a["wg8"] = rows(g["L0_ffn_gate_w"].T)
    a["gateT"] = rows(g["L0_ffn_gate_proj"].reshape(E * FD, C).T)
    a["upT"] = rows(g["L0_ffn_up_proj"].reshape(E * FD, C).T)
    a["downT"] = g["L0_ffn_down_proj"].transpose(0, 2, 1).reshape(NF, P, C).transpose(1, 0, 2)
    p = np.arange(P)
    a["ident"] = np.eye(P, dtype=np.float32)
    a["identb"] = np.eye(P, dtype=bf)
    sel = np.zeros((96, 2 * NS, P), bf)
    for n in range(32):
        sel[[n, 32 + n, 64 + n], n] = 1
    a["sel"] = sel
    a["ones3"] = np.ones((3, 16, 256), bf)
    ex = np.zeros((96, NF, P), bf)
    for f in range(NF):
        for part in range(3):
            ex[32 * part + (f * P + p) // FD, f, p] = 1
    a["ex8"] = ex
    ecs = np.zeros((8, 2, P), np.float32)
    pair = p % D1 // 4 * 2 + p % 4 // 2
    ecs[pair, 0, p] = 1
    ecs[4 + pair, 1, p] = np.where(p % 2, 1, -1)
    a["ecs"] = ecs
    mA = np.zeros((P, 2, 256), bf)
    mB = np.zeros((P, 2, 256), bf)
    mA[:, :, 128:] = np.where(p[None, :] > p[:, None], -1e30, 0)[:, None, :]
    mB[:, :, :128] = np.where(p[:, None] > p[None, :], -1e30, 0)[:, None, :]
    a["maskA"], a["maskB"] = mA, mB
    a["rank8"] = np.broadcast_to(np.arange(E, 0, -1, dtype=np.float32), (P, E))
    a["rank16"] = np.broadcast_to(np.arange(H2, 0, -1, dtype=np.float32), (P, H2))
    a["onesr"] = np.ones((1, P), np.float32)
    a["consts"] = np.broadcast_to(np.array([EPS, 1, 0, 0], np.float32), (P, 4))

    nc = bacc.Bacc("TRN2", target_bir_lowering=False, num_devices=1)
    arrays, d = {}, {}
    for name, v in a.items():
        v = np.ascontiguousarray(v)
        arrays["in_" + name] = v
        d[name] = nc.dram_tensor("in_" + name, v.shape, mybir.dt.from_np(v.dtype), kind="ExternalInput").ap()
    out = nc.dram_tensor("out_y", (B, L, C), F32, kind="ExternalOutput").ap()
    flamingo_program(nc, d, out)
    r = run(nc, [arrays], core_ids=[0])
    return r.results[0]["out_y"]
```
